# Optimizing a Trainium2 kernel written in Bass

```python
import numpy as np
import jax
import jax.numpy as jnp

def _softmax(x, axis=-1):
    return jax.nn.softmax(x, axis=axis)

def _gelu(x):
    return jax.nn.gelu(x, approximate=True)

def _silu(x):
    return jax.nn.silu(x)

def _sigmoid(x):
    return jax.nn.sigmoid(x)

def _layernorm(x, axis=-1, eps=1e-05):
    m = jnp.mean(x, axis=axis, keepdims=True)
    v = jnp.var(x, axis=axis, keepdims=True)
    return (x - m) / jnp.sqrt(v + eps)

def _scatter_add(tgt, idx, src, axis=0):
    return tgt.at[idx].add(src)

def _segment_sum(src, seg, n):
    return jax.ops.segment_sum(src, seg, n)
kernel_name = 'mk_xattn_ffn_d4_seqx_r4_5f5286'

def setup_inputs(seed: int=0):
    np.random.seed(seed)
    _w = jnp.asarray

    def _rec_inputs():
        import jax
        import jax.numpy as jnp
        _rk = jax.random.key(seed)
        x = 7.22e-05 + 1 * jax.random.normal(jax.random.fold_in(_rk, 1), (2, 1024, 256), jnp.float32)
        _lenS = 1024 - jax.random.randint(jax.random.fold_in(_rk, 7), (2,), 0, max(1, 1024 // 4) + 1, jnp.int32)
        _lenS2 = 77 - jax.random.randint(jax.random.fold_in(_rk, 8), (2,), 0, max(1, 77 // 4) + 1, jnp.int32)
        _ctx_1024P = jax.random.normal(jax.random.fold_in(_rk, 11), (2, 16, 256), jnp.float32)
        _ctx_1024c = jax.random.dirichlet(jax.random.fold_in(_rk, 511), 0.3 * jnp.ones((16,), jnp.float32), (2, 77))
        _ctx_1024t = jnp.einsum('bsk,bkd->bsd', _ctx_1024c, _ctx_1024P)
        _ctx_1024t = _ctx_1024t * jax.lax.rsqrt(jnp.mean(jnp.square(_ctx_1024t)) + 1e-12) * 0.953939
        ctx_1024 = 2.81802e-05 + 1.00001 * (_ctx_1024t + 0.3 * jax.random.normal(jax.random.fold_in(_rk, 611), (2, 77, 256), jnp.float32))
        _validS = jnp.arange(1024)[None, :] < _lenS[:, None]
        _validS2 = jnp.arange(77)[None, :] < _lenS2[:, None]
        _causal = jnp.tril(jnp.ones((1024, 1024), dtype=bool))
        mask_1x1xSxS2_ik0 = jnp.where(jnp.broadcast_to(_validS2[0:1, None, None, :], (1, 1, 1024, 77)), 0, 1).astype(jnp.int32)
        mask_BxS2_ik0 = jnp.where(jnp.broadcast_to(_validS2[:, :], (2, 77)), 0, 1).astype(jnp.int32)
        return (x, ctx_1024, mask_1x1xSxS2_ik0, mask_BxS2_ik0)
    x, ctx_1024, mask_1x1xSxS2_ik0, mask_BxS2_ik0 = _rec_inputs()

    def _L0_xattn_setup():
        import jax, jax.numpy as jnp
        import numpy as np
        B, NT, NM, C, H, FF = (8, 256, 512, 256, 8, 1024)

        def _ln(x, g, b):
            m = x.mean(-1, keepdims=True)
            v = jnp.mean((x - m) ** 2, axis=-1, keepdims=True)
            return (x - m) / jnp.sqrt(v + 1e-05) * g + b
        key = jax.random.key(seed)
        ks = jax.random.split(key, 8)
        w = lambda k, shape, s=0.02: jax.random.normal(k, shape, dtype=jnp.float32) * s
        return {'tgt': jax.random.normal(ks[0], (B, NT, C), dtype=jnp.float32), 'memory': jax.random.normal(ks[1], (B, NM, C), dtype=jnp.float32), 'qkv_w': w(ks[2], (3 * C, C)), 'qkv_b': jnp.zeros((3 * C,), jnp.float32), 'sa_out_w': w(ks[3], (C, C)), 'sa_out_b': jnp.zeros((C,), jnp.float32), 'in_proj_w': w(ks[4], (3 * C, C)), 'in_proj_b': jnp.zeros((3 * C,), jnp.float32), 'mha_out_w': w(ks[5], (C, C)), 'mha_out_b': jnp.zeros((C,), jnp.float32), 'lin1_w': w(ks[6], (FF, C)), 'lin1_b': jnp.zeros((FF,), jnp.float32), 'lin2_w': w(ks[7], (C, FF)), 'lin2_b': jnp.zeros((C,), jnp.float32), 'ln1_g': jnp.ones((C,), jnp.float32), 'ln1_b': jnp.zeros((C,), jnp.float32), 'ln2_g': jnp.ones((C,), jnp.float32), 'ln2_b': jnp.zeros((C,), jnp.float32), 'ln3_g': jnp.ones((C,), jnp.float32), 'ln3_b': jnp.zeros((C,), jnp.float32)}
    _L0_xattn_all = _L0_xattn_setup()
    _L0_xattn_in = {k: v for k, v in _L0_xattn_all.items() if k in ('qkv_w', 'qkv_b', 'sa_out_w', 'sa_out_b', 'in_proj_w', 'in_proj_b', 'mha_out_w', 'mha_out_b', 'lin1_w', 'lin1_b', 'lin2_w', 'lin2_b', 'ln1_g', 'ln1_b', 'ln2_g', 'ln2_b', 'ln3_g', 'ln3_b')}
    del _L0_xattn_all

    def _L0_ffn_setup():
        import jax, jax.numpy as jnp
        import numpy as np
        H = 32
        MB = 2
        TOP_K = 2
        key = jax.random.key(seed)
        ks = jax.random.split(key, 8)
        B, S, D, E = (8, 256, 256, 8)
        Fd = 4 * D

        def w(k, shape, fan):
            return jax.random.normal(k, shape, jnp.float32) / np.float32(np.sqrt(fan))
        return dict(x=jax.random.normal(ks[0], (B, S, D), jnp.float32), ln_g=jnp.ones((D,), jnp.float32), ln_b=jnp.zeros((D,), jnp.float32), wq=w(ks[1], (D, D), D), wk=w(ks[2], (D, D), D), wv=w(ks[3], (D, D), D), wo=w(ks[4], (D, D), D), gate_w=w(ks[5], (E, D), D), w1=w(ks[6], (E, D, Fd), D), b1=jnp.zeros((E, Fd), jnp.float32), w2=w(ks[7], (E, Fd, D), Fd), b2=jnp.zeros((E, D), jnp.float32))
    _L0_ffn_all = _L0_ffn_setup()
    _L0_ffn_in = {k: v for k, v in _L0_ffn_all.items() if k in ('ln_g', 'ln_b', 'wq', 'wk', 'wv', 'wo', 'gate_w', 'w1', 'b1', 'w2', 'b2')}
    del _L0_ffn_all

    def _L1_xattn_setup():
        import jax, jax.numpy as jnp
        import numpy as np
        D_MODEL = 256
        NUM_HEADS = 16
        D_K = D_MODEL // NUM_HEADS
        B, T = (2, 512)
        key = jax.random.key(seed)
        ks = jax.random.split(key, 11)
        s = 1.0 / np.sqrt(D_MODEL)
        inp = {'q': jax.random.normal(ks[0], (B, T, D_MODEL), jnp.float32), 'k': jax.random.normal(ks[1], (B, T, D_MODEL), jnp.float32), 'v': jax.random.normal(ks[2], (B, T, D_MODEL), jnp.float32), 'mask': jnp.tril(jnp.ones((1, 1, T, T), jnp.int32)), 'wq': jax.random.normal(ks[3], (D_MODEL, D_MODEL), jnp.float32) * s, 'bq': jnp.zeros((D_MODEL,), jnp.float32), 'wk': jax.random.normal(ks[4], (D_MODEL, D_MODEL), jnp.float32) * s, 'bk': jnp.zeros((D_MODEL,), jnp.float32), 'wv': jax.random.normal(ks[5], (D_MODEL, D_MODEL), jnp.float32) * s, 'bv': jnp.zeros((D_MODEL,), jnp.float32), 'wo': jax.random.normal(ks[6], (D_MODEL, D_MODEL), jnp.float32) * s, 'bo': jnp.zeros((D_MODEL,), jnp.float32)}
        return inp
    _L1_xattn_all = _L1_xattn_setup()
    _L1_xattn_in = {k: v for k, v in _L1_xattn_all.items() if k in ('wq', 'bq', 'wk', 'bk', 'wv', 'bv', 'wo', 'bo')}
    del _L1_xattn_all

    def _L1_ffn_setup():
        import jax, jax.numpy as jnp
        import numpy as np
        B, S, D = (2, 1024, 256)
        H = 1024
        E = 8
        K = 4
        key = jax.random.key(seed)
        kx, kr, ku, kd = jax.random.split(key, 4)
        x = jax.random.normal(kx, (B, S, D), dtype=jnp.float32)
        router_w = jax.random.normal(kr, (D, E), dtype=jnp.float32) / np.sqrt(D)
        up_w = jax.random.normal(ku, (E, D, H), dtype=jnp.float32) / np.sqrt(D)
        down_w = jax.random.normal(kd, (E, H, D), dtype=jnp.float32) / np.sqrt(H)
        return {'x': x, 'router_w': router_w, 'up_w': up_w, 'down_w': down_w}
    _L1_ffn_all = _L1_ffn_setup()
    _L1_ffn_in = {k: v for k, v in _L1_ffn_all.items() if k in ('router_w', 'up_w', 'down_w')}
    del _L1_ffn_all

    def _L2_xattn_setup():
        import math
        import jax, jax.numpy as jnp
        import numpy as np
        NUM_BUCKETS = 32
        MAX_DISTANCE = 128
        NUM_HEADS = 16

        def _relative_position_bucket_bidirectional(relative_position):
            nb = NUM_BUCKETS // 2
            buckets = (relative_position > 0).astype(jnp.int32) * nb
            rp = jnp.abs(relative_position)
            max_exact = nb // 2
            is_small = rp < max_exact
            rp_safe = jnp.maximum(rp, 1)
            large = max_exact + (jnp.log(rp_safe.astype(jnp.float32) / max_exact) / math.log(MAX_DISTANCE / max_exact) * (nb - max_exact)).astype(jnp.int32)
            large = jnp.minimum(large, nb - 1)
            return buckets + jnp.where(is_small, rp, large)

        def compute_bias(rel_bias, tgt_len, src_len):
            ctx = jnp.arange(tgt_len)[:, None]
            mem = jnp.arange(src_len)[None, :]
            buckets = _relative_position_bucket_bidirectional(mem - ctx)
            values = rel_bias[buckets]
            return jnp.transpose(values, (2, 0, 1))[None]
        key = jax.random.key(seed)
        ks = jax.random.split(key, 7)
        B, S, D = (4, 512, 256)
        s = 1.0 / math.sqrt(D)
        return {'query_states': jax.random.normal(ks[0], (B, S, D), jnp.float32), 'key_value_states': jax.random.normal(ks[1], (B, S, D), jnp.float32), 'wq': jax.random.normal(ks[2], (D, D), jnp.float32) * s, 'wk': jax.random.normal(ks[3], (D, D), jnp.float32) * s, 'wv': jax.random.normal(ks[4], (D, D), jnp.float32) * s, 'wo': jax.random.normal(ks[5], (D, D), jnp.float32) * s, 'rel_bias': jax.random.normal(ks[6], (NUM_BUCKETS, NUM_HEADS), jnp.float32)}
    _L2_xattn_all = _L2_xattn_setup()
    _L2_xattn_in = {k: v for k, v in _L2_xattn_all.items() if k in ('wq', 'wk', 'wv', 'wo', 'rel_bias')}
    del _L2_xattn_all

    def _L2_ffn_setup():
        import jax, jax.numpy as jnp
        import numpy as np
        B, T, D, E, H, K = (2, 512, 256, 8, 1024, 2)
        key = jax.random.key(seed)
        ks = jax.random.split(key, 8)
        s = 0.02
        return {'x': jax.random.normal(ks[0], (B, T, D), jnp.float32), 'rw1': jax.random.normal(ks[1], (D, D), jnp.float32) * s, 'rb1': jnp.zeros((D,), jnp.float32), 'rw2': jax.random.normal(ks[2], (D, E), jnp.float32) * s, 'rb2': jnp.zeros((E,), jnp.float32), 'we1': jax.random.normal(ks[3], (E, D, H), jnp.float32) * s, 'be1': jnp.zeros((E, H), jnp.float32), 'we2': jax.random.normal(ks[4], (E, H, D), jnp.float32) * s, 'be2': jnp.zeros((E, D), jnp.float32)}
    _L2_ffn_all = _L2_ffn_setup()
    _L2_ffn_in = {k: v for k, v in _L2_ffn_all.items() if k in ('rw1', 'rb1', 'rw2', 'rb2', 'we1', 'be1', 'we2', 'be2')}
    del _L2_ffn_all

    def _L3_xattn_setup():
        import jax, jax.numpy as jnp
        import numpy as np
        EMBED_DIM = 256
        N_HEAD = 16
        HEAD_DIM = EMBED_DIM // N_HEAD
        key = jax.random.key(seed)
        ks = jax.random.split(key, 12)
        B, T, S, C = (8, 256, 128, EMBED_DIM)
        scale = 1.0 / np.sqrt(C)
        x = jax.random.normal(ks[0], (B, T, C), dtype=jnp.float32)
        context = jax.random.normal(ks[1], (B, S, C), dtype=jnp.float32)
        context_mask = jax.random.randint(ks[2], (B, S), 0, 2, dtype=jnp.int32)
        context_mask = context_mask.at[:, 0].set(1)
        Wq = jax.random.normal(ks[3], (C, C), dtype=jnp.float32) * scale
        bq = jnp.zeros((C,), dtype=jnp.float32)
        Wk = jax.random.normal(ks[4], (C, C), dtype=jnp.float32) * scale
        bk = jnp.zeros((C,), dtype=jnp.float32)
        Wv = jax.random.normal(ks[5], (C, C), dtype=jnp.float32) * scale
        bv = jnp.zeros((C,), dtype=jnp.float32)
        Wp = jax.random.normal(ks[6], (C, C), dtype=jnp.float32) * scale
        bp = jnp.zeros((C,), dtype=jnp.float32)
        return {'x': x, 'context': context, 'context_mask': context_mask, 'Wq': Wq, 'bq': bq, 'Wk': Wk, 'bk': bk, 'Wv': Wv, 'bv': bv, 'Wp': Wp, 'bp': bp}
    _L3_xattn_all = _L3_xattn_setup()
    _L3_xattn_in = {k: v for k, v in _L3_xattn_all.items() if k in ('Wq', 'bq', 'Wk', 'bk', 'Wv', 'bv', 'Wp', 'bp')}
    del _L3_xattn_all

    def _L3_ffn_setup():
        import jax, jax.numpy as jnp
        import numpy as np
        MANT_BITS = 8
        _PWL_X = jnp.linspace(-4.0, 4.0, 33, dtype=jnp.float32)
        _PWL_Y = 0.5 * _PWL_X * (1.0 + jax.lax.erf(_PWL_X / jnp.sqrt(jnp.float32(2.0))))

        def float2fix(x, mantissa_bits):
            s = jnp.float32(2.0 ** mantissa_bits)
            q = jnp.round(x * s) / s
            return x + jax.lax.stop_gradient(q - x)

        def pwlin_gelu_basic(x, mantissa_bits_in, mantissa_bits_out):
            xq = float2fix(x, mantissa_bits_in)
            y = jnp.interp(xq, _PWL_X, _PWL_Y)
            y = jnp.where(xq > 4.0, xq, jnp.where(xq < -4.0, jnp.float32(0.0), y))
            return float2fix(y, mantissa_bits_out)
        key = jax.random.key(seed)
        k_x, k_w1, k_b1, k_w2, k_b2 = jax.random.split(key, 5)
        dim, ff_dim = (256, 1024)
        B, S = (32, 128)
        sc1 = 1.0 / np.sqrt(dim)
        sc2 = 1.0 / np.sqrt(ff_dim)
        return {'x': jax.random.normal(k_x, (B, S, dim), dtype=jnp.float32), 'w1': jax.random.uniform(k_w1, (dim, ff_dim), jnp.float32, -sc1, sc1), 'b1': jax.random.uniform(k_b1, (ff_dim,), jnp.float32, -sc1, sc1), 'w2': jax.random.uniform(k_w2, (ff_dim, dim), jnp.float32, -sc2, sc2), 'b2': jax.random.uniform(k_b2, (dim,), jnp.float32, -sc2, sc2)}
    _L3_ffn_all = _L3_ffn_setup()
    _L3_ffn_in = {k: v for k, v in _L3_ffn_all.items() if k in ('w1', 'b1', 'w2', 'b2')}
    del _L3_ffn_all
    return {'x': x, 'ctx_1024': ctx_1024, 'mask_1x1xSxS2_ik0': mask_1x1xSxS2_ik0, 'mask_BxS2_ik0': mask_BxS2_ik0, 'L0_xattn_qkv_w': _L0_xattn_in['qkv_w'], 'L0_xattn_qkv_b': _L0_xattn_in['qkv_b'], 'L0_xattn_sa_out_w': _L0_xattn_in['sa_out_w'], 'L0_xattn_sa_out_b': _L0_xattn_in['sa_out_b'], 'L0_xattn_in_proj_w': _L0_xattn_in['in_proj_w'], 'L0_xattn_in_proj_b': _L0_xattn_in['in_proj_b'], 'L0_xattn_mha_out_w': _L0_xattn_in['mha_out_w'], 'L0_xattn_mha_out_b': _L0_xattn_in['mha_out_b'], 'L0_xattn_lin1_w': _L0_xattn_in['lin1_w'], 'L0_xattn_lin1_b': _L0_xattn_in['lin1_b'], 'L0_xattn_lin2_w': _L0_xattn_in['lin2_w'], 'L0_xattn_lin2_b': _L0_xattn_in['lin2_b'], 'L0_xattn_ln1_g': _L0_xattn_in['ln1_g'], 'L0_xattn_ln1_b': _L0_xattn_in['ln1_b'], 'L0_xattn_ln2_g': _L0_xattn_in['ln2_g'], 'L0_xattn_ln2_b': _L0_xattn_in['ln2_b'], 'L0_xattn_ln3_g': _L0_xattn_in['ln3_g'], 'L0_xattn_ln3_b': _L0_xattn_in['ln3_b'], 'L0_ffn_ln_g': _L0_ffn_in['ln_g'], 'L0_ffn_ln_b': _L0_ffn_in['ln_b'], 'L0_ffn_wq': _L0_ffn_in['wq'], 'L0_ffn_wk': _L0_ffn_in['wk'], 'L0_ffn_wv': _L0_ffn_in['wv'], 'L0_ffn_wo': _L0_ffn_in['wo'], 'L0_ffn_gate_w': _L0_ffn_in['gate_w'], 'L0_ffn_w1': _L0_ffn_in['w1'], 'L0_ffn_b1': _L0_ffn_in['b1'], 'L0_ffn_w2': _L0_ffn_in['w2'], 'L0_ffn_b2': _L0_ffn_in['b2'], 'L1_xattn_wq': _L1_xattn_in['wq'], 'L1_xattn_bq': _L1_xattn_in['bq'], 'L1_xattn_wk': _L1_xattn_in['wk'], 'L1_xattn_bk': _L1_xattn_in['bk'], 'L1_xattn_wv': _L1_xattn_in['wv'], 'L1_xattn_bv': _L1_xattn_in['bv'], 'L1_xattn_wo': _L1_xattn_in['wo'], 'L1_xattn_bo': _L1_xattn_in['bo'], 'L1_ffn_router_w': _L1_ffn_in['router_w'], 'L1_ffn_up_w': _L1_ffn_in['up_w'], 'L1_ffn_down_w': _L1_ffn_in['down_w'], 'L2_xattn_wq': _L2_xattn_in['wq'], 'L2_xattn_wk': _L2_xattn_in['wk'], 'L2_xattn_wv': _L2_xattn_in['wv'], 'L2_xattn_wo': _L2_xattn_in['wo'], 'L2_xattn_rel_bias': _L2_xattn_in['rel_bias'], 'L2_ffn_rw1': _L2_ffn_in['rw1'], 'L2_ffn_rb1': _L2_ffn_in['rb1'], 'L2_ffn_rw2': _L2_ffn_in['rw2'], 'L2_ffn_rb2': _L2_ffn_in['rb2'], 'L2_ffn_we1': _L2_ffn_in['we1'], 'L2_ffn_be1': _L2_ffn_in['be1'], 'L2_ffn_we2': _L2_ffn_in['we2'], 'L2_ffn_be2': _L2_ffn_in['be2'], 'L3_xattn_Wq': _L3_xattn_in['Wq'], 'L3_xattn_bq': _L3_xattn_in['bq'], 'L3_xattn_Wk': _L3_xattn_in['Wk'], 'L3_xattn_bk': _L3_xattn_in['bk'], 'L3_xattn_Wv': _L3_xattn_in['Wv'], 'L3_xattn_bv': _L3_xattn_in['bv'], 'L3_xattn_Wp': _L3_xattn_in['Wp'], 'L3_xattn_bp': _L3_xattn_in['bp'], 'L3_ffn_w1': _L3_ffn_in['w1'], 'L3_ffn_b1': _L3_ffn_in['b1'], 'L3_ffn_w2': _L3_ffn_in['w2'], 'L3_ffn_b2': _L3_ffn_in['b2']}

def reference(x, ctx_1024, mask_1x1xSxS2_ik0, mask_BxS2_ik0, L0_xattn_qkv_w, L0_xattn_qkv_b, L0_xattn_sa_out_w, L0_xattn_sa_out_b, L0_xattn_in_proj_w, L0_xattn_in_proj_b, L0_xattn_mha_out_w, L0_xattn_mha_out_b, L0_xattn_lin1_w, L0_xattn_lin1_b, L0_xattn_lin2_w, L0_xattn_lin2_b, L0_xattn_ln1_g, L0_xattn_ln1_b, L0_xattn_ln2_g, L0_xattn_ln2_b, L0_xattn_ln3_g, L0_xattn_ln3_b, L0_ffn_ln_g, L0_ffn_ln_b, L0_ffn_wq, L0_ffn_wk, L0_ffn_wv, L0_ffn_wo, L0_ffn_gate_w, L0_ffn_w1, L0_ffn_b1, L0_ffn_w2, L0_ffn_b2, L1_xattn_wq, L1_xattn_bq, L1_xattn_wk, L1_xattn_bk, L1_xattn_wv, L1_xattn_bv, L1_xattn_wo, L1_xattn_bo, L1_ffn_router_w, L1_ffn_up_w, L1_ffn_down_w, L2_xattn_wq, L2_xattn_wk, L2_xattn_wv, L2_xattn_wo, L2_xattn_rel_bias, L2_ffn_rw1, L2_ffn_rb1, L2_ffn_rw2, L2_ffn_rb2, L2_ffn_we1, L2_ffn_be1, L2_ffn_we2, L2_ffn_be2, L3_xattn_Wq, L3_xattn_bq, L3_xattn_Wk, L3_xattn_bk, L3_xattn_Wv, L3_xattn_bv, L3_xattn_Wp, L3_xattn_bp, L3_ffn_w1, L3_ffn_b1, L3_ffn_w2, L3_ffn_b2):
    import jax
    import jax.numpy as jnp

    def _L0_xattn_ref(tgt, memory, qkv_w, qkv_b, sa_out_w, sa_out_b, in_proj_w, in_proj_b, mha_out_w, mha_out_b, lin1_w, lin1_b, lin2_w, lin2_b, ln1_g, ln1_b, ln2_g, ln2_b, ln3_g, ln3_b):
        import jax, jax.numpy as jnp
        import numpy as np
        B, NT, NM, C, H, FF = (8, 256, 512, 256, 8, 1024)

        def _ln(x, g, b):
            m = x.mean(-1, keepdims=True)
            v = jnp.mean((x - m) ** 2, axis=-1, keepdims=True)
            return (x - m) / jnp.sqrt(v + 1e-05) * g + b
        Bx, N, Cx = tgt.shape
        qkv = tgt @ qkv_w.T + qkv_b
        q, k, v = jnp.split(qkv, 3, axis=-1)
        scores = jnp.einsum('bnc,bmc->bnm', q, k) * jnp.sqrt(jnp.float32(Cx))
        diag = jnp.eye(N, dtype=bool)
        scores = jnp.where(diag[None, :, :], scores, -jnp.inf)
        attn = jax.nn.softmax(scores, axis=-1)
        sa = jnp.einsum('bnm,bmc->bnc', attn, v) @ sa_out_w.T + sa_out_b
        x = _ln(tgt + sa, ln1_g, ln1_b)
        d = Cx // H
        wq, wk, wv = jnp.split(in_proj_w, 3, axis=0)
        bq, bk, bv = jnp.split(in_proj_b, 3, axis=0)
        qh = (x @ wq.T + bq).reshape(Bx, N, H, d).transpose(0, 2, 1, 3)
        kh = (memory @ wk.T + bk).reshape(Bx, -1, H, d).transpose(0, 2, 1, 3)
        vh = (memory @ wv.T + bv).reshape(Bx, -1, H, d).transpose(0, 2, 1, 3)
        a = jax.nn.softmax(jnp.einsum('bhnd,bhmd->bhnm', qh, kh) / jnp.sqrt(jnp.float32(d)), axis=-1)
        ca = jnp.einsum('bhnm,bhmd->bhnd', a, vh).transpose(0, 2, 1, 3).reshape(Bx, N, Cx)
        ca = ca @ mha_out_w.T + mha_out_b
        x = _ln(x + ca, ln2_g, ln2_b)
        ff = jax.nn.relu(x @ lin1_w.T + lin1_b) @ lin2_w.T + lin2_b
        return _ln(x + ff, ln3_g, ln3_b)

    def _L0_ffn_ref(x, ln_g, ln_b, wq, wk, wv, wo, gate_w, w1, b1, w2, b2):
        import jax, jax.numpy as jnp
        import numpy as np
        H = 32
        MB = 2
        TOP_K = 2
        B, S, D = x.shape
        E = w1.shape[0]
        hd = D // H
        mu = jnp.mean(x, axis=-1, keepdims=True)
        var = jnp.var(x, axis=-1, keepdims=True)
        xn = (x - mu) / jnp.sqrt(var + 1e-05) * ln_g + ln_b
        q = (xn @ wq).reshape(B, S, H, hd)
        k = (xn @ wk).reshape(B, S, H, hd)
        v = (xn @ wv).reshape(B, S, H, hd)
        att = jnp.einsum('bqhd,bkhd->bhqk', q, k) / np.float32(np.sqrt(hd))
        p = jax.nn.softmax(att, axis=-1)
        o = jnp.einsum('bhqk,bkhd->bqhd', p, v).reshape(B, S, D) @ wo + x
        xf = o.reshape(-1, D)
        logits = xf @ gate_w.T
        _ = jax.lax.top_k(logits, TOP_K)
        tpe = xf.shape[0] // (MB * E)
        xe = xf.reshape(MB, E, tpe, D)
        h = jax.nn.gelu(jnp.einsum('metd,edf->metf', xe, w1) + b1[None, :, None, :], approximate=False)
        y = jnp.einsum('metf,efd->metd', h, w2) + b2[None, :, None, :]
        return y.reshape(B, S, D)

    def _L1_xattn_ref(q, k, v, mask, wq, bq, wk, bk, wv, bv, wo, bo):
        import jax, jax.numpy as jnp
        import numpy as np
        D_MODEL = 256
        NUM_HEADS = 16
        D_K = D_MODEL // NUM_HEADS
        B, T = (2, 512)
        Bq, Tq, _ = q.shape
        Tk = k.shape[1]
        qh = (q @ wq + bq).reshape(Bq, Tq, NUM_HEADS, D_K).transpose(0, 2, 1, 3)
        kh = (k @ wk + bk).reshape(Bq, Tk, NUM_HEADS, D_K).transpose(0, 2, 1, 3)
        vh = (v @ wv + bv).reshape(Bq, Tk, NUM_HEADS, D_K).transpose(0, 2, 1, 3)
        scores = jnp.einsum('bhqd,bhkd->bhqk', qh, kh) / jnp.sqrt(jnp.float32(D_K))
        scores = jnp.where(mask == 0, jnp.float32(-1000000000.0), scores)
        attn = jax.nn.softmax(scores, axis=-1)
        ctx = jnp.einsum('bhqk,bhkd->bhqd', attn, vh)
        ctx = ctx.transpose(0, 2, 1, 3).reshape(Bq, Tq, D_MODEL)
        return ctx @ wo + bo

    def _L1_ffn_ref(x, router_w, up_w, down_w):
        import jax, jax.numpy as jnp
        import numpy as np
        B, S, D = (2, 1024, 256)
        H = 1024
        E = 8
        K = 4
        router_logits = jnp.einsum('bsd,de->bse', x, router_w)
        routing_weights = jax.nn.softmax(router_logits, axis=-1)
        topk_weights, topk_indices = jax.lax.top_k(routing_weights, K)
        topk_weights = topk_weights / jnp.sum(topk_weights, axis=-1, keepdims=True)
        h = jnp.einsum('bsd,edh->bseh', x, up_w)
        h = jax.nn.gelu(h)
        expert_outputs = jnp.einsum('bseh,ehd->bsed', h, down_w)
        gathered = jnp.take_along_axis(expert_outputs, topk_indices[:, :, :, None], axis=2)
        output = jnp.sum(topk_weights[:, :, :, None] * gathered, axis=2)
        return output

    def _L2_xattn_ref(query_states, key_value_states, wq, wk, wv, wo, rel_bias):
        import math
        import jax, jax.numpy as jnp
        import numpy as np
        NUM_BUCKETS = 32
        MAX_DISTANCE = 128
        NUM_HEADS = 16

        def _relative_position_bucket_bidirectional(relative_position):
            nb = NUM_BUCKETS // 2
            buckets = (relative_position > 0).astype(jnp.int32) * nb
            rp = jnp.abs(relative_position)
            max_exact = nb // 2
            is_small = rp < max_exact
            rp_safe = jnp.maximum(rp, 1)
            large = max_exact + (jnp.log(rp_safe.astype(jnp.float32) / max_exact) / math.log(MAX_DISTANCE / max_exact) * (nb - max_exact)).astype(jnp.int32)
            large = jnp.minimum(large, nb - 1)
            return buckets + jnp.where(is_small, rp, large)

        def compute_bias(rel_bias, tgt_len, src_len):
            ctx = jnp.arange(tgt_len)[:, None]
            mem = jnp.arange(src_len)[None, :]
            buckets = _relative_position_bucket_bidirectional(mem - ctx)
            values = rel_bias[buckets]
            return jnp.transpose(values, (2, 0, 1))[None]
        B, T, D = query_states.shape
        S = key_value_states.shape[1]
        H = NUM_HEADS
        dh = D // H

        def shape(x, L):
            return jnp.transpose(x.reshape(B, L, H, dh), (0, 2, 1, 3))
        q = shape(query_states @ wq, T)
        k = shape(key_value_states @ wk, S)
        v = shape(key_value_states @ wv, S)
        bias = compute_bias(rel_bias, T, S)
        scores = jnp.einsum('bhtd,bhsd->bhts', q, k) + bias
        weights = jax.nn.softmax(scores, axis=-1)
        attn = jnp.einsum('bhts,bhsd->bhtd', weights, v)
        attn = jnp.transpose(attn, (0, 2, 1, 3)).reshape(B, T, D)
        return attn @ wo

    def _L2_ffn_ref(x, rw1, rb1, rw2, rb2, we1, be1, we2, be2):
        import jax, jax.numpy as jnp
        import numpy as np
        B, T, D, E, H, K = (2, 512, 256, 8, 1024, 2)
        b, t, d = x.shape
        xt = x.reshape(b * t, d)
        n = xt.shape[0]
        logits = jax.nn.silu(xt @ rw1 + rb1) @ rw2 + rb2
        _, idx = jax.lax.top_k(logits, K)
        mask = jnp.zeros((n, E), bool).at[jnp.arange(n)[:, None], idx].set(True)
        w = jax.nn.softmax(jnp.where(mask, logits, -jnp.inf), axis=1)
        h = jax.nn.silu(jnp.einsum('nd,edh->enh', xt, we1) + be1[:, None, :])
        eo = jnp.einsum('enh,ehd->end', h, we2) + be2[:, None, :]
        y = xt + jnp.einsum('ne,end->nd', w, eo)
        return y.reshape(b, t, d)

    def _L3_xattn_ref(x, context, context_mask, Wq, bq, Wk, bk, Wv, bv, Wp, bp):
        import jax, jax.numpy as jnp
        import numpy as np
        EMBED_DIM = 256
        N_HEAD = 16
        HEAD_DIM = EMBED_DIM // N_HEAD
        B, T, C = x.shape
        S = context.shape[1]
        H, D = (N_HEAD, HEAD_DIM)
        q = (jnp.einsum('btc,oc->bto', x, Wq) + bq).reshape(B, T, H, D).transpose(0, 2, 1, 3)
        k = (jnp.einsum('bsc,oc->bso', context, Wk) + bk).reshape(B, S, H, D).transpose(0, 2, 1, 3)
        v = (jnp.einsum('bsc,oc->bso', context, Wv) + bv).reshape(B, S, H, D).transpose(0, 2, 1, 3)
        att = jnp.einsum('bhtd,bhsd->bhts', q, k) * (1.0 / jnp.sqrt(jnp.float32(D)))
        mask = context_mask[:, None, None, :]
        att = jnp.where(mask == 0, -jnp.inf, att)
        att = jax.nn.softmax(att, axis=-1)
        att = jnp.nan_to_num(att, nan=0.0)
        y = jnp.einsum('bhts,bhsd->bhtd', att, v)
        y = y.transpose(0, 2, 1, 3).reshape(B, T, C)
        y = jnp.einsum('btc,oc->bto', y, Wp) + bp
        return y

    def _L3_ffn_ref(x, w1, b1, w2, b2):
        import jax, jax.numpy as jnp
        import numpy as np
        MANT_BITS = 8
        _PWL_X = jnp.linspace(-4.0, 4.0, 33, dtype=jnp.float32)
        _PWL_Y = 0.5 * _PWL_X * (1.0 + jax.lax.erf(_PWL_X / jnp.sqrt(jnp.float32(2.0))))

        def float2fix(x, mantissa_bits):
            s = jnp.float32(2.0 ** mantissa_bits)
            q = jnp.round(x * s) / s
            return x + jax.lax.stop_gradient(q - x)

        def pwlin_gelu_basic(x, mantissa_bits_in, mantissa_bits_out):
            xq = float2fix(x, mantissa_bits_in)
            y = jnp.interp(xq, _PWL_X, _PWL_Y)
            y = jnp.where(xq > 4.0, xq, jnp.where(xq < -4.0, jnp.float32(0.0), y))
            return float2fix(y, mantissa_bits_out)
        h = jnp.einsum('bsd,df->bsf', x, w1) + b1
        h = float2fix(h, MANT_BITS)
        h = pwlin_gelu_basic(h, MANT_BITS, MANT_BITS)
        h = float2fix(h, MANT_BITS)
        out = jnp.einsum('bsf,fd->bsd', h, w2) + b2
        return float2fix(out, MANT_BITS)
    x = x + _L0_xattn_ref(_layernorm(x, axis=-1), ctx_1024, L0_xattn_qkv_w, L0_xattn_qkv_b, L0_xattn_sa_out_w, L0_xattn_sa_out_b, L0_xattn_in_proj_w, L0_xattn_in_proj_b, L0_xattn_mha_out_w, L0_xattn_mha_out_b, L0_xattn_lin1_w, L0_xattn_lin1_b, L0_xattn_lin2_w, L0_xattn_lin2_b, L0_xattn_ln1_g, L0_xattn_ln1_b, L0_xattn_ln2_g, L0_xattn_ln2_b, L0_xattn_ln3_g, L0_xattn_ln3_b)
    x = x + _L0_ffn_ref(_layernorm(x, axis=-1), L0_ffn_ln_g, L0_ffn_ln_b, L0_ffn_wq, L0_ffn_wk, L0_ffn_wv, L0_ffn_wo, L0_ffn_gate_w, L0_ffn_w1, L0_ffn_b1, L0_ffn_w2, L0_ffn_b2)
    x = x + _L1_xattn_ref(_layernorm(x, axis=-1), ctx_1024, ctx_1024, mask_1x1xSxS2_ik0, L1_xattn_wq, L1_xattn_bq, L1_xattn_wk, L1_xattn_bk, L1_xattn_wv, L1_xattn_bv, L1_xattn_wo, L1_xattn_bo)
    x = x + _L1_ffn_ref(_layernorm(x, axis=-1), L1_ffn_router_w, L1_ffn_up_w, L1_ffn_down_w)
    x = x + _L2_xattn_ref(_layernorm(x, axis=-1), ctx_1024, L2_xattn_wq, L2_xattn_wk, L2_xattn_wv, L2_xattn_wo, L2_xattn_rel_bias)
    x = x + _L2_ffn_ref(_layernorm(x, axis=-1), L2_ffn_rw1, L2_ffn_rb1, L2_ffn_rw2, L2_ffn_rb2, L2_ffn_we1, L2_ffn_be1, L2_ffn_we2, L2_ffn_be2)
    x = x + _L3_xattn_ref(_layernorm(x, axis=-1), ctx_1024, mask_BxS2_ik0, L3_xattn_Wq, L3_xattn_bq, L3_xattn_Wk, L3_xattn_bk, L3_xattn_Wv, L3_xattn_bv, L3_xattn_Wp, L3_xattn_bp)
    x = x + _L3_ffn_ref(_layernorm(x, axis=-1), L3_ffn_w1, L3_ffn_b1, L3_ffn_w2, L3_ffn_b2)
    return x

_drawn_inputs = setup_inputs


def setup_inputs(seed=0):
    import zlib

    import numpy as np

    out = dict(_drawn_inputs(seed))
    spreads = {'L0_xattn_qkv_b': (0.0, 0.402),
     'L0_xattn_sa_out_b': (0.0, 0.1),
     'L0_xattn_in_proj_b': (0.0, 0.383),
     'L0_xattn_mha_out_b': (0.0, 0.1),
     'L0_xattn_lin1_b': (0.0, 0.318),
     'L0_xattn_lin2_b': (0.0, 0.1),
     'L0_xattn_ln1_g': (1.0, 0.2),
     'L0_xattn_ln1_b': (0.0, 0.1),
     'L0_xattn_ln2_g': (1.0, 0.2),
     'L0_xattn_ln2_b': (0.0, 0.1),
     'L0_xattn_ln3_g': (1.0, 0.2),
     'L0_xattn_ln3_b': (0.0, 0.1),
     'L0_ffn_ln_g': (1.0, 0.6),
     'L0_ffn_ln_b': (0.0, 0.1),
     'L0_ffn_b1': (0.0, 0.1),
     'L0_ffn_b2': (0.0, 0.1),
     'L1_xattn_bq': (0.0, 0.506),
     'L1_xattn_bk': (0.0, 0.8),
     'L1_xattn_bv': (0.0, 0.1),
     'L1_xattn_bo': (0.0, 0.1),
     'L2_ffn_rb1': (0.0, 0.556),
     'L2_ffn_rb2': (0.0, 0.1),
     'L2_ffn_be1': (0.0, 0.8),
     'L2_ffn_be2': (0.0, 0.396),
     'L3_xattn_bq': (0.0, 0.8),
     'L3_xattn_bk': (0.0, 0.8),
     'L3_xattn_bv': (0.0, 0.311),
     'L3_xattn_bp': (0.0, 0.267)}
    factors = {'L2_ffn_rw1': 3.408,
     'L2_ffn_rw2': 3.5,
     'L2_ffn_we1': 2.68,
     'L3_ffn_b1': 8.0,
     'L3_ffn_b2': 8.0}
    for name, (base, spread) in spreads.items():
        noise = np.random.default_rng([zlib.crc32(name.encode()), seed]).standard_normal(out[name].shape)
        drawn = base * np.exp(spread * noise) if base else spread * noise
        out[name] = jnp.asarray(drawn.astype(out[name].dtype))
    for name, factor in factors.items():
        out[name] = (out[name] * factor).astype(out[name].dtype)
    return out
```

```python
from contextlib import ExitStack, contextmanager

import numpy as np

import concourse.bass as bass
from concourse import mybir

F32 = mybir.dt.float32
F32R = mybir.dt.float32r
I32 = mybir.dt.int32
ALU = mybir.AluOpType
ACT = mybir.ActivationFunctionType
AX = mybir.AxisListType.X

P = 128
B, S, D = 2, 1024, 256
T = B * S
KD = D // P
CH = 512
NC = T // CH
S2 = 77
FF = 1024
NF = FF // P
E = 8
EPS = 1e-5
MAGIC = 1.5 * 2.0 ** 23
FIX = 256.0
BIG = 1e30
NT = S // P
BUCKETS = 32
OFFS = S + S2 - 1

SH = 32
SD = D // SH
HG = 4
NG = SH // HG
NKC = S // P

VECS = [
    ("a_bsv", 2), ("a_bso", 2), ("a_bq", 2), ("a_bk", 2), ("a_bo", 2), ("fa_b1", 8), ("fa_b2", 2),
    ("ln1_g", 2), ("ln1_b", 2), ("ln2_g", 2), ("ln2_b", 2), ("ln3_g", 2), ("ln3_b", 2),
    ("lni_g", 2), ("lni_b", 2), ("f0_b1", 64), ("f0_b2", 16),
    ("b_bq", 2), ("b_bk", 2), ("b_bo", 2),
    ("r2_b1", 2), ("f2_b1", 64), ("f2_b2", 16),
    ("d_bq", 2), ("d_bk", 2), ("d_bo", 2), ("f3_b1", 8), ("f3_b2", 2),
]
VEC_AT = {}
for _name, _k in VECS:
    VEC_AT[_name] = sum(k for nm, k in VECS[:len(VEC_AT)])
NVEC = sum(k for _, k in VECS)


@contextmanager
def phase(nc, names):
    with ExitStack() as ctx:
        sems = [ctx.enter_context(nc.semaphore(name)) for name in names]
        yield sems
        with nc.Block() as block:
            @block.gpsimd
            def _(pool):
                for s in sems:
                    pool.sem_clear(s)


def chunks(eng):
    with eng.Fori(0, B) as b:
        for cc in range(2):
            yield b * 2 + cc, cc


def tok(c):
    return bass.ds(c * CH, CH)


def wait_apart(m, eng, sem, value):
    eng.wait_ge(sem, value)
    eng.sem_inc(m.passed, 1)


def layer_norm(nc, m, name, src, dst, gain=None, shift=None):
    names = [f"{name}_{s}" for s in ("mean", "centred", "squared", "var", "root", "recip", "scaled")]
    with phase(nc, names) as (mean, centred, squared, var, root, recip, scaled), nc.Block() as block:
        @block.tensor
        def _(pe):
            for c, cc in chunks(pe):
                pe.wait_ge(centred, c + 1)
                for k in range(KD):
                    mm = pe.matmul(m.ps[:, cc, :], m.mean_w[:, :], src[:, k, tok(c)], start=k == 0, stop=k == KD - 1)
                mm.then_inc(mean, 1)
            for c, cc in chunks(pe):
                pe.wait_ge(squared, c + 1)
                pe.wait_ge(root, c + 1)
                for k in range(KD):
                    mm = pe.matmul(m.ps[:, 2 + cc, :], m.mean_w[:, :], m.sq[:, cc, k, :], start=k == 0, stop=k == KD - 1)
                mm.then_inc(var, 1)

        @block.vector
        def _(dve):
            dve.sem_inc(centred, 2)
            for c, cc in chunks(dve):
                dve.wait_ge(mean, c + 1)
                for k in range(KD):
                    ins = dve.tensor_tensor(dst[:, k, tok(c)], src[:, k, tok(c)], m.ps[:, cc, :], ALU.subtract)
                ins.then_inc(centred, 1)
            for c, cc in chunks(dve):
                dve.wait_ge(root, 2 + c + 1)
                dve.wait_ge(scaled, c + 1)
                dve.reciprocal(m.rs[:, cc, :], m.std[:, tok(c)]).then_inc(recip, 1)
            if gain:
                for c, cc in chunks(dve):
                    dve.wait_ge(scaled, 2 + c + 1)
                    dve.tensor_scalar(dst[:, 0, tok(c)], dst[:, 0, tok(c)], m.col(gain, 0), m.col(shift, 0), ALU.mult, ALU.add)
                    dve.tensor_scalar(dst[:, 1, tok(c)], dst[:, 1, tok(c)], m.col(gain, 1), m.col(shift, 1), ALU.mult, ALU.add)

        @block.scalar
        def _(act):
            act.sem_inc(root, 2)
            for c, cc in chunks(act):
                act.wait_ge(centred, 2 + c + 1)
                wait_apart(m, act, var, c + 1)
                act.activation(m.sq[:, cc, :, :], dst[:, :, tok(c)], ACT.Square).then_inc(squared, 1)
            for c, cc in chunks(act):
                wait_apart(m, act, var, 2 + c + 1)
                act.activation(m.std[:, tok(c)], m.ps[:, 2 + cc, :], ACT.Sqrt, bias=m.eps[:, 0:1]).then_inc(root, 1)

        @block.gpsimd
        def _(pool):
            pool.sem_inc(var, 2)
            pool.sem_inc(scaled, 2)
            for c, cc in chunks(pool):
                wait_apart(m, pool, recip, c + 1)
                for k in range(KD):
                    ins = pool.tensor_tensor(dst[:, k, tok(c)], dst[:, k, tok(c)], m.rs[:, cc, :], ALU.mult)
                ins.then_inc(scaled, 1)


def load_weights(nc, m, slots):
    with phase(nc, ["weights_in"]) as (loaded,), nc.Block() as block:
        @block.sync
        def _(sp):
            for slot, w in slots:
                sp.dma_start(m.wp[:, slot], w.rearrange("(k p) n -> p k n", p=P)).then_inc(loaded, 16)
            sp.wait_ge(loaded, 16 * len(slots))


def linear(nc, m, name, src, slot, dst, bias=None, func=ACT.Identity, plus=None):
    with phase(nc, [f"{name}_{s}" for s in ("full", "evac", "added")]) as (full, evac, added), nc.Block() as block:
        @block.tensor
        def _(pe):
            for c, cc in chunks(pe):
                for j in range(KD):
                    pe.wait_ge(evac, 2 * c + j + 1)
                    for k in range(KD):
                        mm = pe.matmul(m.ps[:, 2 * cc + j, :], m.wp[:, slot, k, j * P:(j + 1) * P], src[:, k, tok(c)],
                                       start=k == 0, stop=k == KD - 1)
                    mm.then_inc(full, 1)

        if plus is None:
            @block.scalar
            def _(act):
                act.sem_inc(evac, 4)
                for c, cc in chunks(act):
                    for j in range(KD):
                        wait_apart(m, act, full, 2 * c + j + 1)
                        act.activation(dst[:, j, tok(c)], m.ps[:, 2 * cc + j, :], func,
                                       bias=m.col(bias, j) if bias else 0.0).then_inc(evac, 1)
        else:
            @block.vector
            def _(dve):
                dve.sem_inc(evac, 4)
                for c, cc in chunks(dve):
                    for j in range(KD):
                        dve.wait_ge(full, 2 * c + j + 1)
                        dve.scalar_tensor_tensor(out=dst[:, j, tok(c)], in0=m.ps[:, 2 * cc + j, :],
                                                 scalar=m.col(bias, j) if bias else 0.0,
                                                 in1=plus[:, j, tok(c)], op0=ALU.add, op1=ALU.add).then_inc(evac, 1)


def add(nc, m, name, dst, src):
    with nc.Block() as block:
        @block.vector
        def _(dve):
            for c, cc in chunks(dve):
                dve.tensor_tensor(dst[:, :, tok(c)], dst[:, :, tok(c)], src[:, :, tok(c)], ALU.add)


def cross_attention(nc, m, name, src, dst, heads, adjust, scale, bq, bk, bv_row, io):
    d = D // heads
    hb = P // d
    nj = heads // 4
    hv = 8
    nr = heads // hv
    names = ["in", "kv_full", "kv_evac", "ones_col", "diag", "q_full", "q_evac", "s_full", "adj1", "adjusted",
             "s_max", "s_sub", "exp", "t_full", "t_evac", "o_full", "o_rec", "o_norm", "oT_full", "oT_evac",
             "adj_in", "adj_out", "tb_full", "tb_evac", "tb_out", "bias_in0", "bias_in1"]
    with ExitStack() as ctx:
        sems = ctx.enter_context(phase(nc, [f"{name}_{s}" for s in names]))
        (loaded, kv_full, kv_evac, ones_col, diag, q_full, q_evac, s_full, adj1, adjusted, s_max, s_sub, exp_done,
         t_full, t_evac, o_full, o_rec, o_norm, oT_full, oT_evac, adj_in, adj_out, tb_full, tb_evac, tb_out,
         bias_in0, bias_in1) = sems
        bias_in = [bias_in0, bias_in1]

        def sb(nm, shape, dt=F32):
            return ctx.enter_context(nc.sbuf_tensor(f"{name}_{nm}", shape, dt))

        ctxT = sb("ctxT", [P, KD, B * S2])
        kT = sb("kT", [P, KD, B * S2])
        rows = sb("rows", [P, hb])
        k_diag = sb("k_diag", [P, B, KD, hb, S2])
        val = sb("val", [S2, B, heads, d + 1])
        bv = sb("bv", [1, D])
        one = sb("one", [1, S2])
        qT = sb("qT", [P, KD, S])
        sc = sb("sc", [P, heads, S2])
        pr = sb("pr", [P, 2, heads, S2])
        prT = sb("prT", [S2, heads, P])
        mx = sb("mx", [P, heads])
        rec = sb("rec", [P, heads])
        on = sb("on", [P, D])
        if adjust == "replace":
            mask_i = sb("mask_i", [P, NT, S2], I32)
            keep = sb("keep", [P, NT, S2])
            low = sb("low", [P, NT, S2])
        if adjust == "keep":
            mask_i = sb("mask_i", [P, B, S2], I32)
            keep = sb("keep", [P, B, S2])
            low = sb("low", [P, B, S2])
            mask_c = sb("mask_c", [S2, B], I32)
            keep_c = sb("keep_c", [S2, B])
        if adjust == "bias":
            bias_t = sb("bias_t", [P, 2, heads, S2])
            rel = sb("rel", [BUCKETS, heads])
            hot = sb("hot", [BUCKETS, OFFS])
            by_off = sb("by_off", [heads, OFFS])
            by_off_d = nc.dram_tensor("bias_by_offset", (heads, OFFS), F32).ap()
        n_in = 3 + (bv_row is not None) + {None: 0, "replace": 1, "keep": 3, "bias": 2}[adjust]

        block = ctx.enter_context(nc.Block())

        def score_bank(j):
            return m.ps[:, j, 0:4 * S2]

        scores = m.ps[:, 0:nj, 0:4 * S2].rearrange("p j (h s) -> p j h s", s=S2)

        def by_bank(a):
            return a.rearrange("p (j h) s -> p j h s", j=nj)

        @block.sync
        def _(sp):
            sp.dma_start(ctxT[:, :, :], io["ctxT_reversed" if adjust == "bias" else "ctxT"].rearrange("(k p) n -> p k n", p=P)).then_inc(loaded, 16)
            sp.dma_start(rows[:, :], io[f"rows{hb}"]).then_inc(loaded, 16)
            sp.dma_start(one[:, :], io["one"]).then_inc(loaded, 16)
            if bv_row is not None:
                sp.dma_start(bv[:, :], bv_row).then_inc(loaded, 16)
            if adjust == "replace":
                sp.dma_start(mask_i[:, :, :], io["mask_q"].rearrange("(t p) s -> p t s", p=P)).then_inc(loaded, 16)
            if adjust == "keep":
                for b in range(B):
                    sp.dma_start(mask_i[:, b, :], io["mask_b"][b:b + 1, :].broadcast_to([P, S2])).then_inc(loaded, 16)
                sp.dma_start(mask_c[:, :], io["mask_bT"]).then_inc(loaded, 16)
            if adjust == "bias":
                sp.dma_start(rel[:, :], io["rel"]).then_inc(loaded, 16)
                sp.dma_start(hot[:, :], io["hot"]).then_inc(loaded, 16)
                sp.wait_ge(tb_evac, 3)
                sp.dma_start(by_off_d, by_off[:, :]).then_inc(tb_out, 16)
                sp.wait_ge(tb_out, 16)
                for i in range(B * NT):
                    if i >= 2:
                        sp.wait_ge(adjusted, i - 1)
                    sp.dma_start(bias_t[:, i % 2], bass.AP(by_off_d.tensor, (i % NT) * P, [[1, P], [OFFS, heads], [1, S2]])
                                 ).then_inc(bias_in[i % 2], 16)

        @block.tensor
        def _(pe):
            pe.wait_ge(loaded, 16 * n_in)
            for j in range(KD):
                for k in range(KD):
                    mm = pe.matmul(m.ps[:, j, 0:B * S2], m.wp[:, 2, k, j * P:(j + 1) * P], ctxT[:, k, :],
                                   start=k == 0, stop=k == KD - 1)
                mm.then_inc(kv_full, 1)
            for b in range(B):
                for k in range(KD):
                    mm = pe.matmul(m.ps[0:S2, 2 + b, 0:D], ctxT[:, k, b * S2:(b + 1) * S2], m.wp[:, 3, k, :],
                                   start=k == 0, stop=k == KD - 1 and bv_row is None)
                if bv_row is not None:
                    mm = pe.matmul(m.ps[0:S2, 2 + b, 0:D], one[:, :], bv[:, :], start=False, stop=True)
                mm.then_inc(kv_full, 1)
            if adjust == "bias":
                for i in range(3):
                    w = min(512, OFFS - 512 * i)
                    pe.matmul(m.ps[0:heads, 4 + i, 0:w], rel[:, :], hot[:, 512 * i:512 * i + w],
                              start=True, stop=True).then_inc(tb_full, 1)
                pe.wait_ge(tb_evac, 3)
            pe.wait_ge(kv_evac, 4)
            pe.wait_ge(diag, B * KD)

            with pe.Fori(0, B) as b:
                pe.wait_ge(s_sub, b * NT + 1)
                for cc in range(2):
                    for j in range(KD):
                        for k in range(KD):
                            mm = pe.matmul(m.ps[:, 2 * cc + j, :], m.wp[:, 0, k, j * P:(j + 1) * P],
                                           src[:, k, tok(b * 2 + cc)], start=k == 0, stop=k == KD - 1)
                        mm.then_inc(q_full, 1)

                def scores_of(i):
                    pe.wait_ge(s_sub, b * NT + i + 1)
                    for j in range(nj):
                        fb = 4 * j // hb
                        mm = pe.matmul(score_bank(j), qT[:, fb, i * P:(i + 1) * P],
                                       k_diag[:, bass.ds(b, 1), fb, 4 * j - fb * hb:4 * j - fb * hb + 4, :].rearrange(
                                           "p a h s -> p (a h s)"), start=True, stop=True)
                    mm.then_inc(s_full, 1)

                def back(i):
                    pe.wait_ge(o_norm, b * NT + i + 1)
                    pe.wait_ge(oT_evac, b * NT + i + 1)
                    for k in range(KD):
                        mm = pe.transpose(m.ps[:, 7, k * P:(k + 1) * P], on[:, k * P:(k + 1) * P], m.ident[:, :])
                    mm.then_inc(oT_full, 1)

                pe.wait_ge(q_evac, b * 4 + 4)
                scores_of(0)
                for i in range(NT):
                    if i + 1 < NT:
                        scores_of(i + 1)
                    pe.wait_ge(exp_done, b * NT + i + 2)
                    for r in range(nr):
                        pe.wait_ge(t_evac, b * NT * nr + i * nr + r + 1)
                        for hh in range(hv):
                            mm = pe.transpose(m.ps[0:S2, 4 + hh // 4, (hh % 4) * P:(hh % 4 + 1) * P],
                                              pr[:, i % 2, r * hv + hh, :], m.ident[:, :])
                        mm.then_inc(t_full, 1)
                    if i >= 1:
                        back(i - 1)
                    pe.wait_ge(t_evac, b * NT * nr + (i + 1) * nr + 1)
                    if i >= 1:
                        pe.wait_ge(o_norm, b * NT + i)
                    for hh in range(heads):
                        mm = pe.matmul(m.ps[:, 6, hh * (d + 1):(hh + 1) * (d + 1)], prT[:, hh, :],
                                       val[:, bass.ds(b, 1), hh, :].rearrange("p a e -> p (a e)"), start=True, stop=True)
                    mm.then_inc(o_full, 1)
                back(NT - 1)

        @block.scalar
        def _(act):
            act.sem_inc(t_evac, 1)
            act.sem_inc(oT_evac, 1)
            act.sem_inc(exp_done, 1)
            for j in range(KD):
                act.wait_ge(kv_full, j + 1)
                act.activation(kT[:, j, :], m.ps[:, j, 0:B * S2], ACT.Identity,
                               bias=m.col(bk, j) if bk else 0.0).then_inc(kv_evac, 1)
            act.wait_ge(ones_col, 1)
            for b in range(B):
                act.wait_ge(kv_full, KD + b + 1)
                v = m.ps[0:S2, 2 + b, 0:D].rearrange("s (h d) -> s h d", d=d)
                if adjust == "keep":
                    act.activation(val[:, b, :, 0:d], v, ACT.Copy, scale=keep_c[:, b:b + 1]).then_inc(kv_evac, 1)
                else:
                    act.activation(val[:, b, :, 0:d], v, ACT.Copy).then_inc(kv_evac, 1)
            if adjust == "bias":
                for i in range(3):
                    w = min(512, OFFS - 512 * i)
                    act.wait_ge(tb_full, i + 1)
                    act.activation(by_off[:, 512 * i:512 * i + w], m.ps[0:heads, 4 + i, 0:w], ACT.Copy).then_inc(tb_evac, 1)

            with act.Fori(0, B) as b:
                for cc in range(2):
                    for j in range(KD):
                        act.wait_ge(q_full, b * 4 + 2 * cc + j + 1)
                        act.activation(qT[:, j, cc * CH:(cc + 1) * CH], m.ps[:, 2 * cc + j, :], ACT.Identity,
                                       bias=m.col(bq, j) if bq else 0.0).then_inc(q_evac, 1)

                def back(i):
                    wait_apart(m, act, oT_full, b * NT + i + 2)
                    act.activation(dst[:, :, bass.ds(b * S + i * P, P)],
                                   m.ps[:, 7, 0:D].rearrange("p (k q) -> p k q", k=KD), ACT.Copy).then_inc(oT_evac, 1)

                for i in range(NT):
                    act.wait_ge(s_sub, b * NT + i + 2)
                    act.wait_ge(t_full, b * NT * nr + (i + 1) * nr)
                    act.activation(pr[:, i % 2], sc[:, :, :], ACT.Exp, scale=scale).then_inc(exp_done, 1)
                    for r in range(nr):
                        act.wait_ge(t_full, b * NT * nr + i * nr + r + 1 + 2 * nr)
                        if r == 0:
                            act.wait_ge(o_full, b * NT + i + 1)
                        act.activation(prT[:, r * hv:(r + 1) * hv, :].rearrange("s (c h) q -> s c h q", c=2),
                                       m.ps[0:S2, 4:6, :].rearrange("s c (h q) -> s c h q", q=P), ACT.Copy).then_inc(t_evac, 1)
                    if i >= 1:
                        back(i - 1)
                back(NT - 1)

        @block.gpsimd
        def _(pool):
            pool.sem_inc(o_full, 1)
            pool.sem_inc(t_full, 2 * nr)
            pool.sem_inc(oT_full, 1)

        @block.vector
        def _(dve):
            dve.sem_inc(s_sub, 1)
            dve.wait_ge(loaded, 16 * n_in)
            if adjust == "keep":
                dve.tensor_scalar(keep_c[:, :], mask_c[:, :], 0.0, None, ALU.not_equal).then_inc(adj1, 1)
                dve.tensor_scalar(keep[:, :, :], mask_i[:, :, :], 0.0, None, ALU.not_equal).then_inc(adj1, 1)
                dve.wait_ge(adj1, 2)
                dve.tensor_scalar(low[:, :, :], keep[:, :, :], -1.0, BIG, ALU.add, ALU.mult).then_inc(adj1, 1)
                for b in range(B):
                    ins = dve.tensor_copy(val[:, b, :, d:d + 1].rearrange("s h a -> s (h a)"),
                                          keep_c[:, b:b + 1].broadcast_to([S2, heads]))
                ins.then_inc(ones_col, 1)
                dve.wait_ge(adj1, 3)
            else:
                dve.memset(val[:, :, :, d:d + 1], 1.0).then_inc(ones_col, 1)
            if adjust == "replace":
                dve.tensor_scalar(keep[:, :, :], mask_i[:, :, :], 0.0, None, ALU.not_equal).then_inc(adj1, 1)
                dve.wait_ge(adj1, 1)
                dve.tensor_scalar(low[:, :, :], keep[:, :, :], -1.0, 1e9 / scale, ALU.add, ALU.mult).then_inc(adj1, 1)
                dve.wait_ge(adj1, 2)
            dve.wait_ge(kv_evac, KD)
            for b in range(B):
                for k in range(KD):
                    dve.tensor_tensor(k_diag[:, b, k], kT[:, k, b * S2:(b + 1) * S2].unsqueeze(1).broadcast_to([P, hb, S2]),
                                      rows[:, :].unsqueeze(2).broadcast_to([P, hb, S2]), ALU.mult).then_inc(diag, 1)

            with dve.Fori(0, B) as b:
                def soft(i):
                    dve.wait_ge(s_full, b * NT + i + 1)
                    dve.wait_ge(exp_done, b * NT + i + 1)
                    source = scores
                    if adjust == "replace":
                        k4 = keep[:, i:i + 1, :].unsqueeze(1).broadcast_to([P, nj, 4, S2])
                        l3 = low[:, i:i + 1, :].broadcast_to([P, heads, S2])
                        dve.tensor_tensor(by_bank(sc[:, :, :]), source, k4, ALU.mult).then_inc(adj_out, 1)
                        dve.wait_ge(adj_out, b * NT + i + 1)
                        dve.tensor_tensor(sc[:, :, :], sc[:, :, :], l3, ALU.add).then_inc(adjusted, 1)
                    if adjust == "keep":
                        l4 = low[:, bass.ds(b, 1), :].unsqueeze(1).broadcast_to([P, nj, 4, S2])
                        dve.tensor_tensor(by_bank(sc[:, :, :]), source, l4, ALU.add).then_inc(adjusted, 1)
                    if adjust == "bias":
                        dve.wait_ge(bias_in[i % 2], b * (8 * NT) + 16 * (i // 2 + 1))
                        dve.tensor_tensor(by_bank(sc[:, :, :]), source, by_bank(bias_t[:, i % 2]), ALU.add).then_inc(adjusted, 1)
                    if adjust:
                        dve.wait_ge(adjusted, b * NT + i + 1)
                        source = by_bank(sc[:, :, :])
                    dve.tensor_reduce(mx[:, :].rearrange("p (j h) -> p j h", j=nj), source, AX, ALU.max).then_inc(s_max, 1)
                    dve.wait_ge(s_max, b * NT + i + 1)
                    dve.tensor_tensor(by_bank(sc[:, :, :]), source,
                                      mx[:, :].rearrange("p (j h) -> p j h", j=nj).unsqueeze(3).broadcast_to([P, nj, 4, S2]),
                                      ALU.subtract).then_inc(s_sub, 1)

                def norm(i):
                    o = m.ps[:, 6, 0:heads * (d + 1)].rearrange("p (h e) -> p h e", e=d + 1)
                    dve.wait_ge(o_full, b * NT + i + 2)
                    if adjust == "keep":
                        dve.tensor_scalar(rec[:, :].unsqueeze(2), o[:, :, d:d + 1], 1e-30, None, ALU.max).then_inc(adj_out, 1)
                        dve.wait_ge(adj_out, b * NT + i + 1)
                        dve.reciprocal(rec[:, :], rec[:, :]).then_inc(o_rec, 1)
                    else:
                        dve.reciprocal(rec[:, :].unsqueeze(2), o[:, :, d:d + 1]).then_inc(o_rec, 1)
                    dve.wait_ge(o_rec, b * NT + i + 1)
                    dve.wait_ge(oT_full, b * NT + i + 1)
                    dve.tensor_tensor(on[:, :].rearrange("p (h e) -> p h e", e=d), o[:, :, 0:d],
                                      rec[:, :].unsqueeze(2).broadcast_to([P, heads, d]), ALU.mult).then_inc(o_norm, 1)

                for i in range(NT):
                    soft(i)
                    if i >= 1:
                        norm(i - 1)
                norm(NT - 1)


def experts(nc, m, name, src, dst, n_exp, func, w1_d, w2_d, b1, b2, mode, gates_d=None):
    blocks = mode == "blocks"
    per_chunks = 1 if blocks else NC
    width = 2 * P if blocks else CH
    RING = 4
    LAG = 2
    names = ["w1_in", "w2_in", "w_high", "w1_split", "w2_split", "gate_in0", "gate_in1", "src_high", "src_split", "h_full", "h_raw", "h_high",
             "h_split", "y_step", "y_evac", "y_tmp"]
    with ExitStack() as ctx:
        sems = ctx.enter_context(phase(nc, [f"{name}_{s}" for s in names]))
        (w1_in, w2_in, w_high, w1_split, w2_split, gate_in0, gate_in1, src_high, src_split, h_full, h_raw, h_high,
         h_split, y_step, y_evac, y_tmp) = sems
        gate_in = [gate_in0, gate_in1]

        def sb(nm, shape, dt=F32):
            return ctx.enter_context(nc.sbuf_tensor(f"{name}_{nm}", shape, dt))

        slots = min(n_exp, 2)
        xh, xl = sb("xh", [P, KD, T], F32R), sb("xl", [P, KD, T], F32R)
        raw1, raw2 = sb("raw1", [P, KD, FF]), sb("raw2", [P, NF, D])
        w1h, w1l = sb("w1h", [P, slots, KD, FF], F32R), sb("w1l", [P, slots, KD, FF], F32R)
        w2h, w2l = sb("w2h", [P, slots, NF, D], F32R), sb("w2l", [P, slots, NF, D], F32R)
        hr = sb("hr", [P, RING, width])
        hh, hl = sb("hh", [P, RING, width], F32R), sb("hl", [P, RING, width], F32R)
        yt = sb("yt", [P, 2, width])
        if mode == "gated":
            gate = sb("gate", [P, 2, T])
        block = ctx.enter_context(nc.Block())

        def view(buf, k, c):
            if blocks:
                return buf[:, k, :].rearrange("p (b q) -> p b q", b=B)[:, :, bass.ds(c * P, P)]
            return buf[:, k, tok(c)]

        def cut(ap):
            return ap.rearrange("p (b q) -> p b q", b=B) if blocks else ap

        def units(eng):
            if n_exp == 1:
                for c, cc in chunks(eng):
                    yield 0, 0, c, c
            else:
                with eng.Fori(0, n_exp // 2) as i:
                    for par in range(2):
                        e = i * 2 + par
                        for c in range(per_chunks):
                            yield e, par, (e if blocks else c), i * (2 * per_chunks) + par * per_chunks + c

        TURN = 2 if n_exp == 1 else 2 * per_chunks

        @block.sync
        def _(sp):
            def load(e, par):
                ex = bass.ds(e, 1)
                for raw, w_d, w_in, w_split in ((raw1, w1_d, w1_in, w1_split), (raw2, w2_d, w2_in, w2_split)):
                    if not (isinstance(e, int) and e == 0):
                        sp.wait_ge(w_split, e)
                    sp.dma_start(raw[:, :, :], w_d[ex].rearrange("a (k p) n -> p (a k) n", p=P)).then_inc(w_in, 16)
                if mode == "gated":
                    if not (isinstance(e, int) and e < 2):
                        sp.wait_ge(y_evac, e * (2 * per_chunks) + 4 - 2 * per_chunks)
                    sp.dma_start(gate[:, par, :], gates_d[ex].broadcast_to([P, T])).then_inc(gate_in[par], 16)
            for e in range(slots):
                load(e, e)
            if n_exp > 1:
                with sp.Fori(1, n_exp // 2) as i:
                    for par in range(2):
                        load(i * 2 + par, par)

        @block.tensor
        def _(pe):
            def three(bank_ap, st_h, st_l, mv_h, mv_l, first, last):
                pe.matmul(bank_ap, st_h, mv_h, start=first, stop=False)
                pe.matmul(bank_ap, st_h, mv_l, start=False, stop=False)
                return pe.matmul(bank_ap, st_l, mv_h, start=False, stop=last)

            def hidden_of(J, f, e, par, c, j, unit):
                if f == 0:
                    if n_exp == 1 or blocks or unit == 0:
                        pe.wait_ge(src_split, NC if blocks else c + 1)
                    elif unit < NC:
                        pe.wait_ge(src_split, c + 1)
                    pe.wait_ge(w1_split, e + 1)
                pe.wait_ge(h_raw, J + 1)
                for k in range(KD):
                    mm = three(cut(m.ps[:, f % 4, 0:width]), w1h[:, par, k, f * P:(f + 1) * P], w1l[:, par, k, f * P:(f + 1) * P],
                               view(xh, k, c), view(xl, k, c), k == 0, k == KD - 1)
                mm.then_inc(h_full, 1)

            def out_of(J, f, e, par, c, j, unit):
                pe.wait_ge(h_split, J + RING + 1)
                if f == 0:
                    pe.wait_ge(w2_split, e + 1)
                    pe.wait_ge(y_evac, j * 2 + 2)
                for o in range(KD):
                    mm = three(m.ps[:, 4 + 2 * (unit % 2) + o, 0:width], w2h[:, par, f, o * P:(o + 1) * P], w2l[:, par, f, o * P:(o + 1) * P],
                               hh[:, f % RING, :], hl[:, f % RING, :], f == 0, f == NF - 1)
                mm.then_inc(y_step, 1)

            waiting = []
            for unit, (e, par, c, j) in enumerate(units(pe)):
                for f in range(NF):
                    here = (j * NF + f, f, e, par, c, j, unit)
                    hidden_of(*here)
                    waiting.append(here)
                    if len(waiting) > LAG:
                        out_of(*waiting.pop(0))
                if unit % TURN == TURN - 1:
                    while waiting:
                        out_of(*waiting.pop(0))

        @block.scalar
        def _(act):
            act.sem_inc(h_raw, RING)
            for c, cc in chunks(act):
                act.activation(xh[:, :, tok(c)], src[:, :, tok(c)], ACT.Copy).then_inc(src_high, 1)
            for e, par, c, j in units(act):
                for f in range(NF):
                    if b1 is None:
                        bias = 0.0
                    elif n_exp == 1:
                        bias = m.col(b1, f)
                    else:
                        bias = m.vec[:, bass.ds(e * NF + (VEC_AT[b1] + f), 1)]
                    wait_apart(m, act, h_full, j * NF + f + 1)
                    wait_apart(m, act, h_split, j * NF + f + 1)
                    act.activation(hr[:, f % RING, :], m.ps[:, f % 4, 0:width], func, bias=bias).then_inc(h_raw, 1)

        @block.gpsimd
        def _(pool):
            pool.sem_inc(y_step, RING)
            pool.sem_inc(y_evac, 4)

            def weights_of(e, par):
                if not (isinstance(e, int) and e < 2):
                    wait_apart(m, pool, y_step, e * (NF * per_chunks) - NF * per_chunks + RING)
                for z, (high, low, raw, w_in, w_split) in enumerate(((w1h, w1l, raw1, w1_in, w1_split), (w2h, w2l, raw2, w2_in, w2_split))):
                    wait_apart(m, pool, w_in, e * 16 + 16)
                    pool.tensor_scalar(high[:, par], raw[:, :, :], 1.0, 1.0, ALU.mult, ALU.mult).then_inc(w_high, 1)
                    wait_apart(m, pool, w_high, e * 2 + z + 1)
                    pool.tensor_tensor(low[:, par], raw[:, :, :], high[:, par].bitcast(F32), ALU.subtract).then_inc(w_split, 1)
            for e in range(slots):
                weights_of(e, e)
            if n_exp > 1:
                with pool.Fori(1, n_exp // 2) as i:
                    for par in range(2):
                        weights_of(i * 2 + par, par)

        @block.vector
        def _(dve):
            dve.sem_inc(h_split, RING)
            for c, cc in chunks(dve):
                dve.wait_ge(src_high, c + 1)
                dve.tensor_tensor(xl[:, :, tok(c)], src[:, :, tok(c)], xh[:, :, tok(c)].bitcast(F32), ALU.subtract).then_inc(src_split, 1)

            def outputs(e, par, c, j, unit):
                dve.wait_ge(y_step, j * NF + NF + RING)
                if mode == "gated":
                    dve.wait_ge(gate_in[par], e * 8 + 16 - 8 * par)
                for o in range(KD):
                    y = m.ps[:, 4 + 2 * (unit % 2) + o, 0:width]
                    to = view(dst, o, c)
                    if mode == "gated":
                        bias = m.vec[:, bass.ds(e * KD + (VEC_AT[b2] + o), 1)] if b2 else 0.0
                        dve.scalar_tensor_tensor(out=yt[:, o, :], in0=y, scalar=bias, in1=gate[:, par, tok(c)],
                                                 op0=ALU.add, op1=ALU.mult).then_inc(y_tmp, 1)
                        dve.wait_ge(y_tmp, j * 2 + o + 1)
                        dve.tensor_tensor(to, to, yt[:, o, :], ALU.add).then_inc(y_evac, 1)
                    else:
                        bias = m.vec[:, bass.ds(e * KD + (VEC_AT[b2] + o), 1)] if n_exp > 1 else m.col(b2, o)
                        dve.scalar_tensor_tensor(out=to, in0=cut(y), scalar=bias, in1=to, op0=ALU.add, op1=ALU.add).then_inc(y_evac, 1)

            last = None
            for unit, (e, par, c, j) in enumerate(units(dve)):
                for f in range(NF):
                    J = j * NF + f
                    dve.wait_ge(h_raw, J + RING + 1)
                    dve.wait_ge(y_step, J + 1)
                    dve.tensor_copy(hh[:, f % RING, :], hr[:, f % RING, :]).then_inc(h_high, 1)
                    dve.wait_ge(h_high, J + 1)
                    dve.tensor_tensor(hl[:, f % RING, :], hr[:, f % RING, :], hh[:, f % RING, :].bitcast(F32), ALU.subtract).then_inc(h_split, 1)
                    if f == LAG + 1 and last is not None:
                        outputs(*last)
                last = (e, par, c, j, unit)
                if unit % TURN == TURN - 1:
                    outputs(*last)
                    last = None


def feed_forward(nc, m, name, src, dst, n_exp, func, w1_d, w2_d, b1, b2, mode, gates_d=None):
    per_chunks = 1 if mode == "blocks" else NC
    width = 2 * P if mode == "blocks" else CH
    names = ["w_in0", "w_in1", "gate_in0", "gate_in1", "h_full", "h_evac", "y_full", "y_evac", "y_tmp", "y_tmp2",
             "unit", "whole", "quarter", "floor", "g0", "g1", "frac", "diff", "prod", "sum", "scaled", "hidden", "b1s"]
    with ExitStack() as ctx:
        sems = ctx.enter_context(phase(nc, [f"{name}_{s}" for s in names]))
        (w_in0, w_in1, gate_in0, gate_in1, h_full, h_evac, y_full, y_evac, y_tmp, y_tmp2, unit, whole, quart, floor,
         g0_done, g1_done, frac, diff, prod, summed, scaled, hidden, b1s_done) = sems
        w_in, gate_in = [w_in0, w_in1], [gate_in0, gate_in1]
        w1 = ctx.enter_context(nc.sbuf_tensor(f"{name}_w1", [P, 2, KD, FF], F32))
        w2 = ctx.enter_context(nc.sbuf_tensor(f"{name}_w2", [P, 2, NF, D], F32))
        h = ctx.enter_context(nc.sbuf_tensor(f"{name}_h", [P, 2, NF, CH], F32))
        yt = ctx.enter_context(nc.sbuf_tensor(f"{name}_yt", [P, 2, CH], F32))
        if mode == "gated":
            gate = ctx.enter_context(nc.sbuf_tensor(f"{name}_gate", [P, 2, T], F32))
        if mode == "fixed":
            HW = 4 * CH
            n_ = ctx.enter_context(nc.sbuf_tensor(f"{name}_n", [P, HW], F32))
            fl = ctx.enter_context(nc.sbuf_tensor(f"{name}_fl", [P, HW], F32))
            g0 = ctx.enter_context(nc.sbuf_tensor(f"{name}_g0", [P, HW], F32))
            g1 = ctx.enter_context(nc.sbuf_tensor(f"{name}_g1", [P, HW], F32))
            b1s = ctx.enter_context(nc.sbuf_tensor(f"{name}_b1s", [P, NF], F32))
        block = ctx.enter_context(nc.Block())

        def view(buf, k, c):
            if mode == "blocks":
                return buf[:, k, :].rearrange("p (b q) -> p b q", b=B)[:, :, bass.ds(c * P, P)]
            return buf[:, k, tok(c)]

        def bank(i):
            if mode == "blocks":
                return m.ps[:, i, 0:width].rearrange("p (b q) -> p b q", b=B)
            return m.ps[:, i, 0:width]

        def units(eng):
            if n_exp == 1:
                for c, cc in chunks(eng):
                    yield 0, 0, c, cc, c
            else:
                with eng.Fori(0, n_exp // 2) as i:
                    for par in range(2):
                        e = i * 2 + par
                        for c in range(per_chunks):
                            if mode == "blocks":
                                yield e, par, e, par, e
                            else:
                                yield e, par, c, c % 2, i * (2 * NC) + par * NC + c

        @block.sync
        def _(sp):
            def load(e, par):
                ex = bass.ds(e, 1)
                sp.dma_start(w1[:, par], w1_d[ex].rearrange("a (k p) n -> p (a k) n", p=P)).then_inc(w_in[par], 16)
                sp.dma_start(w2[:, par], w2_d[ex].rearrange("a (k p) n -> p (a k) n", p=P)).then_inc(w_in[par], 16)
                if mode == "gated":
                    sp.dma_start(gate[:, par, :], gates_d[ex].broadcast_to([P, T])).then_inc(gate_in[par], 16)
            for par in range(min(n_exp, 2)):
                load(par, par)
            if n_exp > 1:
                with sp.Fori(1, n_exp // 2) as i:
                    for par in range(2):
                        sp.wait_ge(y_evac, i * (4 * per_chunks) + 4 - 4 * per_chunks + 2 * per_chunks * (par + 1))
                        load(i * 2 + par, par)

        @block.tensor
        def _(pe):
            def hidden_of(e, par, c, slot, j, first):
                if first:
                    if n_exp == 1:
                        pe.wait_ge(w_in[par], 32)
                    else:
                        pe.wait_ge(w_in[par], (e // 2 + 1) * 32 if isinstance(e, int) else e * 16 + 32 - 16 * par)
                for f in range(NF):
                    pe.wait_ge(h_evac, j * NF + f + 1)
                    for k in range(KD):
                        mm = pe.matmul(bank(f % 4), w1[:, par, k, f * P:(f + 1) * P], view(src, k, c),
                                       start=k == 0, stop=k == KD - 1)
                    mm.then_inc(h_full, 1)

            def out_of(e, par, c, slot, j, first):
                if mode == "fixed":
                    pe.wait_ge(hidden, 2 * j + 2)
                else:
                    pe.wait_ge(h_evac, j * NF + NF + 4)
                for o in range(KD):
                    pe.wait_ge(y_evac, j * 2 + o + 1)
                    for f in range(NF):
                        mm = pe.matmul(bank(4 + 2 * slot + o), w2[:, par, f, o * P:(o + 1) * P],
                                       h[:, slot, f, 0:width] if mode != "blocks" else
                                       h[:, slot, f, 0:width].rearrange("p (b q) -> p b q", b=B),
                                       start=f == 0, stop=f == NF - 1)
                    mm.then_inc(y_full, 1)

            last = None
            turn = 2 if n_exp == 1 else 2 * per_chunks
            for i, un in enumerate(units(pe)):
                hidden_of(*un, first=un[2] == 0 if n_exp > 1 and mode != "blocks" else True)
                if last is not None:
                    out_of(*last, first=False)
                last = un
                if i % turn == turn - 1:
                    out_of(*un, first=False)
                    last = None

        @block.scalar
        def _(act):
            act.sem_inc(h_evac, 4)
            if mode == "fixed":
                act.wait_ge(b1s_done, 1)
            for e, par, c, slot, j in units(act):
                for f in range(NF):
                    wait_apart(m, act, h_full, j * NF + f + 1)
                    if mode == "fixed":
                        if f % 4 == 0:
                            act.wait_ge(summed, 2 * j + f // 4 + 1)
                        act.activation(n_[:, (f % 4) * CH:(f % 4 + 1) * CH], bank(f % 4), ACT.Identity,
                                       bias=b1s[:, f:f + 1], scale=FIX).then_inc(h_evac, 1)
                        if f % 4 == 3:
                            half = 2 * j + f // 4
                            act.wait_ge(floor, half + 1)
                            act.activation(g0[:, :], fl[:, :], ACT.Gelu, scale=0.25).then_inc(g0_done, 1)
                            act.activation(g1[:, :], fl[:, :], ACT.Gelu, scale=0.25, bias=m.quarter[:, 0:1]).then_inc(g1_done, 1)
                        continue
                    if f == 0:
                        wait_apart(m, act, y_full, j * 2 + 2)
                    if b1 is None:
                        bias = 0.0
                    elif n_exp == 1:
                        bias = m.col(b1, f)
                    else:
                        bias = m.vec[:, bass.ds(e * NF + (VEC_AT[b1] + f), 1)]
                    hv = h[:, slot, f, 0:width]
                    if mode == "blocks":
                        hv = hv.rearrange("p (b q) -> p b q", b=B)
                    act.activation(hv, bank(f % 4), func, bias=bias).then_inc(h_evac, 1)

        @block.gpsimd
        def _(pool):
            pool.sem_inc(y_full, 4)
            pool.sem_inc(summed, 1)
            if mode == "fixed":
                for c, cc in chunks(pool):
                    for hf in range(2):
                        half = 2 * c + hf
                        pool.wait_ge(g1_done, half + 1)
                        pool.wait_ge(g0_done, half + 1)
                        pool.tensor_tensor(g1[:, :], g1[:, :], g0[:, :], ALU.subtract).then_inc(diff, 1)

        @block.vector
        def _(dve):
            dve.sem_inc(y_evac, 4)
            if mode == "fixed":
                dve.tensor_scalar(b1s[:, :], m.vec[:, VEC_AT[b1]:VEC_AT[b1] + NF], FIX, None, ALU.mult).then_inc(b1s_done, 1)
            for e, par, c, slot, j in units(dve):
                if mode == "fixed":
                    for hf in range(2):
                        half = 2 * j + hf
                        dve.wait_ge(h_evac, j * NF + 4 * hf + 4 + 4)
                        dve.tensor_scalar(n_[:, :], n_[:, :], MAGIC, -MAGIC, ALU.add, ALU.add).then_inc(whole, 1)
                        dve.wait_ge(whole, half + 1)
                        dve.tensor_scalar(fl[:, :], n_[:, :], 4 / FIX, -(0.5 - 2 / FIX), ALU.mult, ALU.add).then_inc(quart, 1)
                        dve.wait_ge(quart, half + 1)
                        dve.tensor_scalar(fl[:, :], fl[:, :], MAGIC, -MAGIC, ALU.add, ALU.add).then_inc(floor, 1)
                        dve.wait_ge(floor, half + 1)
                        dve.scalar_tensor_tensor(out=n_[:, :], in0=n_[:, :], scalar=4 / FIX, in1=fl[:, :],
                                                 op0=ALU.mult, op1=ALU.subtract).then_inc(frac, 1)
                        dve.wait_ge(frac, half + 1)
                        dve.wait_ge(diff, half + 1)
                        dve.tensor_tensor(n_[:, :], n_[:, :], g1[:, :], ALU.mult).then_inc(prod, 1)
                        dve.wait_ge(prod, half + 1)
                        dve.tensor_tensor(g0[:, :], n_[:, :], g0[:, :], ALU.add).then_inc(summed, 1)
                        dve.wait_ge(summed, half + 2)
                        dve.tensor_scalar(g0[:, :], g0[:, :], FIX, MAGIC, ALU.mult, ALU.add).then_inc(scaled, 1)
                        dve.wait_ge(scaled, half + 1)
                        if hf == 0:
                            dve.wait_ge(y_full, 2 * j + 2)
                        dve.tensor_scalar(h[:, slot, 4 * hf:4 * hf + 4, :].rearrange("p f n -> p (f n)"), g0[:, :],
                                          -MAGIC, 1 / FIX, ALU.add, ALU.mult).then_inc(hidden, 1)
                if mode == "gated":
                    dve.wait_ge(gate_in[par], e * 8 + 16 - 8 * par)
                for o in range(KD):
                    dve.wait_ge(y_full, j * 2 + o + 1 + 4)
                    y = bank(4 + 2 * slot + o)
                    to = view(dst, o, c)
                    if mode == "gated":
                        bias = m.vec[:, bass.ds(e * KD + (VEC_AT[b2] + o), 1)] if b2 else 0.0
                        dve.scalar_tensor_tensor(out=yt[:, o, :], in0=y, scalar=bias, in1=gate[:, par, tok(c)],
                                                 op0=ALU.add, op1=ALU.mult).then_inc(y_tmp, 1)
                        dve.wait_ge(y_tmp, j * 2 + o + 1)
                        dve.tensor_tensor(to, to, yt[:, o, :], ALU.add).then_inc(y_evac, 1)
                    elif mode == "fixed":
                        dve.tensor_scalar(yt[:, o, :], y, m.col(b2, o), FIX, ALU.add, ALU.mult).then_inc(y_tmp, 1)
                        dve.wait_ge(y_tmp, j * 2 + o + 1)
                        dve.tensor_scalar(yt[:, o, :], yt[:, o, :], MAGIC, -MAGIC, ALU.add, ALU.add).then_inc(y_tmp2, 1)
                        dve.wait_ge(y_tmp2, j * 2 + o + 1)
                        dve.scalar_tensor_tensor(out=to, in0=yt[:, o, :], scalar=1 / FIX, in1=to,
                                                 op0=ALU.mult, op1=ALU.add).then_inc(y_evac, 1)
                    else:
                        bias = m.vec[:, bass.ds(e * KD + (VEC_AT[b2] + o), 1)] if n_exp > 1 else m.col(b2, o)
                        dve.scalar_tensor_tensor(out=to, in0=y, scalar=bias, in1=to, op0=ALU.add, op1=ALU.add).then_inc(y_evac, 1)


def router(nc, m, name, src, w_d, b_d, top, gates_d, tri_d):
    names = ["in", "full", "logit", "max", "shifted", "exp", "above", "equal", "ahead", "beat", "rank", "kept",
             "gate", "sum", "rec", "out", "t_full", "t_evac", "stored"]
    NTT = T // P
    with ExitStack() as ctx:
        sems = ctx.enter_context(phase(nc, [f"{name}_{s}" for s in names]))
        (loaded, full, logit, s_max, shifted, exp_done, above, equal, ahead, beat, rank_done, kept, gate_done, sum_done,
         rec_done, out, t_full, t_evac, stored) = sems

        def sb(nm, shape):
            return ctx.enter_context(nc.sbuf_tensor(f"{name}_{nm}", shape, F32))

        w = sb("w", [P, KD, E])
        bias = sb("bias", [P, E])
        tri = sb("tri", [P, E, E])
        sh = sb("sh", [P, NTT, E])
        lg, ex, col, rank, g = sb("lg", [P, NTT, E]), sb("ex", [P, NTT, E]), sb("col", [P, NTT]), sb("rank", [P, NTT, E]), sb("g", [P, NTT, E])
        gt, eq = sb("gt", [P, NTT, E, E]), sb("eq", [P, NTT, E, E])
        gT = sb("gT", [E, T])
        n_in = 3 if b_d is not None else 2
        block = ctx.enter_context(nc.Block())

        @block.sync
        def _(sp):
            sp.dma_start(w[:, :, :], w_d.rearrange("(k p) e -> p k e", p=P)).then_inc(loaded, 16)
            sp.dma_start(tri[:, :, :], tri_d).then_inc(loaded, 16)
            if b_d is not None:
                sp.dma_start(bias[:, :], b_d.broadcast_to([P, E])).then_inc(loaded, 16)
            sp.wait_ge(t_evac, 4)
            sp.dma_start(gates_d, gT[:, :]).then_inc(stored, 16)
            sp.wait_ge(stored, 16)

        @block.tensor
        def _(pe):
            pe.wait_ge(loaded, 16 * n_in)
            for i in range(NTT):
                for k in range(KD):
                    mm = pe.matmul(m.ps[:, 0, i * E:(i + 1) * E], src[:, k, i * P:(i + 1) * P], w[:, k, :],
                                   start=k == 0, stop=k == KD - 1)
            mm.then_inc(full, 1)
            pe.wait_ge(out, 1)
            for c in range(NC):
                for i in range(4 * c, 4 * c + 4):
                    mm = pe.transpose(m.ps[0:E, 4 + c, (i % 4) * P:(i % 4 + 1) * P], g[:, i, :], m.ident[:, :])
                mm.then_inc(t_full, 1)

        @block.scalar
        def _(act):
            act.wait_ge(shifted, 1)
            act.activation(ex[:, :, :], sh[:, :, :], ACT.Exp).then_inc(exp_done, 1)
            for c in range(NC):
                act.wait_ge(t_full, c + 1)
                act.activation(gT[:, c * CH:(c + 1) * CH], m.ps[0:E, 4 + c, :], ACT.Copy).then_inc(t_evac, 1)

        @block.vector
        def _(dve):
            dve.wait_ge(loaded, 16 * n_in)
            dve.wait_ge(full, 1)
            p3 = m.ps[:, 0, 0:NTT * E].rearrange("p (i e) -> p i e", e=E)
            if b_d is not None:
                dve.tensor_tensor(lg[:, :, :], p3, bias[:, :].unsqueeze(1).broadcast_to([P, NTT, E]), ALU.add).then_inc(logit, 1)
            else:
                dve.tensor_copy(lg[:, :, :], p3).then_inc(logit, 1)
            dve.wait_ge(logit, 1)
            dve.tensor_reduce(col[:, :], lg[:, :, :], AX, ALU.max).then_inc(s_max, 1)
            dve.wait_ge(s_max, 1)
            dve.tensor_tensor(sh[:, :, :], lg[:, :, :], col[:, :].unsqueeze(2).broadcast_to([P, NTT, E]), ALU.subtract).then_inc(shifted, 1)
            dve.wait_ge(shifted, 1)
            for i in range(NTT):
                lj = lg[:, i:i + 1, :].broadcast_to([P, E, E])
                le = lg[:, i, :].unsqueeze(2).broadcast_to([P, E, E])
                ins = dve.tensor_tensor(gt[:, i], lj, le, ALU.is_gt)
                ins2 = dve.tensor_tensor(eq[:, i], lj, le, ALU.is_equal)
            ins.then_inc(above, 1)
            ins2.then_inc(equal, 1)
            dve.wait_ge(above, 1)
            dve.wait_ge(equal, 1)
            dve.tensor_tensor(eq[:, :, :, :], eq[:, :, :, :], tri[:, :, :].unsqueeze(1).broadcast_to([P, NTT, E, E]), ALU.mult).then_inc(ahead, 1)
            dve.wait_ge(ahead, 1)
            dve.tensor_tensor(gt[:, :, :, :], gt[:, :, :, :], eq[:, :, :, :], ALU.add).then_inc(beat, 1)
            dve.wait_ge(beat, 1)
            dve.tensor_reduce(rank[:, :, :], gt[:, :, :, :], AX, ALU.add).then_inc(rank_done, 1)
            dve.wait_ge(rank_done, 1)
            dve.tensor_scalar(rank[:, :, :], rank[:, :, :], float(top), None, ALU.is_lt).then_inc(kept, 1)
            dve.wait_ge(kept, 1)
            dve.wait_ge(exp_done, 1)
            dve.tensor_tensor(g[:, :, :], ex[:, :, :], rank[:, :, :], ALU.mult).then_inc(gate_done, 1)
            dve.wait_ge(gate_done, 1)
            dve.tensor_reduce(col[:, :], g[:, :, :], AX, ALU.add).then_inc(sum_done, 1)
            dve.wait_ge(sum_done, 1)
            dve.reciprocal(col[:, :], col[:, :]).then_inc(rec_done, 1)
            dve.wait_ge(rec_done, 1)
            dve.tensor_tensor(g[:, :, :], g[:, :, :], col[:, :].unsqueeze(2).broadcast_to([P, NTT, E]), ALU.mult).then_inc(out, 1)


def self_attention(nc, m, src, dst, io):
    names = ["const", "vg_set", "v_full", "v_evac", "w_in", "job_full", "job_evac", "high", "keys", "v_group", "max_full", "max_part",
             "max_both", "max_ready", "s_full", "exp", "pv", "o_evac", "sum_full", "sum_rec", "o_norm", "o_out0", "o_out1", "back_in"]
    with ExitStack() as ctx:
        sems = ctx.enter_context(phase(nc, [f"self_{s}" for s in names]))
        (const, vg_set, v_full, v_evac, w_in, job_full, job_evac, high, keys, v_group, max_full, max_part, max_both, max_ready,
         s_full, exp_done, pv, o_evac, sum_full, sum_rec, o_norm, o_out0, o_out1, back_in) = sems
        o_out = [o_out0, o_out1]

        def sb(nm, shape, dt=F32):
            return ctx.enter_context(nc.sbuf_tensor(f"self_{nm}", shape, dt))

        w = sb("w", [P, 2, KD, P])
        wv = sb("wv", [P, KD, D])
        sel = sb("sel", [P, P])
        rows = sb("rows", [P, 7])
        hi = sb("hi", [P, 2, CH])
        q = sb("q", [P, S], F32R)
        qm = sb("qm", [P, S], F32R)
        kk = sb("kk", [P, S], F32R)
        km = sb("km", [P, 2, HG, S], F32R)
        v = sb("v", [P, B * NKC, SH, SD])
        vg = sb("vg", [P, 2, NKC, HG, 32])
        mp = sb("mp", [P, NT, HG, 2])
        mf = sb("mf", [P, NT, HG])
        mt = sb("mt", [P, NT, P])
        pr = sb("pr", [P, 2, HG, CH])
        o = sb("o", [P, CH])
        rec = sb("rec", [P, CH])
        on = sb("on", [P, 2, CH])
        o_d = nc.dram_tensor("self_out", (D, T), F32).ap()
        block = ctx.enter_context(nc.Block())
        RING = [7, 0, 1]
        STEPS = 2 * NKC
        UNITS = NT * HG * 2
        FIRST = 4
        PER = -(-UNITS // (STEPS - FIRST))

        def idx(g, b, n):
            return g * (2 * n) + b * n

        def groups(eng, body):
            with eng.Fori(0, NG - 1) as g:
                body(g, 0, (g, 1))
                body(g, 1, (g + 1, 0))
            body(NG - 1, 0, (NG - 1, 1))
            body(NG - 1, 1, None)

        def units_at(s):
            return range((s - FIRST) * PER, min(UNITS, (s - FIRST + 1) * PER)) if s >= FIRST else range(0)

        @block.sync
        def _(sp):
            def load(g):
                for z, nm in enumerate(("s_wq", "s_wk")):
                    sp.dma_start(w[:, z], io[nm][g].rearrange("a (k p) n -> p (a k) n", p=P)).then_inc(w_in, 16)
            sp.dma_start(wv[:, :, :], io["s_wv"].rearrange("(k p) n -> p k n", p=P)).then_inc(const, 16)
            sp.dma_start(sel[:, :], io["s_sel"]).then_inc(const, 16)
            sp.dma_start(rows[:, :], io["s_rows"]).then_inc(const, 16)
            load(slice(0, 1))

            def body(g, b, nxt):
                if b == 0 and nxt is not None and not isinstance(g, int):
                    sp.wait_ge(job_full, g * 12 + 10)
                    load(bass.ds(g + 1, 1))
                for half in range(2):
                    sp.wait_ge(o_norm, idx(g, b, 2) + half + 2)
                    for j in range(HG):
                        sp.dma_start(o_d[bass.ds(g * 32 + 8 * j, SD), b * S + half * CH:b * S + half * CH + CH],
                                     on[32 * j:32 * j + SD, half, :]).then_inc(o_out[half], 16)
            groups(sp, body)
            for half in range(2):
                sp.wait_ge(o_out[half], 64 + 64 * 2 * NG)
            sp.dma_start(dst[:, :, :], o_d.rearrange("(k p) n -> p k n", p=P)).then_inc(back_in, 16)
            sp.wait_ge(back_in, 16)

        @block.tensor
        def _(pe):
            pe.wait_ge(const, 48)
            for i in range(B * NKC):
                if i >= 2:
                    pe.wait_ge(v_evac, i - 1)
                for k in range(KD):
                    mm = pe.matmul(m.ps[:, i % 2, 0:D], src[:, k, i * P:(i + 1) * P], wv[:, k, :], start=k == 0, stop=k == KD - 1)
                mm.then_inc(v_full, 1)
            pe.wait_ge(v_evac, B * NKC)

            def proj_mm(bank, z, half, b):
                for k in range(KD):
                    mm = pe.matmul(m.ps[:, bank, :], w[:, z, k, :], src[:, k, b * S + half * CH:b * S + half * CH + CH],
                                   start=k == 0, stop=k == KD - 1)
                mm.then_inc(job_full, 1)

            def max_units(g, b, us, jobs):
                for un in us:
                    if un == 0:
                        pe.wait_ge(keys, idx(g, b, HG) + HG)
                        pe.wait_ge(job_evac, jobs)
                    pe.wait_ge(max_part, idx(g, b, UNITS) + un + 1)
                    i, j, half = un // (2 * HG), un // 2 % HG, un % 2
                    pe.matmul(m.ps[:, un % 2, :], q[:, i * P:(i + 1) * P], km[:, b, j, half * CH:(half + 1) * CH],
                              start=True, stop=True).then_inc(max_full, 1)

            pe.wait_ge(w_in, 32)
            for r in range(4):
                pe.wait_ge(job_evac, r + 1)
                proj_mm(RING[r % 3], r // 2, r % 2, 0)
            max_units(0, 0, range(UNITS), 4 + 3)

            def body(g, b, nxt):
                pe.wait_ge(max_ready, idx(g, b, 1) + 1)
                for half in range(2):
                    pe.wait_ge(job_evac, idx(g, b, 6) + 4 + half + 1)
                    for i in range(4):
                        mm = pe.transpose(m.ps[:, RING[(4 + half) % 3], i * P:(i + 1) * P], mt[:, half * 4 + i, :], m.ident[:, :])
                    mm.then_inc(job_full, 1)

                def values(s):
                    half, kc = s // NKC, s % NKC
                    pe.wait_ge(exp_done, idx(g, b, 2 * STEPS) + 2 * s + 2 + 2)
                    if s == 0:
                        pe.wait_ge(v_group, idx(g, b, 1) + 1)
                    if kc == 0:
                        pe.wait_ge(o_evac, idx(g, b, 2) + half + 1)
                    for j in range(HG):
                        mm = pe.matmul(m.ps[32 * j:32 * j + 32, 6, :], vg[:, b, kc, j, :], pr[:, s % 2, j, :],
                                       start=kc == 0, stop=kc == NKC - 1)
                    mm.then_inc(pv, 1)

                def sums(half):
                    pe.wait_ge(o_evac, idx(g, b, 2) + half + 2)
                    pe.wait_ge(job_evac, idx(g, b, 6) + (6 if nxt is None else 10) + 3)
                    pe.matmul(m.ps[:, 7, :], sel[:, :], o[:, :], start=True, stop=True).then_inc(sum_full, 1)

                for s in range(STEPS):
                    half, kc = s // NKC, s % NKC
                    if kc == 0:
                        pe.wait_ge(job_evac, idx(g, b, 6) + 4 + half + 1 + 3)
                    for pair in range(2):
                        pe.wait_ge(exp_done, idx(g, b, 2 * STEPS) + 2 * s + pair + 1)
                        for jj in range(2):
                            mm = pe.matmul(m.ps[:, 2 + 2 * pair + jj, :], km[:, b, 2 * pair + jj, kc * P:(kc + 1) * P],
                                           qm[:, half * CH:(half + 1) * CH], start=True, stop=True)
                        mm.then_inc(s_full, 1)
                    if nxt is not None and s < 4:
                        job = idx(g, b, 6) + 6 + s
                        if s == 0:
                            pe.wait_ge(w_in, nxt[0] * 32 + 32)
                            pe.wait_ge(sum_rec, idx(g, b, 2) + 1)
                        pe.wait_ge(job_evac, job + 1)
                        proj_mm(RING[s % 3], s // 2, s % 2, nxt[1])
                    if s >= 1:
                        values(s - 1)
                    if nxt is not None:
                        max_units(*nxt, units_at(s), idx(g, b, 6) + 10 + 3)
                    if s == NKC + 1:
                        sums(0)
                values(STEPS - 1)
                sums(1)
            groups(pe, body)

        @block.scalar
        def _(act):
            act.sem_inc(exp_done, 2)
            act.sem_inc(o_evac, 1)
            for i in range(B * NKC):
                act.wait_ge(v_full, i + 1)
                act.activation(v[:, i], m.ps[:, i % 2, 0:D].rearrange("p (h d) -> p h d", d=SD), ACT.Copy).then_inc(v_evac, 1)

            def high_part(r, bank, full_at, n_before):
                act.wait_ge(job_full, full_at)
                act.wait_ge(job_evac, full_at + 1)
                act.activation(hi[:, r % 2, :], m.ps[:, bank, :], ACT.Copy, scale=rows[:, r // 2:r // 2 + 1]).then_inc(high, 1)

            act.wait_ge(const, 48)
            for r in range(4):
                high_part(r, RING[r % 3], r + 1, 0)

            def body(g, b, nxt):
                for s in range(STEPS):
                    act.wait_ge(pv, idx(g, b, STEPS) + s + 1)
                    for pair in range(2):
                        act.wait_ge(s_full, idx(g, b, 2 * STEPS) + 2 * s + pair + 1)
                        act.activation(pr[:, s % 2, 2 * pair:2 * pair + 2, :], m.ps[:, 2 + 2 * pair:4 + 2 * pair, :], ACT.Exp,
                                       scale=1.0 / float(np.float32(np.sqrt(SD)))).then_inc(exp_done, 1)
                    if nxt is not None and s < 4:
                        high_part(s, RING[s % 3], idx(g, b, 6) + 6 + s + 1, 0)
                    if s in (NKC, STEPS - 1):
                        half = s // NKC - (s == NKC)
                        act.wait_ge(pv, idx(g, b, STEPS) + NKC * (half + 1) + 2)
                        act.wait_ge(o_norm, idx(g, b, 2) + half + 1)
                        act.activation(o[:, :], m.ps[:, 6, :], ACT.Copy).then_inc(o_evac, 1)
            groups(act, body)

        @block.gpsimd
        def _(pool):
            pool.sem_inc(pv, 2)
            for half in range(2):
                pool.sem_inc(o_out[half], 64)
            pool.memset(vg[:, :, :, :, :], 0.0).then_inc(vg_set, 1)
            pool.wait_ge(vg_set, 1)
            pool.memset(vg[:, :, :, :, SD:SD + 1], 1.0).then_inc(vg_set, 1)
            pool.wait_ge(vg_set, 2)
            pool.wait_ge(const, 48)

            def prepare(g, b, jobs):
                pool.tensor_copy(vg[:, b, :, :, 0:SD], v[:, b * NKC:(b + 1) * NKC, bass.ds(g * HG, HG), :]).then_inc(v_group, 1)
                wait_apart(m, pool, job_evac, jobs)
                for j in range(HG):
                    pool.tensor_scalar(km[:, b, j, :], kk[:, :].bitcast(F32), rows[:, 3 + j:4 + j], 1.0, ALU.mult, ALU.mult).then_inc(keys, 1)

            pool.wait_ge(v_evac, B * NKC)
            prepare(0, 0, 4 + 3)

            def body(g, b, nxt):
                if nxt is not None:
                    pool.wait_ge(pv, idx(g, b, STEPS) + 2)
                    prepare(*nxt, idx(g, b, 6) + 10 + 3)
            groups(pool, body)

        @block.vector
        def _(dve):
            dve.sem_inc(job_evac, 3)
            dve.sem_inc(max_part, 2)
            dve.sem_inc(sum_rec, 1)
            dve.sem_inc(o_norm, 1)
            dve.memset(mt[:, :, :], 0.0).then_inc(max_both, 1)
            dve.wait_ge(max_both, 1)
            dve.wait_ge(const, 48)

            def split(r, bank, full_at, high_at):
                z, half = r // 2, r % 2
                dve.wait_ge(job_full, full_at)
                dve.wait_ge(high, high_at)
                at = slice(half * CH, (half + 1) * CH)
                if z == 0:
                    dve.tensor_tensor(q[:, at], m.ps[:, bank, :], hi[:, r % 2, :], ALU.subtract).then_inc(job_evac, 1)
                else:
                    dve.scalar_tensor_tensor(out=kk[:, at], in0=m.ps[:, bank, :], scalar=rows[:, 2:3], in1=hi[:, r % 2, :],
                                             op0=ALU.add, op1=ALU.subtract).then_inc(job_evac, 1)

            def maxima(g, b, us):
                for un in us:
                    i, j, half = un // (2 * HG), un // 2 % HG, un % 2
                    dve.wait_ge(max_full, idx(g, b, UNITS) + un + 1)
                    dve.tensor_reduce(mp[:, i, j, half:half + 1], m.ps[:, un % 2, :], AX, ALU.max).then_inc(max_part, 1)
                    if un == UNITS - 1:
                        dve.wait_ge(max_part, idx(g, b, UNITS) + UNITS + 2)
                        dve.tensor_tensor(mf[:, :, :], mp[:, :, :, 0:1].rearrange("p i j a -> p i (j a)"),
                                          mp[:, :, :, 1:2].rearrange("p i j a -> p i (j a)"), ALU.max).then_inc(max_both, 1)
                        dve.wait_ge(max_both, idx(g, b, 1) + 2)
                        dve.tensor_scalar(mt[:, :, 24:P:32], mf[:, :, :], -1.0, None, ALU.mult).then_inc(max_ready, 1)

            for r in range(4):
                split(r, RING[r % 3], r + 1, r + 1)
            maxima(0, 0, range(UNITS))

            def body(g, b, nxt):
                for half in range(2):
                    at = slice(half * CH, (half + 1) * CH)
                    dve.wait_ge(job_full, idx(g, b, 6) + 4 + half + 1)
                    dve.tensor_tensor(qm[:, at], m.ps[:, RING[(4 + half) % 3], :], q[:, at].bitcast(F32), ALU.add).then_inc(job_evac, 1)

                def normalise(half):
                    dve.wait_ge(sum_full, idx(g, b, 2) + half + 1)
                    dve.reciprocal(rec[:, :], m.ps[:, 7, :]).then_inc(sum_rec, 1)
                    dve.wait_ge(sum_rec, idx(g, b, 2) + half + 2)
                    dve.wait_ge(o_out[half], idx(g, b, 64) + 64)
                    dve.tensor_tensor(on[:, half, :], o[:, :], rec[:, :], ALU.mult).then_inc(o_norm, 1)

                for s in range(STEPS):
                    if nxt is not None:
                        if s < 4:
                            split(s, RING[s % 3], idx(g, b, 6) + 6 + s + 1, idx(*nxt, 4) + s + 1)
                        maxima(*nxt, units_at(s))
                    if s == NKC + 1:
                        normalise(0)
                normalise(1)
            groups(dve, body)


def build(nc, io, out):
    class M:
        pass
    m = M()
    with ExitStack() as ctx:
        def sb(name, shape, dt=F32):
            return ctx.enter_context(nc.sbuf_tensor(name, shape, dt))
        m.ps = ctx.enter_context(nc.psum_tensor("ps", [P, 8, 512], F32))
        x, n = (sb(nm, [P, KD, T]) for nm in "xn")
        m.vec = sb("vec_sb", [P, NVEC])
        m.mean_w, m.ident = sb("mean_w", [P, P]), sb("ident_sb", [P, P])
        m.eps, m.quarter = sb("eps", [P, 1]), sb("quarter", [P, 1])
        m.wp = sb("wp", [P, 4, KD, D])

        def col(name, i):
            at = VEC_AT[name] + i
            return m.vec[:, at:at + 1]
        m.col = col
        m.passed = ctx.enter_context(nc.semaphore("passed"))
        gates_d = [nc.dram_tensor(f"gates{i}", (E, T), F32).ap() for i in range(2)]

        with phase(nc, ["x_in", "const_set"]) as (x_in, const_set), nc.Block() as block:
            @block.sync
            def _(sp):
                sp.dma_start(x[:, :, :], io["xT"].rearrange("(k p) n -> p k n", p=P)).then_inc(x_in, 16)
                sp.dma_start(m.vec[:, :], io["vec"]).then_inc(x_in, 16)
                sp.dma_start(m.ident[:, :], io["ident"]).then_inc(x_in, 16)
                sp.wait_ge(x_in, 48)

            @block.vector
            def _(dve):
                dve.memset(m.mean_w[:, :], 1.0 / D)
                dve.memset(m.eps[:, :], EPS)
                dve.memset(m.quarter[:, :], 0.25).then_inc(const_set, 1)
                dve.wait_ge(const_set, 1)

        def norm(name, src, dst, g=None, b=None):
            with ExitStack() as sc:
                m.sq = sc.enter_context(nc.sbuf_tensor(f"{name}_sq", [P, 2, KD, CH], F32))
                m.std = sc.enter_context(nc.sbuf_tensor(f"{name}_std", [P, T], F32))
                m.rs = sc.enter_context(nc.sbuf_tensor(f"{name}_rs", [P, 2, CH], F32))
                layer_norm(nc, m, name, src, dst, g, b)

        @contextmanager
        def scratch(i):
            with nc.sbuf_tensor(f"u{i}", [P, KD, T], F32) as u, nc.sbuf_tensor(f"t{i}", [P, KD, T], F32) as t:
                yield u, t

        def store(src):
            with phase(nc, ["stored"]) as (stored,), nc.Block() as block:
                @block.sync
                def _(sp):
                    sp.dma_start(out.rearrange("(k p) n -> p k n", p=P), src[:, :, :]).then_inc(stored, 16)
                    sp.wait_ge(stored, 16)

        with scratch(0) as (u, t):
            norm("n0", x, n)
            load_weights(nc, m, [(0, io["a_wsv"]), (1, io["a_wso"])])
            linear(nc, m, "sv", n, 0, t, bias="a_bsv")
            linear(nc, m, "so", t, 1, u, bias="a_bso", plus=n)
            norm("n1", u, u, "ln1_g", "ln1_b")
            load_weights(nc, m, [(s, io[f"a_w{k}"]) for s, k in enumerate("qokv")])
            cross_attention(nc, m, "xa", u, t, 8, None, 1.0 / float(np.sqrt(np.float32(32))), "a_bq", "a_bk", io["a_bv"], io)
            linear(nc, m, "ao", t, 1, n, bias="a_bo", plus=u)
        norm("n2", n, n, "ln2_g", "ln2_b")
        experts(nc, m, "fa", n, n, 1, ACT.Relu, io["fa_w1"], io["fa_w2"], "fa_b1", "fa_b2", "dense")
        norm("n3", n, n, "ln3_g", "ln3_b")
        add(nc, m, "r0", x, n)

        norm("n4", x, n)
        with scratch(1) as (u, t):
            norm("n5", n, u, "lni_g", "lni_b")
            self_attention(nc, m, u, t, io)
            load_weights(nc, m, [(0, io["s_wo"])])
            linear(nc, m, "wo", t, 0, n, plus=n)
        experts(nc, m, "f0", n, x, E, ACT.Gelu, io["f0_w1"], io["f0_w2"], "f0_b1", "f0_b2", "blocks")

        norm("n6", x, n)
        with scratch(2) as (u, t):
            load_weights(nc, m, [(s, io[f"b_w{k}"]) for s, k in enumerate("qokv")])
            cross_attention(nc, m, "xb", n, t, 16, "replace", 0.25, "b_bq", "b_bk", io["b_bv"], io)
            linear(nc, m, "bo", t, 1, x, bias="b_bo", plus=x)
        norm("n7", x, n)
        router(nc, m, "r1", n, io["r1_w"], None, 4, gates_d[0], io["tri"])
        experts(nc, m, "f1", n, x, E, ACT.Gelu_apprx_tanh, io["f1_w1"], io["f1_w2"], None, None, "gated", gates_d[0])

        norm("n8", x, n)
        with scratch(3) as (u, t):
            load_weights(nc, m, [(s, io[f"c_w{k}"]) for s, k in enumerate("qokv")])
            cross_attention(nc, m, "xc", n, t, 16, "bias", 1.0, None, None, None, io)
            linear(nc, m, "co", t, 1, x, plus=x)
        norm("n9", x, n)
        with scratch(4) as (u, t):
            load_weights(nc, m, [(0, io["r2_w1"])])
            linear(nc, m, "rh", n, 0, u, bias="r2_b1", func=ACT.Silu)
            router(nc, m, "r2", u, io["r2_w2"], io["r2_b2"], 2, gates_d[1], io["tri"])
        add(nc, m, "r2x", x, n)
        experts(nc, m, "f2", n, x, E, ACT.Silu, io["f2_w1"], io["f2_w2"], "f2_b1", "f2_b2", "gated", gates_d[1])

        norm("n10", x, n)
        with scratch(5) as (u, t):
            load_weights(nc, m, [(s, io[f"d_w{k}"]) for s, k in enumerate("qokv")])
            cross_attention(nc, m, "xd", n, t, 16, "keep", 0.25, "d_bq", "d_bk", io["d_bv"], io)
            linear(nc, m, "do", t, 1, x, bias="d_bo", plus=x)
        norm("n11", x, n)
        feed_forward(nc, m, "f3", n, x, 1, None, io["f3_w1"], io["f3_w2"], "f3_b1", "f3_b2", "fixed")
        store(x)


def bucket(offset):
    half, exact = BUCKETS // 2, BUCKETS // 4
    r = np.abs(offset)
    far = np.log(np.maximum(r, 1).astype(np.float32) / np.float32(exact)) / np.float32(np.log(128 / exact)) * np.float32(half - exact)
    return half * (offset > 0) + np.where(r < exact, r, np.minimum(exact + far.astype(np.int32), half - 1))


def lay_out(a):
    f = lambda v: np.asarray(v)
    c = np.ascontiguousarray
    io = {"xT": c(f(a["x"]).reshape(T, D).T), "ctxT": c(f(a["ctx_1024"]).reshape(B * S2, D).T)}
    io["ctxT_reversed"] = c(f(a["ctx_1024"])[:, ::-1].reshape(B * S2, D).T)
    vec = {}
    io["a_wsv"], io["a_wso"] = c(f(a["L0_xattn_qkv_w"])[2 * D:].T), c(f(a["L0_xattn_sa_out_w"]).T)
    for z, k in enumerate("qkv"):
        io[f"a_w{k}"] = c(f(a["L0_xattn_in_proj_w"])[z * D:(z + 1) * D].T)
    io["a_wo"] = c(f(a["L0_xattn_mha_out_w"]).T)
    bi = f(a["L0_xattn_in_proj_b"])
    vec["a_bsv"], vec["a_bso"] = f(a["L0_xattn_qkv_b"])[2 * D:], a["L0_xattn_sa_out_b"]
    vec["a_bq"], vec["a_bk"], vec["a_bo"] = bi[0:D], bi[D:2 * D], a["L0_xattn_mha_out_b"]
    io["a_bv"] = c(bi[2 * D:].reshape(1, D))
    io["fa_w1"], io["fa_w2"] = c(f(a["L0_xattn_lin1_w"]).T[None]), c(f(a["L0_xattn_lin2_w"]).T[None])
    vec["fa_b1"], vec["fa_b2"] = a["L0_xattn_lin1_b"], a["L0_xattn_lin2_b"]
    for i in (1, 2, 3):
        vec[f"ln{i}_g"], vec[f"ln{i}_b"] = a[f"L0_xattn_ln{i}_g"], a[f"L0_xattn_ln{i}_b"]
    vec["lni_g"], vec["lni_b"] = a["L0_ffn_ln_g"], a["L0_ffn_ln_b"]
    for nm, key in (("s_wq", "L0_ffn_wq"), ("s_wk", "L0_ffn_wk")):
        w = f(a[key]).reshape(D, NG, HG, SD).transpose(1, 0, 2, 3)
        s = np.zeros((NG, D, HG, 4, SD), w.dtype)
        s[:, :, :, 0:3] = w[:, :, :, None]
        io[nm] = s.reshape(NG, D, P)
    io["s_wv"], io["s_wo"] = f(a["L0_ffn_wv"]), f(a["L0_ffn_wo"])
    io["f0_w1"], io["f0_w2"], vec["f0_b1"], vec["f0_b2"] = (f(a[f"L0_ffn_{k}"]) for k in ("w1", "w2", "b1", "b2"))
    for k in "qkvo":
        io[f"b_w{k}"] = f(a[f"L1_xattn_w{k}"])
        io[f"c_w{k}"] = f(a[f"L2_xattn_w{k}"])
        io[f"d_w{k}"] = c(f(a[f"L3_xattn_W{'p' if k == 'o' else k}"]).T)
    for k in "qko":
        vec[f"b_b{k}"], vec[f"d_b{k}"] = a[f"L1_xattn_b{k}"], a[f"L3_xattn_b{'p' if k == 'o' else k}"]
    io["b_bv"], io["d_bv"] = c(f(a["L1_xattn_bv"]).reshape(1, D)), c(f(a["L3_xattn_bv"]).reshape(1, D))
    io["r1_w"], io["f1_w1"], io["f1_w2"] = f(a["L1_ffn_router_w"]), f(a["L1_ffn_up_w"]), f(a["L1_ffn_down_w"])
    io["r2_w1"], io["r2_w2"], io["r2_b2"] = f(a["L2_ffn_rw1"]), f(a["L2_ffn_rw2"]), c(f(a["L2_ffn_rb2"]).reshape(1, E))
    vec["r2_b1"] = a["L2_ffn_rb1"]
    io["f2_w1"], io["f2_w2"], vec["f2_b1"], vec["f2_b2"] = (f(a[f"L2_ffn_{k}"]) for k in ("we1", "we2", "be1", "be2"))
    io["rel"] = f(a["L2_xattn_rel_bias"])
    io["f3_w1"], io["f3_w2"] = f(a["L3_ffn_w1"])[None], f(a["L3_ffn_w2"])[None]
    vec["f3_b1"], vec["f3_b2"] = a["L3_ffn_b1"], a["L3_ffn_b2"]
    io["vec"] = c(np.concatenate([f(vec[nm]).reshape(k, P) for nm, k in VECS]).T)
    io["mask_q"] = c(f(a["mask_1x1xSxS2_ik0"]).reshape(S, S2))
    io["mask_b"] = f(a["mask_BxS2_ik0"])
    io["mask_bT"] = c(f(a["mask_BxS2_ik0"]).T)
    p = np.arange(P)
    io["ident"] = np.eye(P, dtype=np.float32)
    io["one"] = np.ones((1, S2), np.float32)
    for hb in (4, 8):
        io[f"rows{hb}"] = (p[:, None] // (P // hb) == np.arange(hb)).astype(np.float32)
    io["s_sel"] = (p[:, None] == 32 * (p // 32) + SD).astype(np.float32)
    part, row = p % 32 // SD, p % 32
    io["s_rows"] = c(np.stack([part == 2, part == 1, row == 24] + [p // 32 == j for j in range(HG)], 1).astype(np.float32))
    io["tri"] = c(np.broadcast_to(np.arange(E)[None, :] < np.arange(E)[:, None], (P, E, E)).astype(np.float32))
    io["hot"] = (bucket(S2 - 1 - np.arange(OFFS))[None, :] == np.arange(BUCKETS)[:, None]).astype(np.float32)
    return io


def kernel(**inputs):
    import concourse.bacc as bacc
    from concourse.bass_utils import run_bass_kernel_spmd

    laid = lay_out(inputs)
    arrays = {f"in_{name}": v for name, v in laid.items()}
    nc = bacc.Bacc("TRN2", target_bir_lowering=False, num_devices=1)
    io = {name: nc.dram_tensor(f"in_{name}", v.shape, mybir.dt.from_np(v.dtype), kind="ExternalInput").ap()
          for name, v in laid.items()}
    out = nc.dram_tensor("out", (D, T), F32, kind="ExternalOutput").ap()
    build(nc, io, out)
    r = run_bass_kernel_spmd(nc, [arrays], core_ids=[0])
    return np.ascontiguousarray(r.results[0]["out"].T).reshape(B, S, D)
```

```python
from contextlib import ExitStack, contextmanager

import numpy as np

import concourse.bass as bass
from concourse import mybir

F32 = mybir.dt.float32
F32R = mybir.dt.float32r
I32 = mybir.dt.int32
ALU = mybir.AluOpType
ACT = mybir.ActivationFunctionType
AX = mybir.AxisListType.X

P = 128
B, S, D = 2, 1024, 256
T = B * S
KD = D // P
CH = 512
NC = T // CH
S2 = 77
FF = 1024
NF = FF // P
E = 8
EPS = 1e-5
MAGIC = 1.5 * 2.0 ** 23
FIX = 256.0
BIG = 1e30
NT = S // P
BUCKETS = 32
OFFS = S + S2 - 1

SH = 32
SD = D // SH
HG = 4
NG = SH // HG
NKC = S // P

VECS = [
    ("a_bsv", 2), ("a_bso", 2), ("a_bq", 2), ("a_bk", 2), ("a_bo", 2), ("fa_b1", 8), ("fa_b2", 2),
    ("ln1_g", 2), ("ln1_b", 2), ("ln2_g", 2), ("ln2_b", 2), ("ln3_g", 2), ("ln3_b", 2),
    ("lni_g", 2), ("lni_b", 2), ("f0_b1", 64), ("f0_b2", 16),
    ("b_bq", 2), ("b_bk", 2), ("b_bo", 2),
    ("r2_b1", 2), ("f2_b1", 64), ("f2_b2", 16),
    ("d_bq", 2), ("d_bk", 2), ("d_bo", 2), ("f3_b1", 8), ("f3_b2", 2),
]
VEC_AT = {}
for _name, _k in VECS:
    VEC_AT[_name] = sum(k for nm, k in VECS[:len(VEC_AT)])
NVEC = sum(k for _, k in VECS)


@contextmanager
def phase(nc, names):
    with ExitStack() as ctx:
        sems = [ctx.enter_context(nc.semaphore(name)) for name in names]
        yield sems
        with nc.Block() as block:
            @block.gpsimd
            def _(pool):
                for s in sems:
                    pool.sem_clear(s)


def chunks(eng):
    with eng.Fori(0, B) as b:
        for cc in range(2):
            yield b * 2 + cc, cc


def tok(c):
    return bass.ds(c * CH, CH)


def wait_apart(m, eng, sem, value):
    eng.wait_ge(sem, value)
    eng.sem_inc(m.passed, 1)


def layer_norm(nc, m, name, src, dst, gain=None, shift=None):
    names = [f"{name}_{s}" for s in ("mean", "centred", "squared", "var", "root", "recip", "scaled")]
    with phase(nc, names) as (mean, centred, squared, var, root, recip, scaled), nc.Block() as block:
        @block.tensor
        def _(pe):
            for c, cc in chunks(pe):
                pe.wait_ge(centred, c + 1)
                for k in range(KD):
                    mm = pe.matmul(m.ps[:, cc, :], m.mean_w[:, :], src[:, k, tok(c)], start=k == 0, stop=k == KD - 1)
                mm.then_inc(mean, 1)
            for c, cc in chunks(pe):
                pe.wait_ge(squared, c + 1)
                pe.wait_ge(root, c + 1)
                for k in range(KD):
                    mm = pe.matmul(m.ps[:, 2 + cc, :], m.mean_w[:, :], m.sq[:, cc, k, :], start=k == 0, stop=k == KD - 1)
                mm.then_inc(var, 1)

        @block.vector
        def _(dve):
            dve.sem_inc(centred, 2)
            for c, cc in chunks(dve):
                dve.wait_ge(mean, c + 1)
                for k in range(KD):
                    ins = dve.tensor_tensor(dst[:, k, tok(c)], src[:, k, tok(c)], m.ps[:, cc, :], ALU.subtract)
                ins.then_inc(centred, 1)
            for c, cc in chunks(dve):
                dve.wait_ge(root, 2 + c + 1)
                dve.wait_ge(scaled, c + 1)
                dve.reciprocal(m.rs[:, cc, :], m.std[:, tok(c)]).then_inc(recip, 1)
            if gain:
                for c, cc in chunks(dve):
                    dve.wait_ge(scaled, 2 + c + 1)
                    dve.tensor_scalar(dst[:, 0, tok(c)], dst[:, 0, tok(c)], m.col(gain, 0), m.col(shift, 0), ALU.mult, ALU.add)
                    dve.tensor_scalar(dst[:, 1, tok(c)], dst[:, 1, tok(c)], m.col(gain, 1), m.col(shift, 1), ALU.mult, ALU.add)

        @block.scalar
        def _(act):
            act.sem_inc(root, 2)
            for c, cc in chunks(act):
                act.wait_ge(centred, 2 + c + 1)
                wait_apart(m, act, var, c + 1)
                act.activation(m.sq[:, cc, :, :], dst[:, :, tok(c)], ACT.Square).then_inc(squared, 1)
            for c, cc in chunks(act):
                wait_apart(m, act, var, 2 + c + 1)
                act.activation(m.std[:, tok(c)], m.ps[:, 2 + cc, :], ACT.Sqrt, bias=m.eps[:, 0:1]).then_inc(root, 1)

        @block.gpsimd
        def _(pool):
            pool.sem_inc(var, 2)
            pool.sem_inc(scaled, 2)
            for c, cc in chunks(pool):
                wait_apart(m, pool, recip, c + 1)
                for k in range(KD):
                    ins = pool.tensor_tensor(dst[:, k, tok(c)], dst[:, k, tok(c)], m.rs[:, cc, :], ALU.mult)
                ins.then_inc(scaled, 1)


def load_weights(nc, m, slots):
    with phase(nc, ["weights_in"]) as (loaded,), nc.Block() as block:
        @block.sync
        def _(sp):
            for slot, w in slots:
                sp.dma_start(m.wp[:, slot], w.rearrange("(k p) n -> p k n", p=P)).then_inc(loaded, 16)
            sp.wait_ge(loaded, 16 * len(slots))


def linear(nc, m, name, src, slot, dst, bias=None, func=ACT.Identity, plus=None):
    with phase(nc, [f"{name}_{s}" for s in ("full", "evac", "added")]) as (full, evac, added), nc.Block() as block:
        @block.tensor
        def _(pe):
            for c, cc in chunks(pe):
                for j in range(KD):
                    pe.wait_ge(evac, 2 * c + j + 1)
                    for k in range(KD):
                        mm = pe.matmul(m.ps[:, 2 * cc + j, :], m.wp[:, slot, k, j * P:(j + 1) * P], src[:, k, tok(c)],
                                       start=k == 0, stop=k == KD - 1)
                    mm.then_inc(full, 1)

        if plus is None:
            @block.scalar
            def _(act):
                act.sem_inc(evac, 4)
                for c, cc in chunks(act):
                    for j in range(KD):
                        wait_apart(m, act, full, 2 * c + j + 1)
                        act.activation(dst[:, j, tok(c)], m.ps[:, 2 * cc + j, :], func,
                                       bias=m.col(bias, j) if bias else 0.0).then_inc(evac, 1)
        else:
            @block.vector
            def _(dve):
                dve.sem_inc(evac, 4)
                for c, cc in chunks(dve):
                    for j in range(KD):
                        dve.wait_ge(full, 2 * c + j + 1)
                        dve.scalar_tensor_tensor(out=dst[:, j, tok(c)], in0=m.ps[:, 2 * cc + j, :],
                                                 scalar=m.col(bias, j) if bias else 0.0,
                                                 in1=plus[:, j, tok(c)], op0=ALU.add, op1=ALU.add).then_inc(evac, 1)


def add(nc, m, name, dst, src):
    with nc.Block() as block:
        @block.vector
        def _(dve):
            for c, cc in chunks(dve):
                dve.tensor_tensor(dst[:, :, tok(c)], dst[:, :, tok(c)], src[:, :, tok(c)], ALU.add)


def cross_attention(nc, m, name, src, dst, heads, adjust, scale, bq, bk, bv_row, io):
    d = D // heads
    hb = P // d
    hv = 8
    nj = hv // 4
    nr = heads // hv
    NU = NT * nr
    names = ["in", "kv_full", "kv_evac", "ones_col", "diag", "q_full", "q_evac", "s_full", "adj1", "adjusted",
             "s_max", "s_sub", "exp", "t_full", "floor", "t_evac", "o_full", "o_rec", "o_norm", "oT_full", "oT_evac",
             "adj_in", "adj_out", "tb_full", "tb_evac", "tb_out", "bias_in0", "bias_in1"]
    with ExitStack() as ctx:
        sems = ctx.enter_context(phase(nc, [f"{name}_{s}" for s in names]))
        (loaded, kv_full, kv_evac, ones_col, diag, q_full, q_evac, s_full, adj1, adjusted, s_max, s_sub, exp_done,
         t_full, floor, t_evac, o_full, o_rec, o_norm, oT_full, oT_evac, adj_in, adj_out, tb_full, tb_evac, tb_out,
         bias_in0, bias_in1) = sems
        bias_in = [bias_in0, bias_in1]

        def sb(nm, shape, dt=F32):
            return ctx.enter_context(nc.sbuf_tensor(f"{name}_{nm}", shape, dt))

        ctxT = sb("ctxT", [P, KD, B * S2])
        kT = sb("kT", [P, KD, B * S2])
        rows = sb("rows", [P, hb])
        k_diag = sb("k_diag", [P, B, KD, hb, S2])
        val = sb("val", [S2, B, heads, d + 1])
        bv = sb("bv", [1, D])
        one = sb("one", [1, S2])
        qT = sb("qT", [P, KD, S])
        sc = sb("sc", [P, 2, hv, S2])
        pr = sb("pr", [P, 2, hv, S2])
        prT = sb("prT", [S2, 2, hv, P])
        mx = sb("mx", [P, 2, hv])
        rec = sb("rec", [P, heads])
        on = sb("on", [P, 2, D])
        if adjust == "replace":
            mask_i = sb("mask_i", [P, NT, S2], I32)
            keep = sb("keep", [P, NT, S2])
            low = sb("low", [P, NT, S2])
        if adjust == "keep":
            mask_i = sb("mask_i", [P, B, S2], I32)
            keep = sb("keep", [P, B, S2])
            low = sb("low", [P, B, S2])
            mask_c = sb("mask_c", [S2, B], I32)
            keep_c = sb("keep_c", [S2, B])
        if adjust == "bias":
            bias_t = sb("bias_t", [P, 2, heads, S2])
            rel = sb("rel", [BUCKETS, heads])
            hot = sb("hot", [BUCKETS, OFFS])
            by_off = sb("by_off", [heads, OFFS])
            by_off_d = nc.dram_tensor("bias_by_offset", (heads, OFFS), F32).ap()
        n_in = 3 + (bv_row is not None) + {None: 0, "replace": 1, "keep": 3, "bias": 2}[adjust]

        block = ctx.enter_context(nc.Block())

        s_read = {None: s_sub, "replace": adj_out, "keep": adjusted, "bias": adjusted}[adjust]

        def credit(sem):
            return 2 if sem is s_read else 0

        def by_bank(a):
            return a.rearrange("p (j h) s -> p j h s", j=nj)

        @block.sync
        def _(sp):
            sp.dma_start(ctxT[:, :, :], io["ctxT_reversed" if adjust == "bias" else "ctxT"].rearrange("(k p) n -> p k n", p=P)).then_inc(loaded, 16)
            sp.dma_start(rows[:, :], io[f"rows{hb}"]).then_inc(loaded, 16)
            sp.dma_start(one[:, :], io["one"]).then_inc(loaded, 16)
            if bv_row is not None:
                sp.dma_start(bv[:, :], bv_row).then_inc(loaded, 16)
            if adjust == "replace":
                sp.dma_start(mask_i[:, :, :], io["mask_q"].rearrange("(t p) s -> p t s", p=P)).then_inc(loaded, 16)
            if adjust == "keep":
                for b in range(B):
                    sp.dma_start(mask_i[:, b, :], io["mask_b"][b:b + 1, :].broadcast_to([P, S2])).then_inc(loaded, 16)
                sp.dma_start(mask_c[:, :], io["mask_bT"]).then_inc(loaded, 16)
            if adjust == "bias":
                sp.dma_start(rel[:, :], io["rel"]).then_inc(loaded, 16)
                sp.dma_start(hot[:, :], io["hot"]).then_inc(loaded, 16)
                sp.wait_ge(tb_evac, 3)
                sp.dma_start(by_off_d, by_off[:, :]).then_inc(tb_out, 16)
                sp.wait_ge(tb_out, 16)
                for i in range(B * NT):
                    if i >= 2:
                        sp.wait_ge(adjusted, nr * (i - 1) + 2)
                    sp.dma_start(bias_t[:, i % 2], bass.AP(by_off_d.tensor, (i % NT) * P, [[1, P], [OFFS, heads], [1, S2]])
                                 ).then_inc(bias_in[i % 2], 16)

        @block.tensor
        def _(pe):
            pe.wait_ge(loaded, 16 * n_in)
            for j in range(KD):
                for k in range(KD):
                    mm = pe.matmul(m.ps[:, j, 0:B * S2], m.wp[:, 2, k, j * P:(j + 1) * P], ctxT[:, k, :],
                                   start=k == 0, stop=k == KD - 1)
                mm.then_inc(kv_full, 1)
            for b in range(B):
                for k in range(KD):
                    mm = pe.matmul(m.ps[0:S2, 2 + b, 0:D], ctxT[:, k, b * S2:(b + 1) * S2], m.wp[:, 3, k, :],
                                   start=k == 0, stop=k == KD - 1 and bv_row is None)
                if bv_row is not None:
                    mm = pe.matmul(m.ps[0:S2, 2 + b, 0:D], one[:, :], bv[:, :], start=False, stop=True)
                mm.then_inc(kv_full, 1)
            if adjust == "bias":
                for i in range(3):
                    w = min(512, OFFS - 512 * i)
                    pe.matmul(m.ps[0:heads, 4 + i, 0:w], rel[:, :], hot[:, 512 * i:512 * i + w],
                              start=True, stop=True).then_inc(tb_full, 1)
                pe.wait_ge(tb_evac, 3)
            pe.wait_ge(kv_evac, 4)
            pe.wait_ge(diag, B * KD)

            with pe.Fori(0, B) as b:
                pe.wait_ge(s_read, b * NU + 2)
                for cc in range(2):
                    for j in range(KD):
                        for k in range(KD):
                            mm = pe.matmul(m.ps[:, 2 * cc + j, :], m.wp[:, 0, k, j * P:(j + 1) * P],
                                           src[:, k, tok(b * 2 + cc)], start=k == 0, stop=k == KD - 1)
                        mm.then_inc(q_full, 1)

                def scores_of(n):
                    i, r = n // nr, n % nr
                    if n >= 2:
                        pe.wait_ge(s_read, b * NU + n + 1)
                    for j in range(nj):
                        fb, h = (hv * r + 4 * j) // hb, (hv * r + 4 * j) % hb
                        mm = pe.matmul(m.ps[:, 2 * (n % 2) + j, 0:4 * S2], qT[:, fb, i * P:(i + 1) * P],
                                       k_diag[:, bass.ds(b, 1), fb, h:h + 4, :].rearrange("p a h s -> p (a h s)"),
                                       start=True, stop=True)
                    mm.then_inc(s_full, 1)

                def turn(n):
                    pe.wait_ge(exp_done, b * NU + n + 3)
                    pe.wait_ge(t_evac, b * NU + n + 1)
                    for hh in range(hv):
                        mm = pe.transpose(m.ps[0:S2, 4 + hh // 4, (hh % 4) * P:(hh % 4 + 1) * P], pr[:, n % 2, hh, :], m.ident[:, :])
                    mm.then_inc(t_full, 1)

                def values(n):
                    i, r = n // nr, n % nr
                    pe.wait_ge(t_evac, b * NU + n + 2)
                    if r == 0:
                        pe.wait_ge(o_norm, b * NT + i + 1)
                    for hh in range(hv):
                        h = hv * r + hh
                        mm = pe.matmul(m.ps[:, 6, h * (d + 1):(h + 1) * (d + 1)], prT[:, n % 2, hh, :],
                                       val[:, bass.ds(b, 1), h, :].rearrange("p a e -> p (a e)"), start=True, stop=True)
                    mm.then_inc(o_full, 1)

                def back(i):
                    pe.wait_ge(o_norm, b * NT + i + 2)
                    pe.wait_ge(oT_evac, b * NT + i + 1)
                    for k in range(KD):
                        mm = pe.transpose(m.ps[:, 7, k * P:(k + 1) * P], on[:, i % 2, k * P:(k + 1) * P], m.ident[:, :])
                    mm.then_inc(oT_full, 1)

                pe.wait_ge(q_evac, b * 4 + 4)
                scores_of(0)
                scores_of(1)
                for n in range(NU + 3):
                    if n + 2 < NU:
                        scores_of(n + 2)
                    if n < NU:
                        turn(n)
                    if 1 <= n <= NU:
                        values(n - 1)
                    if n >= 3 and (n - 3) % nr == nr - 1:
                        back((n - 3) // nr)

        @block.scalar
        def _(act):
            act.sem_inc(t_evac, 1)
            act.sem_inc(oT_evac, 1)
            act.sem_inc(exp_done, 2)
            for j in range(KD):
                act.wait_ge(kv_full, j + 1)
                act.activation(kT[:, j, :], m.ps[:, j, 0:B * S2], ACT.Identity,
                               bias=m.col(bk, j) if bk else 0.0).then_inc(kv_evac, 1)
            act.wait_ge(ones_col, 1)
            for b in range(B):
                act.wait_ge(kv_full, KD + b + 1)
                v = m.ps[0:S2, 2 + b, 0:D].rearrange("s (h d) -> s h d", d=d)
                if adjust == "keep":
                    act.activation(val[:, b, :, 0:d], v, ACT.Copy, scale=keep_c[:, b:b + 1]).then_inc(kv_evac, 1)
                else:
                    act.activation(val[:, b, :, 0:d], v, ACT.Copy).then_inc(kv_evac, 1)
            if adjust == "bias":
                for i in range(3):
                    w = min(512, OFFS - 512 * i)
                    act.wait_ge(tb_full, i + 1)
                    act.activation(by_off[:, 512 * i:512 * i + w], m.ps[0:heads, 4 + i, 0:w], ACT.Copy).then_inc(tb_evac, 1)

            with act.Fori(0, B) as b:
                for cc in range(2):
                    for j in range(KD):
                        act.wait_ge(q_full, b * 4 + 2 * cc + j + 1)
                        act.activation(qT[:, j, cc * CH:(cc + 1) * CH], m.ps[:, 2 * cc + j, :], ACT.Identity,
                                       bias=m.col(bq, j) if bq else 0.0).then_inc(q_evac, 1)

                def exp_of(n):
                    act.wait_ge(s_sub, b * NU + n + 1 + credit(s_sub))
                    act.wait_ge(t_full, b * NU + n + 1)
                    act.activation(pr[:, n % 2], sc[:, n % 2], ACT.Exp, scale=scale).then_inc(exp_done, 1)

                exp_of(0)
                for n in range(NU + 3):
                    if n + 1 < NU:
                        exp_of(n + 1)
                    if n < NU:
                        act.wait_ge(t_full, b * NU + n + 3)
                        act.wait_ge(o_full, b * NU + n + 1)
                        act.activation(prT[:, n % 2].rearrange("s (c h) q -> s c h q", c=2),
                                       m.ps[0:S2, 4:6, :].rearrange("s c (h q) -> s c h q", q=P), ACT.Copy).then_inc(t_evac, 1)
                    if n >= 3 and (n - 3) % nr == nr - 1:
                        i = (n - 3) // nr
                        wait_apart(m, act, oT_full, b * NT + i + 3)
                        act.activation(dst[:, :, bass.ds(b * S + i * P, P)],
                                       m.ps[:, 7, 0:D].rearrange("p (k q) -> p k q", k=KD), ACT.Copy).then_inc(oT_evac, 1)

        @block.gpsimd
        def _(pool):
            pool.sem_inc(o_full, 2)
            pool.sem_inc(t_full, 2)
            pool.sem_inc(oT_full, 2)

        @block.vector
        def _(dve):
            dve.sem_inc(s_read, 2)
            dve.sem_inc(o_norm, 1)
            dve.wait_ge(loaded, 16 * n_in)
            if adjust == "keep":
                dve.tensor_scalar(keep_c[:, :], mask_c[:, :], 0.0, None, ALU.not_equal).then_inc(adj1, 1)
                dve.tensor_scalar(keep[:, :, :], mask_i[:, :, :], 0.0, None, ALU.not_equal).then_inc(adj1, 1)
                dve.wait_ge(adj1, 2)
                dve.tensor_scalar(low[:, :, :], keep[:, :, :], -1.0, BIG, ALU.add, ALU.mult).then_inc(adj1, 1)
                for b in range(B):
                    ins = dve.tensor_copy(val[:, b, :, d:d + 1].rearrange("s h a -> s (h a)"),
                                          keep_c[:, b:b + 1].broadcast_to([S2, heads]))
                ins.then_inc(ones_col, 1)
                dve.wait_ge(adj1, 3)
            else:
                dve.memset(val[:, :, :, d:d + 1], 1.0).then_inc(ones_col, 1)
            if adjust == "replace":
                dve.tensor_scalar(keep[:, :, :], mask_i[:, :, :], 0.0, None, ALU.not_equal).then_inc(adj1, 1)
                dve.wait_ge(adj1, 1)
                dve.tensor_scalar(low[:, :, :], keep[:, :, :], -1.0, 1e9 / scale, ALU.add, ALU.mult).then_inc(adj1, 1)
                dve.wait_ge(adj1, 2)
            dve.wait_ge(kv_evac, KD)
            for b in range(B):
                for k in range(KD):
                    dve.tensor_tensor(k_diag[:, b, k], kT[:, k, b * S2:(b + 1) * S2].unsqueeze(1).broadcast_to([P, hb, S2]),
                                      rows[:, :].unsqueeze(2).broadcast_to([P, hb, S2]), ALU.mult).then_inc(diag, 1)

            with dve.Fori(0, B) as b:
                def soft(n):
                    i, r = n // nr, n % nr
                    at = b * NU + n + 1
                    s3, s4 = sc[:, n % 2], by_bank(sc[:, n % 2])
                    dve.wait_ge(s_full, at)
                    dve.wait_ge(exp_done, at)
                    source = m.ps[:, 2 * (n % 2):2 * (n % 2) + nj, 0:4 * S2].rearrange("p j (h s) -> p j h s", s=S2)
                    if adjust == "replace":
                        k4 = keep[:, i:i + 1, :].unsqueeze(1).broadcast_to([P, nj, 4, S2])
                        l3 = low[:, i:i + 1, :].broadcast_to([P, hv, S2])
                        dve.tensor_tensor(s4, source, k4, ALU.mult).then_inc(adj_out, 1)
                        dve.wait_ge(adj_out, at + 2)
                        dve.tensor_tensor(s3, s3, l3, ALU.add).then_inc(adjusted, 1)
                    if adjust == "keep":
                        l4 = low[:, bass.ds(b, 1), :].unsqueeze(1).broadcast_to([P, nj, 4, S2])
                        dve.tensor_tensor(s4, source, l4, ALU.add).then_inc(adjusted, 1)
                    if adjust == "bias":
                        dve.wait_ge(bias_in[i % 2], b * (8 * NT) + 16 * (i // 2 + 1))
                        dve.tensor_tensor(s4, source, by_bank(bias_t[:, i % 2, hv * r:hv * (r + 1)]), ALU.add).then_inc(adjusted, 1)
                    if adjust:
                        dve.wait_ge(adjusted, at + credit(adjusted))
                        source = s4
                    dve.tensor_reduce(mx[:, n % 2, :].rearrange("p (j h) -> p j h", j=nj), source, AX, ALU.max).then_inc(s_max, 1)
                    dve.wait_ge(s_max, at)
                    dve.tensor_tensor(s4, source, mx[:, n % 2, :].rearrange("p (j h) -> p j h", j=nj).unsqueeze(3).broadcast_to([P, nj, 4, S2]),
                                      ALU.subtract).then_inc(s_sub, 1)

                def norm(i):
                    o = m.ps[:, 6, 0:heads * (d + 1)].rearrange("p (h e) -> p h e", e=d + 1)
                    dve.wait_ge(o_full, b * NU + (i + 1) * nr + 2)
                    if adjust == "keep":
                        dve.tensor_scalar(rec[:, :].unsqueeze(2), o[:, :, d:d + 1], 1e-30, None, ALU.max).then_inc(floor, 1)
                        dve.wait_ge(floor, b * NT + i + 1)
                        dve.reciprocal(rec[:, :], rec[:, :]).then_inc(o_rec, 1)
                    else:
                        dve.reciprocal(rec[:, :].unsqueeze(2), o[:, :, d:d + 1]).then_inc(o_rec, 1)
                    dve.wait_ge(o_rec, b * NT + i + 1)
                    dve.wait_ge(oT_full, b * NT + i + 1)
                    dve.tensor_tensor(on[:, i % 2, :].rearrange("p (h e) -> p h e", e=d), o[:, :, 0:d],
                                      rec[:, :].unsqueeze(2).broadcast_to([P, heads, d]), ALU.mult).then_inc(o_norm, 1)

                for n in range(NU + 2):
                    if n < NU:
                        soft(n)
                    if n >= 2 and (n - 2) % nr == nr - 1:
                        norm((n - 2) // nr)


def experts(nc, m, name, src, dst, n_exp, func, w1_d, w2_d, b1, b2, mode, gates_d=None):
    blocks = mode == "blocks"
    per_chunks = 1 if blocks else NC
    width = 2 * P if blocks else CH
    RING = 4
    LAG = 2
    names = ["w1_in", "w2_in", "w_high", "w1_split", "w2_split", "gate_in0", "gate_in1", "src_high", "src_split", "h_full", "h_raw", "h_high",
             "h_split", "y_step", "y_evac", "y_tmp"]
    with ExitStack() as ctx:
        sems = ctx.enter_context(phase(nc, [f"{name}_{s}" for s in names]))
        (w1_in, w2_in, w_high, w1_split, w2_split, gate_in0, gate_in1, src_high, src_split, h_full, h_raw, h_high,
         h_split, y_step, y_evac, y_tmp) = sems
        gate_in = [gate_in0, gate_in1]

        def sb(nm, shape, dt=F32):
            return ctx.enter_context(nc.sbuf_tensor(f"{name}_{nm}", shape, dt))

        slots = min(n_exp, 2)
        xh, xl = sb("xh", [P, KD, T], F32R), sb("xl", [P, KD, T], F32R)
        raw1, raw2 = sb("raw1", [P, KD, FF]), sb("raw2", [P, NF, D])
        w1h, w1l = sb("w1h", [P, slots, KD, FF], F32R), sb("w1l", [P, slots, KD, FF], F32R)
        w2h, w2l = sb("w2h", [P, slots, NF, D], F32R), sb("w2l", [P, slots, NF, D], F32R)
        hr = sb("hr", [P, RING, width])
        hh, hl = sb("hh", [P, RING, width], F32R), sb("hl", [P, RING, width], F32R)
        yt = sb("yt", [P, 2, width])
        if mode == "gated":
            gate = sb("gate", [P, 2, T])
        block = ctx.enter_context(nc.Block())

        def view(buf, k, c):
            if blocks:
                return buf[:, k, :].rearrange("p (b q) -> p b q", b=B)[:, :, bass.ds(c * P, P)]
            return buf[:, k, tok(c)]

        def cut(ap):
            return ap.rearrange("p (b q) -> p b q", b=B) if blocks else ap

        def units(eng):
            if n_exp == 1:
                for c, cc in chunks(eng):
                    yield 0, 0, c, c
            else:
                with eng.Fori(0, n_exp // 2) as i:
                    for par in range(2):
                        e = i * 2 + par
                        for c in range(per_chunks):
                            yield e, par, (e if blocks else c), i * (2 * per_chunks) + par * per_chunks + c

        TURN = 2 if n_exp == 1 else 2 * per_chunks

        @block.sync
        def _(sp):
            def load(e, par):
                ex = bass.ds(e, 1)
                for raw, w_d, w_in, w_split in ((raw1, w1_d, w1_in, w1_split), (raw2, w2_d, w2_in, w2_split)):
                    if not (isinstance(e, int) and e == 0):
                        sp.wait_ge(w_split, e)
                    sp.dma_start(raw[:, :, :], w_d[ex].rearrange("a (k p) n -> p (a k) n", p=P)).then_inc(w_in, 16)
                if mode == "gated":
                    if not (isinstance(e, int) and e < 2):
                        sp.wait_ge(y_evac, e * (2 * per_chunks) + 4 - 2 * per_chunks)
                    sp.dma_start(gate[:, par, :], gates_d[ex].broadcast_to([P, T])).then_inc(gate_in[par], 16)
            for e in range(slots):
                load(e, e)
            if n_exp > 1:
                with sp.Fori(1, n_exp // 2) as i:
                    for par in range(2):
                        load(i * 2 + par, par)

        @block.tensor
        def _(pe):
            def three(bank_ap, st_h, st_l, mv_h, mv_l, first, last):
                pe.matmul(bank_ap, st_h, mv_h, start=first, stop=False)
                pe.matmul(bank_ap, st_h, mv_l, start=False, stop=False)
                return pe.matmul(bank_ap, st_l, mv_h, start=False, stop=last)

            def hidden_of(J, f, e, par, c, j, unit):
                if f == 0:
                    if n_exp == 1 or blocks or unit == 0:
                        pe.wait_ge(src_split, NC if blocks else c + 1)
                    elif unit < NC:
                        pe.wait_ge(src_split, c + 1)
                    pe.wait_ge(w1_split, e + 1)
                pe.wait_ge(h_raw, J + 1)
                for k in range(KD):
                    mm = three(cut(m.ps[:, f % 4, 0:width]), w1h[:, par, k, f * P:(f + 1) * P], w1l[:, par, k, f * P:(f + 1) * P],
                               view(xh, k, c), view(xl, k, c), k == 0, k == KD - 1)
                mm.then_inc(h_full, 1)

            def out_of(J, f, e, par, c, j, unit):
                pe.wait_ge(h_split, J + RING + 1)
                if f == 0:
                    pe.wait_ge(w2_split, e + 1)
                    pe.wait_ge(y_evac, j * 2 + 2)
                for o in range(KD):
                    mm = three(m.ps[:, 4 + 2 * (unit % 2) + o, 0:width], w2h[:, par, f, o * P:(o + 1) * P], w2l[:, par, f, o * P:(o + 1) * P],
                               hh[:, f % RING, :], hl[:, f % RING, :], f == 0, f == NF - 1)
                mm.then_inc(y_step, 1)

            waiting = []
            for unit, (e, par, c, j) in enumerate(units(pe)):
                for f in range(NF):
                    here = (j * NF + f, f, e, par, c, j, unit)
                    hidden_of(*here)
                    waiting.append(here)
                    if len(waiting) > LAG:
                        out_of(*waiting.pop(0))
                if unit % TURN == TURN - 1:
                    while waiting:
                        out_of(*waiting.pop(0))

        @block.scalar
        def _(act):
            act.sem_inc(h_raw, RING)
            for c, cc in chunks(act):
                act.activation(xh[:, :, tok(c)], src[:, :, tok(c)], ACT.Copy).then_inc(src_high, 1)
            for e, par, c, j in units(act):
                for f in range(NF):
                    if b1 is None:
                        bias = 0.0
                    elif n_exp == 1:
                        bias = m.col(b1, f)
                    else:
                        bias = m.vec[:, bass.ds(e * NF + (VEC_AT[b1] + f), 1)]
                    wait_apart(m, act, h_full, j * NF + f + 1)
                    wait_apart(m, act, h_split, j * NF + f + 1)
                    act.activation(hr[:, f % RING, :], m.ps[:, f % 4, 0:width], func, bias=bias).then_inc(h_raw, 1)

        @block.gpsimd
        def _(pool):
            pool.sem_inc(y_step, RING)
            pool.sem_inc(y_evac, 4)

            def weights_of(e, par):
                if not (isinstance(e, int) and e < 2):
                    wait_apart(m, pool, y_step, e * (NF * per_chunks) - NF * per_chunks + RING)
                for z, (high, low, raw, w_in, w_split) in enumerate(((w1h, w1l, raw1, w1_in, w1_split), (w2h, w2l, raw2, w2_in, w2_split))):
                    wait_apart(m, pool, w_in, e * 16 + 16)
                    pool.tensor_scalar(high[:, par], raw[:, :, :], 1.0, 1.0, ALU.mult, ALU.mult).then_inc(w_high, 1)
                    wait_apart(m, pool, w_high, e * 2 + z + 1)
                    pool.tensor_tensor(low[:, par], raw[:, :, :], high[:, par].bitcast(F32), ALU.subtract).then_inc(w_split, 1)
            for e in range(slots):
                weights_of(e, e)
            if n_exp > 1:
                with pool.Fori(1, n_exp // 2) as i:
                    for par in range(2):
                        weights_of(i * 2 + par, par)

        @block.vector
        def _(dve):
            dve.sem_inc(h_split, RING)
            for c, cc in chunks(dve):
                dve.wait_ge(src_high, c + 1)
                dve.tensor_tensor(xl[:, :, tok(c)], src[:, :, tok(c)], xh[:, :, tok(c)].bitcast(F32), ALU.subtract).then_inc(src_split, 1)

            def outputs(e, par, c, j, unit):
                dve.wait_ge(y_step, j * NF + NF + RING)
                if mode == "gated":
                    dve.wait_ge(gate_in[par], e * 8 + 16 - 8 * par)
                for o in range(KD):
                    y = m.ps[:, 4 + 2 * (unit % 2) + o, 0:width]
                    to = view(dst, o, c)
                    if mode == "gated":
                        bias = m.vec[:, bass.ds(e * KD + (VEC_AT[b2] + o), 1)] if b2 else 0.0
                        dve.scalar_tensor_tensor(out=yt[:, o, :], in0=y, scalar=bias, in1=gate[:, par, tok(c)],
                                                 op0=ALU.add, op1=ALU.mult).then_inc(y_tmp, 1)
                        dve.wait_ge(y_tmp, j * 2 + o + 1)
                        dve.tensor_tensor(to, to, yt[:, o, :], ALU.add).then_inc(y_evac, 1)
                    else:
                        bias = m.vec[:, bass.ds(e * KD + (VEC_AT[b2] + o), 1)] if n_exp > 1 else m.col(b2, o)
                        dve.scalar_tensor_tensor(out=to, in0=cut(y), scalar=bias, in1=to, op0=ALU.add, op1=ALU.add).then_inc(y_evac, 1)

            last = None
            for unit, (e, par, c, j) in enumerate(units(dve)):
                for f in range(NF):
                    J = j * NF + f
                    dve.wait_ge(h_raw, J + RING + 1)
                    dve.wait_ge(y_step, J + 1)
                    dve.tensor_copy(hh[:, f % RING, :], hr[:, f % RING, :]).then_inc(h_high, 1)
                    dve.wait_ge(h_high, J + 1)
                    dve.tensor_tensor(hl[:, f % RING, :], hr[:, f % RING, :], hh[:, f % RING, :].bitcast(F32), ALU.subtract).then_inc(h_split, 1)
                    if f == LAG + 1 and last is not None:
                        outputs(*last)
                last = (e, par, c, j, unit)
                if unit % TURN == TURN - 1:
                    outputs(*last)
                    last = None


def feed_forward(nc, m, name, src, dst, n_exp, func, w1_d, w2_d, b1, b2, mode, gates_d=None):
    per_chunks = 1 if mode == "blocks" else NC
    width = 2 * P if mode == "blocks" else CH
    names = ["w_in0", "w_in1", "gate_in0", "gate_in1", "h_full", "h_evac", "y_full", "y_evac", "y_tmp", "y_tmp2",
             "unit", "whole", "quarter", "floor", "g0", "g1", "frac", "diff", "prod", "sum", "scaled", "hidden", "b1s"]
    with ExitStack() as ctx:
        sems = ctx.enter_context(phase(nc, [f"{name}_{s}" for s in names]))
        (w_in0, w_in1, gate_in0, gate_in1, h_full, h_evac, y_full, y_evac, y_tmp, y_tmp2, unit, whole, quart, floor,
         g0_done, g1_done, frac, diff, prod, summed, scaled, hidden, b1s_done) = sems
        w_in, gate_in = [w_in0, w_in1], [gate_in0, gate_in1]
        w1 = ctx.enter_context(nc.sbuf_tensor(f"{name}_w1", [P, 2, KD, FF], F32))
        w2 = ctx.enter_context(nc.sbuf_tensor(f"{name}_w2", [P, 2, NF, D], F32))
        h = ctx.enter_context(nc.sbuf_tensor(f"{name}_h", [P, 2, NF, CH], F32))
        yt = ctx.enter_context(nc.sbuf_tensor(f"{name}_yt", [P, 2, CH], F32))
        if mode == "gated":
            gate = ctx.enter_context(nc.sbuf_tensor(f"{name}_gate", [P, 2, T], F32))
        if mode == "fixed":
            HW = 4 * CH
            n_ = ctx.enter_context(nc.sbuf_tensor(f"{name}_n", [P, HW], F32))
            fl = ctx.enter_context(nc.sbuf_tensor(f"{name}_fl", [P, HW], F32))
            g0 = ctx.enter_context(nc.sbuf_tensor(f"{name}_g0", [P, HW], F32))
            g1 = ctx.enter_context(nc.sbuf_tensor(f"{name}_g1", [P, HW], F32))
            b1s = ctx.enter_context(nc.sbuf_tensor(f"{name}_b1s", [P, NF], F32))
        block = ctx.enter_context(nc.Block())

        def view(buf, k, c):
            if mode == "blocks":
                return buf[:, k, :].rearrange("p (b q) -> p b q", b=B)[:, :, bass.ds(c * P, P)]
            return buf[:, k, tok(c)]

        def bank(i):
            if mode == "blocks":
                return m.ps[:, i, 0:width].rearrange("p (b q) -> p b q", b=B)
            return m.ps[:, i, 0:width]

        def units(eng):
            if n_exp == 1:
                for c, cc in chunks(eng):
                    yield 0, 0, c, cc, c
            else:
                with eng.Fori(0, n_exp // 2) as i:
                    for par in range(2):
                        e = i * 2 + par
                        for c in range(per_chunks):
                            if mode == "blocks":
                                yield e, par, e, par, e
                            else:
                                yield e, par, c, c % 2, i * (2 * NC) + par * NC + c

        @block.sync
        def _(sp):
            def load(e, par):
                ex = bass.ds(e, 1)
                sp.dma_start(w1[:, par], w1_d[ex].rearrange("a (k p) n -> p (a k) n", p=P)).then_inc(w_in[par], 16)
                sp.dma_start(w2[:, par], w2_d[ex].rearrange("a (k p) n -> p (a k) n", p=P)).then_inc(w_in[par], 16)
                if mode == "gated":
                    sp.dma_start(gate[:, par, :], gates_d[ex].broadcast_to([P, T])).then_inc(gate_in[par], 16)
            for par in range(min(n_exp, 2)):
                load(par, par)
            if n_exp > 1:
                with sp.Fori(1, n_exp // 2) as i:
                    for par in range(2):
                        sp.wait_ge(y_evac, i * (4 * per_chunks) + 4 - 4 * per_chunks + 2 * per_chunks * (par + 1))
                        load(i * 2 + par, par)

        @block.tensor
        def _(pe):
            def hidden_of(e, par, c, slot, j, first):
                if first:
                    if n_exp == 1:
                        pe.wait_ge(w_in[par], 32)
                    else:
                        pe.wait_ge(w_in[par], (e // 2 + 1) * 32 if isinstance(e, int) else e * 16 + 32 - 16 * par)
                for f in range(NF):
                    pe.wait_ge(h_evac, j * NF + f + 1)
                    for k in range(KD):
                        mm = pe.matmul(bank(f % 4), w1[:, par, k, f * P:(f + 1) * P], view(src, k, c),
                                       start=k == 0, stop=k == KD - 1)
                    mm.then_inc(h_full, 1)

            def out_of(e, par, c, slot, j, first):
                if mode == "fixed":
                    pe.wait_ge(hidden, 2 * j + 2)
                else:
                    pe.wait_ge(h_evac, j * NF + NF + 4)
                for o in range(KD):
                    pe.wait_ge(y_evac, j * 2 + o + 1)
                    for f in range(NF):
                        mm = pe.matmul(bank(4 + 2 * slot + o), w2[:, par, f, o * P:(o + 1) * P],
                                       h[:, slot, f, 0:width] if mode != "blocks" else
                                       h[:, slot, f, 0:width].rearrange("p (b q) -> p b q", b=B),
                                       start=f == 0, stop=f == NF - 1)
                    mm.then_inc(y_full, 1)

            last = None
            turn = 2 if n_exp == 1 else 2 * per_chunks
            for i, un in enumerate(units(pe)):
                hidden_of(*un, first=un[2] == 0 if n_exp > 1 and mode != "blocks" else True)
                if last is not None:
                    out_of(*last, first=False)
                last = un
                if i % turn == turn - 1:
                    out_of(*un, first=False)
                    last = None

        @block.scalar
        def _(act):
            act.sem_inc(h_evac, 4)
            if mode == "fixed":
                act.wait_ge(b1s_done, 1)
            for e, par, c, slot, j in units(act):
                for f in range(NF):
                    wait_apart(m, act, h_full, j * NF + f + 1)
                    if mode == "fixed":
                        if f % 4 == 0:
                            act.wait_ge(summed, 2 * j + f // 4 + 1)
                        act.activation(n_[:, (f % 4) * CH:(f % 4 + 1) * CH], bank(f % 4), ACT.Identity,
                                       bias=b1s[:, f:f + 1], scale=FIX).then_inc(h_evac, 1)
                        if f % 4 == 3:
                            half = 2 * j + f // 4
                            act.wait_ge(floor, half + 1)
                            act.activation(g0[:, :], fl[:, :], ACT.Gelu, scale=0.25).then_inc(g0_done, 1)
                            act.activation(g1[:, :], fl[:, :], ACT.Gelu, scale=0.25, bias=m.quarter[:, 0:1]).then_inc(g1_done, 1)
                        continue
                    if f == 0:
                        wait_apart(m, act, y_full, j * 2 + 2)
                    if b1 is None:
                        bias = 0.0
                    elif n_exp == 1:
                        bias = m.col(b1, f)
                    else:
                        bias = m.vec[:, bass.ds(e * NF + (VEC_AT[b1] + f), 1)]
                    hv = h[:, slot, f, 0:width]
                    if mode == "blocks":
                        hv = hv.rearrange("p (b q) -> p b q", b=B)
                    act.activation(hv, bank(f % 4), func, bias=bias).then_inc(h_evac, 1)

        @block.gpsimd
        def _(pool):
            pool.sem_inc(y_full, 4)
            pool.sem_inc(summed, 1)
            if mode == "fixed":
                for c, cc in chunks(pool):
                    for hf in range(2):
                        half = 2 * c + hf
                        pool.wait_ge(g1_done, half + 1)
                        pool.wait_ge(g0_done, half + 1)
                        pool.tensor_tensor(g1[:, :], g1[:, :], g0[:, :], ALU.subtract).then_inc(diff, 1)

        @block.vector
        def _(dve):
            dve.sem_inc(y_evac, 4)
            if mode == "fixed":
                dve.tensor_scalar(b1s[:, :], m.vec[:, VEC_AT[b1]:VEC_AT[b1] + NF], FIX, None, ALU.mult).then_inc(b1s_done, 1)
            for e, par, c, slot, j in units(dve):
                if mode == "fixed":
                    for hf in range(2):
                        half = 2 * j + hf
                        dve.wait_ge(h_evac, j * NF + 4 * hf + 4 + 4)
                        dve.tensor_scalar(n_[:, :], n_[:, :], MAGIC, -MAGIC, ALU.add, ALU.add).then_inc(whole, 1)
                        dve.wait_ge(whole, half + 1)
                        dve.tensor_scalar(fl[:, :], n_[:, :], 4 / FIX, -(0.5 - 2 / FIX), ALU.mult, ALU.add).then_inc(quart, 1)
                        dve.wait_ge(quart, half + 1)
                        dve.tensor_scalar(fl[:, :], fl[:, :], MAGIC, -MAGIC, ALU.add, ALU.add).then_inc(floor, 1)
                        dve.wait_ge(floor, half + 1)
                        dve.scalar_tensor_tensor(out=n_[:, :], in0=n_[:, :], scalar=4 / FIX, in1=fl[:, :],
                                                 op0=ALU.mult, op1=ALU.subtract).then_inc(frac, 1)
                        dve.wait_ge(frac, half + 1)
                        dve.wait_ge(diff, half + 1)
                        dve.tensor_tensor(n_[:, :], n_[:, :], g1[:, :], ALU.mult).then_inc(prod, 1)
                        dve.wait_ge(prod, half + 1)
                        dve.tensor_tensor(g0[:, :], n_[:, :], g0[:, :], ALU.add).then_inc(summed, 1)
                        dve.wait_ge(summed, half + 2)
                        dve.tensor_scalar(g0[:, :], g0[:, :], FIX, MAGIC, ALU.mult, ALU.add).then_inc(scaled, 1)
                        dve.wait_ge(scaled, half + 1)
                        if hf == 0:
                            dve.wait_ge(y_full, 2 * j + 2)
                        dve.tensor_scalar(h[:, slot, 4 * hf:4 * hf + 4, :].rearrange("p f n -> p (f n)"), g0[:, :],
                                          -MAGIC, 1 / FIX, ALU.add, ALU.mult).then_inc(hidden, 1)
                if mode == "gated":
                    dve.wait_ge(gate_in[par], e * 8 + 16 - 8 * par)
                for o in range(KD):
                    dve.wait_ge(y_full, j * 2 + o + 1 + 4)
                    y = bank(4 + 2 * slot + o)
                    to = view(dst, o, c)
                    if mode == "gated":
                        bias = m.vec[:, bass.ds(e * KD + (VEC_AT[b2] + o), 1)] if b2 else 0.0
                        dve.scalar_tensor_tensor(out=yt[:, o, :], in0=y, scalar=bias, in1=gate[:, par, tok(c)],
                                                 op0=ALU.add, op1=ALU.mult).then_inc(y_tmp, 1)
                        dve.wait_ge(y_tmp, j * 2 + o + 1)
                        dve.tensor_tensor(to, to, yt[:, o, :], ALU.add).then_inc(y_evac, 1)
                    elif mode == "fixed":
                        dve.tensor_scalar(yt[:, o, :], y, m.col(b2, o), FIX, ALU.add, ALU.mult).then_inc(y_tmp, 1)
                        dve.wait_ge(y_tmp, j * 2 + o + 1)
                        dve.tensor_scalar(yt[:, o, :], yt[:, o, :], MAGIC, -MAGIC, ALU.add, ALU.add).then_inc(y_tmp2, 1)
                        dve.wait_ge(y_tmp2, j * 2 + o + 1)
                        dve.scalar_tensor_tensor(out=to, in0=yt[:, o, :], scalar=1 / FIX, in1=to,
                                                 op0=ALU.mult, op1=ALU.add).then_inc(y_evac, 1)
                    else:
                        bias = m.vec[:, bass.ds(e * KD + (VEC_AT[b2] + o), 1)] if n_exp > 1 else m.col(b2, o)
                        dve.scalar_tensor_tensor(out=to, in0=y, scalar=bias, in1=to, op0=ALU.add, op1=ALU.add).then_inc(y_evac, 1)


def router(nc, m, name, src, w_d, b_d, top, gates_d, tri_d):
    names = ["in", "full", "logit", "max", "shifted", "exp", "above", "equal", "ahead", "beat", "rank", "kept",
             "gate", "sum", "rec", "out", "t_full", "t_evac", "stored"]
    NTT = T // P
    with ExitStack() as ctx:
        sems = ctx.enter_context(phase(nc, [f"{name}_{s}" for s in names]))
        (loaded, full, logit, s_max, shifted, exp_done, above, equal, ahead, beat, rank_done, kept, gate_done, sum_done,
         rec_done, out, t_full, t_evac, stored) = sems

        def sb(nm, shape):
            return ctx.enter_context(nc.sbuf_tensor(f"{name}_{nm}", shape, F32))

        w = sb("w", [P, KD, E])
        bias = sb("bias", [P, E])
        tri = sb("tri", [P, E, E])
        sh = sb("sh", [P, NTT, E])
        lg, ex, col, rank, g = sb("lg", [P, NTT, E]), sb("ex", [P, NTT, E]), sb("col", [P, NTT]), sb("rank", [P, NTT, E]), sb("g", [P, NTT, E])
        gt, eq = sb("gt", [P, NTT, E, E]), sb("eq", [P, NTT, E, E])
        gT = sb("gT", [E, T])
        n_in = 3 if b_d is not None else 2
        block = ctx.enter_context(nc.Block())

        @block.sync
        def _(sp):
            sp.dma_start(w[:, :, :], w_d.rearrange("(k p) e -> p k e", p=P)).then_inc(loaded, 16)
            sp.dma_start(tri[:, :, :], tri_d).then_inc(loaded, 16)
            if b_d is not None:
                sp.dma_start(bias[:, :], b_d.broadcast_to([P, E])).then_inc(loaded, 16)
            sp.wait_ge(t_evac, 4)
            sp.dma_start(gates_d, gT[:, :]).then_inc(stored, 16)
            sp.wait_ge(stored, 16)

        @block.tensor
        def _(pe):
            pe.wait_ge(loaded, 16 * n_in)
            for i in range(NTT):
                for k in range(KD):
                    mm = pe.matmul(m.ps[:, 0, i * E:(i + 1) * E], src[:, k, i * P:(i + 1) * P], w[:, k, :],
                                   start=k == 0, stop=k == KD - 1)
            mm.then_inc(full, 1)
            pe.wait_ge(out, 1)
            for c in range(NC):
                for i in range(4 * c, 4 * c + 4):
                    mm = pe.transpose(m.ps[0:E, 4 + c, (i % 4) * P:(i % 4 + 1) * P], g[:, i, :], m.ident[:, :])
                mm.then_inc(t_full, 1)

        @block.scalar
        def _(act):
            act.wait_ge(shifted, 1)
            act.activation(ex[:, :, :], sh[:, :, :], ACT.Exp).then_inc(exp_done, 1)
            for c in range(NC):
                act.wait_ge(t_full, c + 1)
                act.activation(gT[:, c * CH:(c + 1) * CH], m.ps[0:E, 4 + c, :], ACT.Copy).then_inc(t_evac, 1)

        @block.vector
        def _(dve):
            dve.wait_ge(loaded, 16 * n_in)
            dve.wait_ge(full, 1)
            p3 = m.ps[:, 0, 0:NTT * E].rearrange("p (i e) -> p i e", e=E)
            if b_d is not None:
                dve.tensor_tensor(lg[:, :, :], p3, bias[:, :].unsqueeze(1).broadcast_to([P, NTT, E]), ALU.add).then_inc(logit, 1)
            else:
                dve.tensor_copy(lg[:, :, :], p3).then_inc(logit, 1)
            dve.wait_ge(logit, 1)
            dve.tensor_reduce(col[:, :], lg[:, :, :], AX, ALU.max).then_inc(s_max, 1)
            dve.wait_ge(s_max, 1)
            dve.tensor_tensor(sh[:, :, :], lg[:, :, :], col[:, :].unsqueeze(2).broadcast_to([P, NTT, E]), ALU.subtract).then_inc(shifted, 1)
            dve.wait_ge(shifted, 1)
            for i in range(NTT):
                lj = lg[:, i:i + 1, :].broadcast_to([P, E, E])
                le = lg[:, i, :].unsqueeze(2).broadcast_to([P, E, E])
                ins = dve.tensor_tensor(gt[:, i], lj, le, ALU.is_gt)
                ins2 = dve.tensor_tensor(eq[:, i], lj, le, ALU.is_equal)
            ins.then_inc(above, 1)
            ins2.then_inc(equal, 1)
            dve.wait_ge(above, 1)
            dve.wait_ge(equal, 1)
            dve.tensor_tensor(eq[:, :, :, :], eq[:, :, :, :], tri[:, :, :].unsqueeze(1).broadcast_to([P, NTT, E, E]), ALU.mult).then_inc(ahead, 1)
            dve.wait_ge(ahead, 1)
            dve.tensor_tensor(gt[:, :, :, :], gt[:, :, :, :], eq[:, :, :, :], ALU.add).then_inc(beat, 1)
            dve.wait_ge(beat, 1)
            dve.tensor_reduce(rank[:, :, :], gt[:, :, :, :], AX, ALU.add).then_inc(rank_done, 1)
            dve.wait_ge(rank_done, 1)
            dve.tensor_scalar(rank[:, :, :], rank[:, :, :], float(top), None, ALU.is_lt).then_inc(kept, 1)
            dve.wait_ge(kept, 1)
            dve.wait_ge(exp_done, 1)
            dve.tensor_tensor(g[:, :, :], ex[:, :, :], rank[:, :, :], ALU.mult).then_inc(gate_done, 1)
            dve.wait_ge(gate_done, 1)
            dve.tensor_reduce(col[:, :], g[:, :, :], AX, ALU.add).then_inc(sum_done, 1)
            dve.wait_ge(sum_done, 1)
            dve.reciprocal(col[:, :], col[:, :]).then_inc(rec_done, 1)
            dve.wait_ge(rec_done, 1)
            dve.tensor_tensor(g[:, :, :], g[:, :, :], col[:, :].unsqueeze(2).broadcast_to([P, NTT, E]), ALU.mult).then_inc(out, 1)


def self_attention(nc, m, src, dst, io):
    names = ["const", "vg_set", "v_full", "v_evac", "w_in", "job_full", "job_evac", "high", "keys", "v_group", "max_full", "max_part",
             "max_both", "max_ready", "s_full", "exp", "pv", "o_evac", "o_out0", "o_out1", "o_in", "sum_in", "recip", "recip_out",
             "spread"]
    with ExitStack() as ctx:
        sems = ctx.enter_context(phase(nc, [f"self_{s}" for s in names]))
        (const, vg_set, v_full, v_evac, w_in, job_full, job_evac, high, keys, v_group, max_full, max_part, max_both, max_ready,
         s_full, exp_done, pv, o_evac, o_out0, o_out1, o_in, sum_in, recip, recip_out, spread) = sems
        o_out = [o_out0, o_out1]

        def sb(nm, shape, dt=F32):
            return ctx.enter_context(nc.sbuf_tensor(f"self_{nm}", shape, dt))

        w = sb("w", [P, 2, KD, P])
        wv = sb("wv", [P, KD, D])
        rows = sb("rows", [P, 7])
        hi = sb("hi", [P, 2, CH])
        q = sb("q", [P, 2, S], F32R)
        qm = sb("qm", [P, S], F32R)
        kk = sb("kk", [P, S], F32R)
        km = sb("km", [P, 2, HG, S], F32R)
        v = sb("v", [P, B * NKC, SH, SD])
        vg = sb("vg", [P, 2, NKC, HG, 32])
        mp = sb("mp", [P, NT, HG, 2])
        mf = sb("mf", [P, NT, HG])
        mt = sb("mt", [P, NT, P])
        pr = sb("pr", [P, 2, HG, CH])
        o = sb("o", [P, 2, CH])
        sums = sb("sums", [P, SH * T // P])
        o_d = nc.dram_tensor("self_out", (D, T), F32).ap()
        sum_d = nc.dram_tensor("self_sum", (SH, T), F32).ap()
        rec_d = nc.dram_tensor("self_rec", (SH, T), F32).ap()
        block = ctx.enter_context(nc.Block())
        FIRST_BANKS = [7, 2, 3, 4]
        STEPS = 2 * NKC
        UNITS = HG * NT * 2
        PER = UNITS // STEPS
        JOB_AT = {3: 0, 5: 1, 7: 2, 9: 3}

        def idx(g, b, n):
            return g * (2 * n) + b * n

        def jobs_before(g, b):
            last = isinstance(g, int) and g == NG - 1 and b == 1
            return 8 + 12 * g + 2 if last else idx(g, b, 6) + 8

        def groups(eng, body):
            with eng.Fori(0, NG - 1) as g:
                body(g, 0, (g, 1), True)
                body(g, 1, (g + 1, 0), True)
            body(NG - 1, 0, (NG - 1, 1), False)
            body(NG - 1, 1, None, False)

        @block.sync
        def _(sp):
            def load(g):
                for z, nm in enumerate(("s_wq", "s_wk")):
                    sp.dma_start(w[:, z], io[nm][g].rearrange("a (k p) n -> p (a k) n", p=P)).then_inc(w_in, 16)
            sp.dma_start(wv[:, :, :], io["s_wv"].rearrange("(k p) n -> p k n", p=P)).then_inc(const, 16)
            sp.dma_start(rows[:, :], io["s_rows"]).then_inc(const, 16)
            load(slice(0, 1))

            def body(g, b, nxt, project):
                if b == 0 and project:
                    sp.wait_ge(job_full, g * 12 + 8)
                    load(bass.ds(g + 1, 1))
                for half in range(2):
                    sp.wait_ge(o_evac, idx(g, b, 2) + half + 2)
                    at = slice(b * S + half * CH, b * S + half * CH + CH)
                    for j in range(HG):
                        sp.dma_start(o_d[bass.ds(g * 32 + 8 * j, SD), at], o[32 * j:32 * j + SD, half, :]).then_inc(o_out[half], 16)
                    sp.dma_start(sum_d[bass.ds(g * HG, HG), at], o[SD:P:32, half, :]).then_inc(o_out[half], 16)
            groups(sp, body)
            for half in range(2):
                sp.wait_ge(o_out[half], 80 + 80 * 2 * NG)
            sp.dma_start(sums[:, :], sum_d.rearrange("h (a n) -> (h a) n", n=SH * T // P)).then_inc(sum_in, 16)
            sp.dma_start(dst[:, :, :], o_d.rearrange("(k p) n -> p k n", p=P)).then_inc(o_in, 16)
            sp.wait_ge(recip, 1)
            sp.dma_start(rec_d.rearrange("h (a n) -> (h a) n", n=SH * T // P), sums[:, :]).then_inc(recip_out, 16)
            sp.wait_ge(recip_out, 16)
            for h in range(SH):
                k, p = h * SD // P, h * SD % P
                sp.dma_start(src[p:p + SD, k, :], rec_d[h:h + 1, :].broadcast_to([SD, T])).then_inc(spread, 16)

        @block.tensor
        def _(pe):
            pe.wait_ge(const, 32)
            for i in range(B * NKC):
                if i >= 2:
                    pe.wait_ge(v_evac, i - 1)
                for k in range(KD):
                    mm = pe.matmul(m.ps[:, i % 2, 0:D], src[:, k, i * P:(i + 1) * P], wv[:, k, :], start=k == 0, stop=k == KD - 1)
                mm.then_inc(v_full, 1)
            pe.wait_ge(v_evac, B * NKC)

            def project(bank, r, b):
                z, half = r // 2, r % 2
                for k in range(KD):
                    mm = pe.matmul(m.ps[:, bank, :], w[:, z, k, :], src[:, k, b * S + half * CH:b * S + half * CH + CH],
                                   start=k == 0, stop=k == KD - 1)
                mm.then_inc(job_full, 1)

            def max_unit(g, b, un):
                j, i, half = un // (2 * NT), un // 2 % NT, un % 2
                if i == 0 and half == 0:
                    pe.wait_ge(keys, idx(g, b, HG) + j + 1)
                pe.wait_ge(max_part, idx(g, b, UNITS) + un + 1)
                pe.matmul(m.ps[:, un % 2, :], q[:, b, i * P:(i + 1) * P], km[:, b, j, half * CH:(half + 1) * CH],
                          start=True, stop=True).then_inc(max_full, 1)

            pe.wait_ge(w_in, 32)
            for job in range(8):
                if job >= 4:
                    pe.wait_ge(job_evac, job - 3)
                project(FIRST_BANKS[job % 4], job % 4, job // 4)
            for un in range(UNITS):
                max_unit(0, 0, un)
            pe.wait_ge(job_evac, 8)

            def body(g, b, nxt, projects):
                before = jobs_before(g, b)

                def turn_maxima(half):
                    pe.wait_ge(job_evac, before + half)
                    for i in range(4):
                        mm = pe.transpose(m.ps[:, 7, i * P:(i + 1) * P], mt[:, half * 4 + i, :], m.ident[:, :])
                    mm.then_inc(job_full, 1)

                def values(s):
                    half, kc = s // NKC, s % NKC
                    pe.wait_ge(exp_done, idx(g, b, 2 * STEPS) + 2 * s + 2 + 2)
                    if s == 0:
                        pe.wait_ge(v_group, idx(g, b, 1) + 1)
                    if kc == 0:
                        pe.wait_ge(o_evac, idx(g, b, 2) + half + 1)
                    for j in range(HG):
                        mm = pe.matmul(m.ps[32 * j:32 * j + 32, 6, :], vg[:, b, kc, j, :], pr[:, s % 2, j, :],
                                       start=kc == 0, stop=kc == NKC - 1)
                    mm.then_inc(pv, 1)

                def next_max(s, i):
                    if nxt is not None:
                        max_unit(*nxt, s * PER + i)

                pe.wait_ge(max_ready, idx(g, b, 1) + 1)
                turn_maxima(0)
                for s in range(STEPS):
                    half, kc = s // NKC, s % NKC
                    next_max(s, 0)
                    for pair in range(2):
                        if kc == 0 and pair == 0:
                            pe.wait_ge(job_evac, before + half + 1)
                        pe.wait_ge(exp_done, idx(g, b, 2 * STEPS) + 2 * s + pair + 1)
                        for jj in range(2):
                            mm = pe.matmul(m.ps[:, 2 + 2 * pair + jj, :], km[:, b, 2 * pair + jj, kc * P:(kc + 1) * P],
                                           qm[:, half * CH:(half + 1) * CH], start=True, stop=True)
                        mm.then_inc(s_full, 1)
                        next_max(s, 1 + pair)
                    if s >= 1:
                        values(s - 1)
                    next_max(s, 3)
                    if s == 1:
                        turn_maxima(1)
                    if projects and s in JOB_AT:
                        if s == 3:
                            pe.wait_ge(w_in, g * 32 + 64)
                        pe.wait_ge(job_evac, before + 2 + JOB_AT[s])
                        project(7, JOB_AT[s], b)
                values(STEPS - 1)
            groups(pe, body)

        @block.scalar
        def _(act):
            act.sem_inc(exp_done, 2)
            act.sem_inc(o_evac, 1)
            for i in range(B * NKC):
                act.wait_ge(v_full, i + 1)
                act.activation(v[:, i], m.ps[:, i % 2, 0:D].rearrange("p (h d) -> p h d", d=SD), ACT.Copy).then_inc(v_evac, 1)

            def high_part(r, bank, job):
                act.wait_ge(job_full, job + 1)
                if not isinstance(job, int) or job >= 2:
                    act.wait_ge(job_evac, job - 1)
                act.activation(hi[:, r % 2, :], m.ps[:, bank, :], ACT.Copy, scale=rows[:, r // 2:r // 2 + 1]).then_inc(high, 1)

            for job in range(8):
                high_part(job % 4, FIRST_BANKS[job % 4], job)

            def body(g, b, nxt, projects):
                before = jobs_before(g, b)
                for s in range(STEPS):
                    act.wait_ge(pv, idx(g, b, STEPS) + s + 1)
                    for pair in range(2):
                        act.wait_ge(s_full, idx(g, b, 2 * STEPS) + 2 * s + pair + 2)
                        act.activation(pr[:, s % 2, 2 * pair:2 * pair + 2, :], m.ps[:, 2 + 2 * pair:4 + 2 * pair, :], ACT.Exp,
                                       scale=1.0 / float(np.float32(np.sqrt(SD)))).then_inc(exp_done, 1)
                        if pair == 0 and projects and s - 1 in JOB_AT:
                            high_part(JOB_AT[s - 1], 7, before + 2 + JOB_AT[s - 1])
                    if s in (NKC, STEPS - 1):
                        half = s // NKC - (s == NKC)
                        act.wait_ge(pv, idx(g, b, STEPS) + NKC * (half + 1) + 2)
                        act.wait_ge(o_out[half], idx(g, b, 80) + 80)
                        act.activation(o[:, half, :], m.ps[:, 6, :], ACT.Copy).then_inc(o_evac, 1)
            groups(act, body)

        @block.gpsimd
        def _(pool):
            pool.sem_inc(pv, 2)
            pool.sem_inc(s_full, 1)
            for half in range(2):
                pool.sem_inc(o_out[half], 80)
            pool.memset(vg[:, :, :, :, :], 0.0).then_inc(vg_set, 1)
            pool.wait_ge(vg_set, 1)
            pool.memset(vg[:, :, :, :, SD:SD + 1], 1.0).then_inc(vg_set, 1)
            pool.wait_ge(vg_set, 2)
            pool.wait_ge(const, 32)

            def spread_keys(b):
                for j in range(HG):
                    pool.tensor_scalar(km[:, b, j, :], kk[:, :].bitcast(F32), rows[:, 3 + j:4 + j], 1.0, ALU.mult, ALU.mult).then_inc(keys, 1)

            def pick_values(g, b):
                pool.tensor_copy(vg[:, b, :, :, 0:SD], v[:, b * NKC:(b + 1) * NKC, bass.ds(g * HG, HG), :]).then_inc(v_group, 1)

            pool.wait_ge(job_evac, 4)
            spread_keys(0)
            pool.wait_ge(v_evac, B * NKC)
            pick_values(0, 0)

            def body(g, b, nxt, projects):
                if nxt is not None:
                    if not isinstance(g, int):
                        wait_apart(m, pool, job_evac, jobs_before(g, b))
                        wait_apart(m, pool, s_full, idx(g, b, 2 * STEPS) + 1)
                    else:
                        pool.wait_ge(job_evac, jobs_before(g, b))
                        pool.wait_ge(s_full, idx(g, b, 2 * STEPS) + 1)
                    spread_keys(nxt[1])
                    pool.wait_ge(pv, idx(g, b, STEPS) + 2)
                    pick_values(*nxt)
            groups(pool, body)

            pool.wait_ge(o_in, 16)
            pool.wait_ge(spread, 16 * SH)
            pool.tensor_tensor(dst[:, :, 0:T // 4], dst[:, :, 0:T // 4], src[:, :, 0:T // 4], ALU.mult)

        @block.vector
        def _(dve):
            dve.sem_inc(max_part, 2)
            dve.memset(mt[:, :, :], 0.0).then_inc(max_both, 1)
            dve.wait_ge(max_both, 1)
            dve.wait_ge(const, 32)

            def split(r, b, bank, job, high_at):
                z, half = r // 2, r % 2
                dve.wait_ge(job_full, job + 1)
                dve.wait_ge(high, high_at)
                at = slice(half * CH, (half + 1) * CH)
                if z == 0:
                    dve.tensor_tensor(q[:, b, at], m.ps[:, bank, :], hi[:, r % 2, :], ALU.subtract).then_inc(job_evac, 1)
                else:
                    dve.scalar_tensor_tensor(out=kk[:, at], in0=m.ps[:, bank, :], scalar=rows[:, 2:3], in1=hi[:, r % 2, :],
                                             op0=ALU.add, op1=ALU.subtract).then_inc(job_evac, 1)

            def max_unit(g, b, un):
                j, i, half = un // (2 * NT), un // 2 % NT, un % 2
                dve.wait_ge(max_full, idx(g, b, UNITS) + un + 1)
                dve.tensor_reduce(mp[:, i, j, half:half + 1], m.ps[:, un % 2, :], AX, ALU.max).then_inc(max_part, 1)
                if un == UNITS - 1:
                    dve.wait_ge(max_part, idx(g, b, UNITS) + UNITS + 2)
                    dve.tensor_tensor(mf[:, :, :], mp[:, :, :, 0:1].rearrange("p i j a -> p i (j a)"),
                                      mp[:, :, :, 1:2].rearrange("p i j a -> p i (j a)"), ALU.max).then_inc(max_both, 1)
                    dve.wait_ge(max_both, idx(g, b, 1) + 2)
                    dve.tensor_scalar(mt[:, :, 24:P:32], mf[:, :, :], -1.0, None, ALU.mult).then_inc(max_ready, 1)

            for job in range(8):
                if job == 6:
                    dve.wait_ge(keys, HG)
                split(job % 4, job // 4, FIRST_BANKS[job % 4], job, job + 1)
            for un in range(UNITS):
                max_unit(0, 0, un)

            def body(g, b, nxt, projects):
                before = jobs_before(g, b)

                def with_maxima(half):
                    at = slice(half * CH, (half + 1) * CH)
                    dve.wait_ge(job_full, before + half + 1)
                    dve.tensor_tensor(qm[:, at], m.ps[:, 7, :], q[:, b, at].bitcast(F32), ALU.add).then_inc(job_evac, 1)

                with_maxima(0)
                for s in range(STEPS):
                    if projects and s - 2 in JOB_AT:
                        r = JOB_AT[s - 2]
                        if r == 2:
                            dve.wait_ge(keys, idx(*nxt, HG) + HG)
                        split(r, b, 7, before + 2 + r, idx(g, b, 4) + 8 + r + 1)
                    if nxt is not None:
                        for i in range(PER):
                            max_unit(*nxt, s * PER + i)
                    if s == 1:
                        with_maxima(1)
            groups(dve, body)

            dve.wait_ge(sum_in, 16)
            dve.reciprocal(sums[:, :], sums[:, :]).then_inc(recip, 1)
            dve.wait_ge(o_in, 16)
            dve.wait_ge(spread, 16 * SH)
            dve.tensor_tensor(dst[:, :, T // 4:T], dst[:, :, T // 4:T], src[:, :, T // 4:T], ALU.mult)


def build(nc, io, out):
    class M:
        pass
    m = M()
    with ExitStack() as ctx:
        def sb(name, shape, dt=F32):
            return ctx.enter_context(nc.sbuf_tensor(name, shape, dt))
        m.ps = ctx.enter_context(nc.psum_tensor("ps", [P, 8, 512], F32))
        x, n = (sb(nm, [P, KD, T]) for nm in "xn")
        m.vec = sb("vec_sb", [P, NVEC])
        m.mean_w, m.ident = sb("mean_w", [P, P]), sb("ident_sb", [P, P])
        m.eps, m.quarter = sb("eps", [P, 1]), sb("quarter", [P, 1])
        m.wp = sb("wp", [P, 4, KD, D])

        def col(name, i):
            at = VEC_AT[name] + i
            return m.vec[:, at:at + 1]
        m.col = col
        m.passed = ctx.enter_context(nc.semaphore("passed"))
        gates_d = [nc.dram_tensor(f"gates{i}", (E, T), F32).ap() for i in range(2)]

        with phase(nc, ["x_in", "const_set"]) as (x_in, const_set), nc.Block() as block:
            @block.sync
            def _(sp):
                sp.dma_start(x[:, :, :], io["xT"].rearrange("(k p) n -> p k n", p=P)).then_inc(x_in, 16)
                sp.dma_start(m.vec[:, :], io["vec"]).then_inc(x_in, 16)
                sp.dma_start(m.ident[:, :], io["ident"]).then_inc(x_in, 16)
                sp.wait_ge(x_in, 48)

            @block.vector
            def _(dve):
                dve.memset(m.mean_w[:, :], 1.0 / D)
                dve.memset(m.eps[:, :], EPS)
                dve.memset(m.quarter[:, :], 0.25).then_inc(const_set, 1)
                dve.wait_ge(const_set, 1)

        def norm(name, src, dst, g=None, b=None):
            with ExitStack() as sc:
                m.sq = sc.enter_context(nc.sbuf_tensor(f"{name}_sq", [P, 2, KD, CH], F32))
                m.std = sc.enter_context(nc.sbuf_tensor(f"{name}_std", [P, T], F32))
                m.rs = sc.enter_context(nc.sbuf_tensor(f"{name}_rs", [P, 2, CH], F32))
                layer_norm(nc, m, name, src, dst, g, b)

        @contextmanager
        def scratch(i):
            with nc.sbuf_tensor(f"u{i}", [P, KD, T], F32) as u, nc.sbuf_tensor(f"t{i}", [P, KD, T], F32) as t:
                yield u, t

        def store(src):
            with phase(nc, ["stored"]) as (stored,), nc.Block() as block:
                @block.sync
                def _(sp):
                    sp.dma_start(out.rearrange("(k p) n -> p k n", p=P), src[:, :, :]).then_inc(stored, 16)
                    sp.wait_ge(stored, 16)

        with scratch(0) as (u, t):
            norm("n0", x, n)
            load_weights(nc, m, [(0, io["a_wsv"]), (1, io["a_wso"])])
            linear(nc, m, "sv", n, 0, t, bias="a_bsv")
            linear(nc, m, "so", t, 1, u, bias="a_bso", plus=n)
            norm("n1", u, u, "ln1_g", "ln1_b")
            load_weights(nc, m, [(s, io[f"a_w{k}"]) for s, k in enumerate("qokv")])
            cross_attention(nc, m, "xa", u, t, 8, None, 1.0 / float(np.sqrt(np.float32(32))), "a_bq", "a_bk", io["a_bv"], io)
            linear(nc, m, "ao", t, 1, n, bias="a_bo", plus=u)
        norm("n2", n, n, "ln2_g", "ln2_b")
        experts(nc, m, "fa", n, n, 1, ACT.Relu, io["fa_w1"], io["fa_w2"], "fa_b1", "fa_b2", "dense")
        norm("n3", n, n, "ln3_g", "ln3_b")
        add(nc, m, "r0", x, n)

        norm("n4", x, n)
        with scratch(1) as (u, t):
            norm("n5", n, u, "lni_g", "lni_b")
            self_attention(nc, m, u, t, io)
            load_weights(nc, m, [(0, io["s_wo"])])
            linear(nc, m, "wo", t, 0, n, plus=n)
        experts(nc, m, "f0", n, x, E, ACT.Gelu, io["f0_w1"], io["f0_w2"], "f0_b1", "f0_b2", "blocks")

        norm("n6", x, n)
        with scratch(2) as (u, t):
            load_weights(nc, m, [(s, io[f"b_w{k}"]) for s, k in enumerate("qokv")])
            cross_attention(nc, m, "xb", n, t, 16, "replace", 0.25, "b_bq", "b_bk", io["b_bv"], io)
            linear(nc, m, "bo", t, 1, x, bias="b_bo", plus=x)
        norm("n7", x, n)
        router(nc, m, "r1", n, io["r1_w"], None, 4, gates_d[0], io["tri"])
        experts(nc, m, "f1", n, x, E, ACT.Gelu_apprx_tanh, io["f1_w1"], io["f1_w2"], None, None, "gated", gates_d[0])

        norm("n8", x, n)
        with scratch(3) as (u, t):
            load_weights(nc, m, [(s, io[f"c_w{k}"]) for s, k in enumerate("qokv")])
            cross_attention(nc, m, "xc", n, t, 16, "bias", 1.0, None, None, None, io)
            linear(nc, m, "co", t, 1, x, plus=x)
        norm("n9", x, n)
        with scratch(4) as (u, t):
            load_weights(nc, m, [(0, io["r2_w1"])])
            linear(nc, m, "rh", n, 0, u, bias="r2_b1", func=ACT.Silu)
            router(nc, m, "r2", u, io["r2_w2"], io["r2_b2"], 2, gates_d[1], io["tri"])
        add(nc, m, "r2x", x, n)
        experts(nc, m, "f2", n, x, E, ACT.Silu, io["f2_w1"], io["f2_w2"], "f2_b1", "f2_b2", "gated", gates_d[1])

        norm("n10", x, n)
        with scratch(5) as (u, t):
            load_weights(nc, m, [(s, io[f"d_w{k}"]) for s, k in enumerate("qokv")])
            cross_attention(nc, m, "xd", n, t, 16, "keep", 0.25, "d_bq", "d_bk", io["d_bv"], io)
            linear(nc, m, "do", t, 1, x, bias="d_bo", plus=x)
        norm("n11", x, n)
        feed_forward(nc, m, "f3", n, x, 1, None, io["f3_w1"], io["f3_w2"], "f3_b1", "f3_b2", "fixed")
        store(x)


def bucket(offset):
    half, exact = BUCKETS // 2, BUCKETS // 4
    r = np.abs(offset)
    far = np.log(np.maximum(r, 1).astype(np.float32) / np.float32(exact)) / np.float32(np.log(128 / exact)) * np.float32(half - exact)
    return half * (offset > 0) + np.where(r < exact, r, np.minimum(exact + far.astype(np.int32), half - 1))


def lay_out(a):
    f = lambda v: np.asarray(v)
    c = np.ascontiguousarray
    io = {"xT": c(f(a["x"]).reshape(T, D).T), "ctxT": c(f(a["ctx_1024"]).reshape(B * S2, D).T)}
    io["ctxT_reversed"] = c(f(a["ctx_1024"])[:, ::-1].reshape(B * S2, D).T)
    vec = {}
    io["a_wsv"], io["a_wso"] = c(f(a["L0_xattn_qkv_w"])[2 * D:].T), c(f(a["L0_xattn_sa_out_w"]).T)
    for z, k in enumerate("qkv"):
        io[f"a_w{k}"] = c(f(a["L0_xattn_in_proj_w"])[z * D:(z + 1) * D].T)
    io["a_wo"] = c(f(a["L0_xattn_mha_out_w"]).T)
    bi = f(a["L0_xattn_in_proj_b"])
    vec["a_bsv"], vec["a_bso"] = f(a["L0_xattn_qkv_b"])[2 * D:], a["L0_xattn_sa_out_b"]
    vec["a_bq"], vec["a_bk"], vec["a_bo"] = bi[0:D], bi[D:2 * D], a["L0_xattn_mha_out_b"]
    io["a_bv"] = c(bi[2 * D:].reshape(1, D))
    io["fa_w1"], io["fa_w2"] = c(f(a["L0_xattn_lin1_w"]).T[None]), c(f(a["L0_xattn_lin2_w"]).T[None])
    vec["fa_b1"], vec["fa_b2"] = a["L0_xattn_lin1_b"], a["L0_xattn_lin2_b"]
    for i in (1, 2, 3):
        vec[f"ln{i}_g"], vec[f"ln{i}_b"] = a[f"L0_xattn_ln{i}_g"], a[f"L0_xattn_ln{i}_b"]
    vec["lni_g"], vec["lni_b"] = a["L0_ffn_ln_g"], a["L0_ffn_ln_b"]
    for nm, key in (("s_wq", "L0_ffn_wq"), ("s_wk", "L0_ffn_wk")):
        w = f(a[key]).reshape(D, NG, HG, SD).transpose(1, 0, 2, 3)
        s = np.zeros((NG, D, HG, 4, SD), w.dtype)
        s[:, :, :, 0:3] = w[:, :, :, None]
        io[nm] = s.reshape(NG, D, P)
    io["s_wv"], io["s_wo"] = f(a["L0_ffn_wv"]), f(a["L0_ffn_wo"])
    io["f0_w1"], io["f0_w2"], vec["f0_b1"], vec["f0_b2"] = (f(a[f"L0_ffn_{k}"]) for k in ("w1", "w2", "b1", "b2"))
    for k in "qkvo":
        io[f"b_w{k}"] = f(a[f"L1_xattn_w{k}"])
        io[f"c_w{k}"] = f(a[f"L2_xattn_w{k}"])
        io[f"d_w{k}"] = c(f(a[f"L3_xattn_W{'p' if k == 'o' else k}"]).T)
    for k in "qko":
        vec[f"b_b{k}"], vec[f"d_b{k}"] = a[f"L1_xattn_b{k}"], a[f"L3_xattn_b{'p' if k == 'o' else k}"]
    io["b_bv"], io["d_bv"] = c(f(a["L1_xattn_bv"]).reshape(1, D)), c(f(a["L3_xattn_bv"]).reshape(1, D))
    io["r1_w"], io["f1_w1"], io["f1_w2"] = f(a["L1_ffn_router_w"]), f(a["L1_ffn_up_w"]), f(a["L1_ffn_down_w"])
    io["r2_w1"], io["r2_w2"], io["r2_b2"] = f(a["L2_ffn_rw1"]), f(a["L2_ffn_rw2"]), c(f(a["L2_ffn_rb2"]).reshape(1, E))
    vec["r2_b1"] = a["L2_ffn_rb1"]
    io["f2_w1"], io["f2_w2"], vec["f2_b1"], vec["f2_b2"] = (f(a[f"L2_ffn_{k}"]) for k in ("we1", "we2", "be1", "be2"))
    io["rel"] = f(a["L2_xattn_rel_bias"])
    io["f3_w1"], io["f3_w2"] = f(a["L3_ffn_w1"])[None], f(a["L3_ffn_w2"])[None]
    vec["f3_b1"], vec["f3_b2"] = a["L3_ffn_b1"], a["L3_ffn_b2"]
    io["vec"] = c(np.concatenate([f(vec[nm]).reshape(k, P) for nm, k in VECS]).T)
    io["mask_q"] = c(f(a["mask_1x1xSxS2_ik0"]).reshape(S, S2))
    io["mask_b"] = f(a["mask_BxS2_ik0"])
    io["mask_bT"] = c(f(a["mask_BxS2_ik0"]).T)
    p = np.arange(P)
    io["ident"] = np.eye(P, dtype=np.float32)
    io["one"] = np.ones((1, S2), np.float32)
    for hb in (4, 8):
        io[f"rows{hb}"] = (p[:, None] // (P // hb) == np.arange(hb)).astype(np.float32)
    part, row = p % 32 // SD, p % 32
    io["s_rows"] = c(np.stack([part == 2, part == 1, row == 24] + [p // 32 == j for j in range(HG)], 1).astype(np.float32))
    io["tri"] = c(np.broadcast_to(np.arange(E)[None, :] < np.arange(E)[:, None], (P, E, E)).astype(np.float32))
    io["hot"] = (bucket(S2 - 1 - np.arange(OFFS))[None, :] == np.arange(BUCKETS)[:, None]).astype(np.float32)
    return io


def kernel(**inputs):
    import concourse.bacc as bacc
    from concourse.bass_utils import run_bass_kernel_spmd

    laid = lay_out(inputs)
    arrays = {f"in_{name}": v for name, v in laid.items()}
    nc = bacc.Bacc("TRN2", target_bir_lowering=False, num_devices=1)
    io = {name: nc.dram_tensor(f"in_{name}", v.shape, mybir.dt.from_np(v.dtype), kind="ExternalInput").ap()
          for name, v in laid.items()}
    out = nc.dram_tensor("out", (D, T), F32, kind="ExternalOutput").ap()
    build(nc, io, out)
    r = run_bass_kernel_spmd(nc, [arrays], core_ids=[0])
    return np.ascontiguousarray(r.results[0]["out"].T).reshape(B, S, D)
```

```python
from contextlib import ExitStack, contextmanager

import numpy as np

import concourse.bass as bass
from concourse import mybir

F32 = mybir.dt.float32
F32R = mybir.dt.float32r
I32 = mybir.dt.int32
ALU = mybir.AluOpType
ACT = mybir.ActivationFunctionType
AX = mybir.AxisListType.X

P = 128
B, S, D = 2, 1024, 256
T = B * S
KD = D // P
CH = 512
NC = T // CH
S2 = 77
FF = 1024
NF = FF // P
E = 8
EPS = 1e-5
MAGIC = 1.5 * 2.0 ** 23
FIX = 256.0
BIG = 1e30
NT = S // P
BUCKETS = 32
OFFS = S + S2 - 1

SH = 32
SD = D // SH
HG = 4
NG = SH // HG
NKC = S // P

VECS = [
    ("a_bsv", 2), ("a_bso", 2), ("a_bq", 2), ("a_bk", 2), ("a_bo", 2), ("fa_b1", 8), ("fa_b2", 2),
    ("ln1_g", 2), ("ln1_b", 2), ("ln2_g", 2), ("ln2_b", 2), ("ln3_g", 2), ("ln3_b", 2),
    ("lni_g", 2), ("lni_b", 2), ("f0_b1", 64), ("f0_b2", 16),
    ("b_bq", 2), ("b_bk", 2), ("b_bo", 2),
    ("r2_b1", 2), ("f2_b1", 64), ("f2_b2", 16),
    ("d_bq", 2), ("d_bk", 2), ("d_bo", 2), ("f3_b1", 8), ("f3_b2", 2),
]
VEC_AT = {}
for _name, _k in VECS:
    VEC_AT[_name] = sum(k for nm, k in VECS[:len(VEC_AT)])
NVEC = sum(k for _, k in VECS)


@contextmanager
def phase(nc, names):
    with ExitStack() as ctx:
        sems = [ctx.enter_context(nc.semaphore(name)) for name in names]
        yield sems
        with nc.Block() as block:
            @block.gpsimd
            def _(pool):
                for s in sems:
                    pool.sem_clear(s)


def chunks(eng):
    with eng.Fori(0, B) as b:
        for cc in range(2):
            yield b * 2 + cc, cc


def tok(c):
    return bass.ds(c * CH, CH)


def wait_apart(m, eng, sem, value):
    eng.wait_ge(sem, value)
    eng.sem_inc(m.passed, 1)


def arrive(block, sem, loads):
    if loads:
        @block.sync
        def _(sp):
            for buf, data in loads:
                sp.dma_start(buf, data).then_inc(sem, 16)
            sp.wait_ge(sem, 16 * len(loads))


def layer_norm(nc, m, name, src, dst, gain=None, shift=None, loads=()):
    TC = CH // P
    names = [f"{name}_{s}" for s in ("mean", "centred", "squared", "var", "root", "recip", "diag", "spread", "scaled", "loaded")]
    with phase(nc, names) as (mean, centred, squared, var, root, recip, diag, spread, scaled, loaded), nc.Block() as block:
        arrive(block, loaded, loads)

        def at(c):
            return slice(c * CH, (c + 1) * CH)

        def over_features(bank):
            return m.ps[:, bank, :].unsqueeze(1).broadcast_to([P, KD, CH])

        @block.tensor
        def _(pe):
            for c in range(NC):
                for k in range(KD):
                    mm = pe.matmul(m.ps[:, c, :], m.mean_w[:, :], src[:, k, at(c)], start=k == 0, stop=k == KD - 1)
                mm.then_inc(mean, 1)
            for c in range(NC):
                pe.wait_ge(squared, c + 1)
                for i in range(TC):
                    col = c % 2 * TC + i
                    for k in range(KD):
                        mm = pe.matmul(m.ps[:, 4 + c // 2, col:col + 1], m.sq[:, c, k, i * P:(i + 1) * P], m.mean_w[:, 0:1],
                                       start=k == 0, stop=k == KD - 1)
                mm.then_inc(var, 1)
            for c in range(NC):
                pe.wait_ge(diag, TC * (c + 1))
                pe.matmul(m.ps[:, c, :], m.ones[:, :], m.diag[:, c, :], start=True, stop=True).then_inc(spread, 1)

        @block.vector
        def _(dve):
            for c in range(NC):
                dve.wait_ge(mean, c + 1)
                dve.tensor_tensor(dst[:, :, at(c)], src[:, :, at(c)], over_features(c), ALU.subtract).then_inc(centred, 1)
            for half in range(2):
                dve.wait_ge(root, half + 1)
                dve.reciprocal(m.rs[:, half, :], m.std[:, half, :]).then_inc(recip, 1)
                dve.wait_ge(recip, half + 1)
                for i in range(2 * TC):
                    dve.tensor_scalar(m.diag[:, 2 * half + i // TC, i % TC * P:(i % TC + 1) * P], m.ident[:, :],
                                      m.rs[:, half, i:i + 1], None, ALU.mult).then_inc(diag, 1)
            for c in range(NC):
                dve.wait_ge(spread, c + 1)
                dve.tensor_tensor(dst[:, :, at(c)], dst[:, :, at(c)], over_features(c), ALU.mult).then_inc(scaled, 1)

        @block.scalar
        def _(act):
            for c in range(NC):
                act.wait_ge(centred, c + 1)
                act.activation(m.sq[:, c, :, :], dst[:, :, at(c)], ACT.Square).then_inc(squared, 1)
            for half in range(2):
                act.wait_ge(var, 2 * half + 2)
                act.activation(m.std[:, half, :], m.ps[:, 4 + half, 0:2 * TC], ACT.Sqrt, bias=m.eps[:, 0:1]).then_inc(root, 1)
            if gain:
                for c in range(NC):
                    act.wait_ge(scaled, c + 1)
                    for k in range(KD):
                        act.activation(dst[:, k, at(c)], dst[:, k, at(c)], ACT.Identity, bias=m.col(shift, k), scale=m.col(gain, k))


def linear(nc, m, name, src, slot, dst, bias=None, func=ACT.Identity, plus=None, loads=()):
    with phase(nc, [f"{name}_{s}" for s in ("full", "evac", "loaded")]) as (full, evac, loaded), nc.Block() as block:
        arrive(block, loaded, loads)

        @block.tensor
        def _(pe):
            for c, cc in chunks(pe):
                for j in range(KD):
                    pe.wait_ge(evac, 2 * c + j + 1)
                    for k in range(KD):
                        mm = pe.matmul(m.ps[:, 2 * cc + j, :], m.wp[:, slot, k, j * P:(j + 1) * P], src[:, k, tok(c)],
                                       start=k == 0, stop=k == KD - 1)
                    mm.then_inc(full, 1)

        if plus is None:
            @block.scalar
            def _(act):
                act.sem_inc(evac, 4)
                for c, cc in chunks(act):
                    for j in range(KD):
                        wait_apart(m, act, full, 2 * c + j + 1)
                        act.activation(dst[:, j, tok(c)], m.ps[:, 2 * cc + j, :], func,
                                       bias=m.col(bias, j) if bias else 0.0).then_inc(evac, 1)
        else:
            @block.vector
            def _(dve):
                dve.sem_inc(evac, 4)
                for c, cc in chunks(dve):
                    for j in range(KD):
                        dve.wait_ge(full, 2 * c + j + 1)
                        dve.scalar_tensor_tensor(out=dst[:, j, tok(c)], in0=m.ps[:, 2 * cc + j, :],
                                                 scalar=m.col(bias, j) if bias else 0.0,
                                                 in1=plus[:, j, tok(c)], op0=ALU.add, op1=ALU.add).then_inc(evac, 1)


def add(nc, m, name, dst, src, loads=()):
    with phase(nc, [f"{name}_loaded"]) as (loaded,), nc.Block() as block:
        arrive(block, loaded, loads)

        @block.vector
        def _(dve):
            for c, cc in chunks(dve):
                dve.tensor_tensor(dst[:, :, tok(c)], dst[:, :, tok(c)], src[:, :, tok(c)], ALU.add)


def cross_attention(nc, m, name, src, dst, heads, adjust, scale, bq, bk, bv_row, io):
    d = D // heads
    hb = P // d
    hv = 8
    nj = hv // 4
    nr = heads // hv
    NU = NT * nr
    names = ["in", "kv_full", "kv_evac", "ones_col", "diag", "q_full", "q_evac", "s_full", "adj1", "adjusted",
             "s_max", "s_sub", "exp", "t_full", "floor", "t_evac", "o_full", "o_rec", "o_norm", "oT_full",
             "adj_in", "adj_out", "tb_full", "tb_evac", "tb_out", "bias_in0", "bias_in1"]
    with ExitStack() as ctx:
        sems = ctx.enter_context(phase(nc, [f"{name}_{s}" for s in names]))
        (loaded, kv_full, kv_evac, ones_col, diag, q_full, q_evac, s_full, adj1, adjusted, s_max, s_sub, exp_done,
         t_full, floor, t_evac, o_full, o_rec, o_norm, oT_full, adj_in, adj_out, tb_full, tb_evac, tb_out,
         bias_in0, bias_in1) = sems
        bias_in = [bias_in0, bias_in1]

        def sb(nm, shape, dt=F32):
            return ctx.enter_context(nc.sbuf_tensor(f"{name}_{nm}", shape, dt))

        ctxT = m.context_reversed if adjust == "bias" else m.context
        kT = sb("kT", [P, KD, B * S2])
        rows = m.head_rows[hb]
        k_diag = sb("k_diag", [P, B, KD, hb, S2])
        val = sb("val", [S2, B, heads, d + 1])
        bv = sb("bv", [1, D])
        qT = sb("qT", [P, KD, S])
        sc = sb("sc", [P, 2, hv, S2])
        pr = sb("pr", [P, 2, hv, S2])
        prT = sb("prT", [S2, 2, hv, P])
        mx = sb("mx", [P, 2, hv])
        rec = sb("rec", [P, 2, heads])
        on = sb("on", [P, 2, D])
        if adjust == "replace":
            mask_i = sb("mask_i", [P, NT, S2], I32)
            keep = sb("keep", [P, NT, S2])
            low = sb("low", [P, NT, S2])
        if adjust == "keep":
            mask_i = sb("mask_i", [P, B, S2], I32)
            keep = sb("keep", [P, B, S2])
            low = sb("low", [P, B, S2])
            mask_c = sb("mask_c", [S2, B], I32)
            keep_c = sb("keep_c", [S2, B])
        if adjust == "bias":
            bias_t = sb("bias_t", [P, 2, heads, S2])
            rel = sb("rel", [BUCKETS, heads])
            hot = sb("hot", [BUCKETS, OFFS])
            by_off = sb("by_off", [heads, OFFS])
            by_off_d = nc.dram_tensor("bias_by_offset", (heads, OFFS), F32).ap()
        n_in = (bv_row is not None) + {None: 0, "replace": 1, "keep": 3, "bias": 2}[adjust]

        block = ctx.enter_context(nc.Block())

        s_read = {None: s_sub, "replace": adj_out, "keep": adjusted, "bias": adjusted}[adjust]

        def credit(sem):
            return 2 if sem is s_read else 0

        turned = [job for n in range(NU + 4) for job in
                  ([("unit", n)] if n < NU else []) + ([("tile", (n - 4) // nr)] if n >= 4 and (n - 4) % nr == nr - 1 else [])]

        def turned_before(b, what, n):
            return b * len(turned) + turned.index((what, n))

        def by_bank(a):
            return a.rearrange("p (j h) s -> p j h s", j=nj)

        @block.sync
        def _(sp):
            if bv_row is not None:
                sp.dma_start(bv[:, :], bv_row).then_inc(loaded, 16)
            if adjust == "replace":
                sp.dma_start(mask_i[:, :, :], io["mask_q"].rearrange("(t p) s -> p t s", p=P)).then_inc(loaded, 16)
            if adjust == "keep":
                for b in range(B):
                    sp.dma_start(mask_i[:, b, :], io["mask_b"][b:b + 1, :].broadcast_to([P, S2])).then_inc(loaded, 16)
                sp.dma_start(mask_c[:, :], io["mask_bT"]).then_inc(loaded, 16)
            if adjust == "bias":
                sp.dma_start(rel[:, :], io["rel"]).then_inc(loaded, 16)
                sp.dma_start(hot[:, :], io["hot"]).then_inc(loaded, 16)
                sp.wait_ge(tb_evac, 3)
                sp.dma_start(by_off_d, by_off[:, :]).then_inc(tb_out, 16)
                sp.wait_ge(tb_out, 16)
                for i in range(B * NT):
                    if i >= 2:
                        sp.wait_ge(adjusted, nr * (i - 1) + 2)
                    sp.dma_start(bias_t[:, i % 2], bass.AP(by_off_d.tensor, (i % NT) * P, [[1, P], [OFFS, heads], [1, S2]])
                                 ).then_inc(bias_in[i % 2], 16)

        @block.tensor
        def _(pe):
            for j in range(KD):
                for k in range(KD):
                    mm = pe.matmul(m.ps[:, j, 0:B * S2], m.wp[:, 2, k, j * P:(j + 1) * P], ctxT[:, k, :],
                                   start=k == 0, stop=k == KD - 1)
                mm.then_inc(kv_full, 1)
            pe.wait_ge(loaded, 16 * n_in)
            for b in range(B):
                for k in range(KD):
                    mm = pe.matmul(m.ps[0:S2, 2 + b, 0:D], ctxT[:, k, b * S2:(b + 1) * S2], m.wp[:, 3, k, :],
                                   start=k == 0, stop=k == KD - 1 and bv_row is None)
                if bv_row is not None:
                    mm = pe.matmul(m.ps[0:S2, 2 + b, 0:D], m.ones[0:1, 0:S2], bv[:, :], start=False, stop=True)
                mm.then_inc(kv_full, 1)
            if adjust == "bias":
                for i in range(3):
                    w = min(512, OFFS - 512 * i)
                    pe.matmul(m.ps[0:heads, 4 + i, 0:w], rel[:, :], hot[:, 512 * i:512 * i + w],
                              start=True, stop=True).then_inc(tb_full, 1)
                pe.wait_ge(tb_evac, 3)
            pe.wait_ge(kv_evac, 4)
            pe.wait_ge(diag, B * KD)

            with pe.Fori(0, B) as b:
                pe.wait_ge(s_read, b * NU + 2)
                for cc in range(2):
                    for j in range(KD):
                        for k in range(KD):
                            mm = pe.matmul(m.ps[:, 2 * cc + j, :], m.wp[:, 0, k, j * P:(j + 1) * P],
                                           src[:, k, tok(b * 2 + cc)], start=k == 0, stop=k == KD - 1)
                        mm.then_inc(q_full, 1)

                def scores_of(n):
                    i, r = n // nr, n % nr
                    if n >= 2:
                        pe.wait_ge(s_read, b * NU + n + 1)
                    for j in range(nj):
                        fb, h = (hv * r + 4 * j) // hb, (hv * r + 4 * j) % hb
                        mm = pe.matmul(m.ps[:, 2 * (n % 2) + j, 0:4 * S2], qT[:, fb, i * P:(i + 1) * P],
                                       k_diag[:, bass.ds(b, 1), fb, h:h + 4, :].rearrange("p a h s -> p (a h s)"),
                                       start=True, stop=True)
                    mm.then_inc(s_full, 1)

                def turn(n):
                    pe.wait_ge(exp_done, b * NU + n + 3)
                    pe.wait_ge(t_evac, turned_before(b, "unit", n) + 1)
                    for hh in range(hv):
                        mm = pe.transpose(m.ps[0:S2, 4 + hh // 4, (hh % 4) * P:(hh % 4 + 1) * P], pr[:, n % 2, hh, :], m.ident[:, :])
                    mm.then_inc(t_full, 1)

                def values(n):
                    i, r = n // nr, n % nr
                    pe.wait_ge(t_evac, turned_before(b, "unit", n) + 2)
                    if r == 0:
                        pe.wait_ge(o_norm, b * NT + i + 1)
                    for hh in range(hv):
                        h = hv * r + hh
                        mm = pe.matmul(m.ps[:, 6 + i % 2, h * (d + 1):(h + 1) * (d + 1)], prT[:, n % 2, hh, :],
                                       val[:, bass.ds(b, 1), h, :].rearrange("p a e -> p (a e)"), start=True, stop=True)
                    mm.then_inc(o_full, 1)

                def back(i):
                    pe.wait_ge(o_norm, b * NT + i + 3)
                    pe.wait_ge(t_evac, turned_before(b, "tile", i) + 1)
                    for k in range(KD):
                        mm = pe.transpose(m.ps[:, 4, k * P:(k + 1) * P], on[:, i % 2, k * P:(k + 1) * P], m.ident[:, :])
                    mm.then_inc(oT_full, 1)

                pe.wait_ge(q_evac, b * 4 + 4)
                scores_of(0)
                scores_of(1)
                for n in range(NU + 4):
                    if n + 2 < NU:
                        scores_of(n + 2)
                    if n < NU:
                        turn(n)
                    if 1 <= n <= NU:
                        values(n - 1)
                    if n >= 4 and (n - 4) % nr == nr - 1:
                        back((n - 4) // nr)

        @block.scalar
        def _(act):
            act.sem_inc(t_evac, 1)
            act.sem_inc(exp_done, 2)
            for j in range(KD):
                act.wait_ge(kv_full, j + 1)
                act.activation(kT[:, j, :], m.ps[:, j, 0:B * S2], ACT.Identity,
                               bias=m.col(bk, j) if bk else 0.0).then_inc(kv_evac, 1)
            act.wait_ge(ones_col, 1)
            for b in range(B):
                act.wait_ge(kv_full, KD + b + 1)
                v = m.ps[0:S2, 2 + b, 0:D].rearrange("s (h d) -> s h d", d=d)
                if adjust == "keep":
                    act.activation(val[:, b, :, 0:d], v, ACT.Copy, scale=keep_c[:, b:b + 1]).then_inc(kv_evac, 1)
                else:
                    act.activation(val[:, b, :, 0:d], v, ACT.Copy).then_inc(kv_evac, 1)
            if adjust == "bias":
                for i in range(3):
                    w = min(512, OFFS - 512 * i)
                    act.wait_ge(tb_full, i + 1)
                    act.activation(by_off[:, 512 * i:512 * i + w], m.ps[0:heads, 4 + i, 0:w], ACT.Copy).then_inc(tb_evac, 1)

            with act.Fori(0, B) as b:
                for cc in range(2):
                    for j in range(KD):
                        act.wait_ge(q_full, b * 4 + 2 * cc + j + 1)
                        act.activation(qT[:, j, cc * CH:(cc + 1) * CH], m.ps[:, 2 * cc + j, :], ACT.Identity,
                                       bias=m.col(bq, j) if bq else 0.0).then_inc(q_evac, 1)

                def exp_of(n):
                    act.wait_ge(s_sub, b * NU + n + 1 + credit(s_sub))
                    act.wait_ge(t_full, b * NU + n + 1)
                    act.activation(pr[:, n % 2], sc[:, n % 2], ACT.Exp, scale=scale).then_inc(exp_done, 1)

                exp_of(0)
                for n in range(NU + 4):
                    if n + 1 < NU:
                        exp_of(n + 1)
                    if n < NU:
                        act.wait_ge(t_full, b * NU + n + 3)
                        act.wait_ge(o_full, b * NU + n + 1)
                        act.activation(prT[:, n % 2].rearrange("s (c h) q -> s c h q", c=2),
                                       m.ps[0:S2, 4:6, :].rearrange("s c (h q) -> s c h q", q=P), ACT.Copy).then_inc(t_evac, 1)
                    if n >= 4 and (n - 4) % nr == nr - 1:
                        i = (n - 4) // nr
                        wait_apart(m, act, oT_full, b * NT + i + 3)
                        act.activation(dst[:, :, bass.ds(b * S + i * P, P)],
                                       m.ps[:, 4, 0:D].rearrange("p (k q) -> p k q", k=KD), ACT.Copy).then_inc(t_evac, 1)

        @block.gpsimd
        def _(pool):
            pool.sem_inc(o_full, 2)
            pool.sem_inc(t_full, 2)
            pool.sem_inc(oT_full, 2)

        @block.vector
        def _(dve):
            dve.sem_inc(s_read, 2)
            dve.sem_inc(o_norm, 2)
            dve.wait_ge(loaded, 16 * n_in)
            if adjust == "keep":
                dve.tensor_scalar(keep_c[:, :], mask_c[:, :], 0.0, None, ALU.not_equal).then_inc(adj1, 1)
                dve.tensor_scalar(keep[:, :, :], mask_i[:, :, :], 0.0, None, ALU.not_equal).then_inc(adj1, 1)
                dve.wait_ge(adj1, 2)
                dve.tensor_scalar(low[:, :, :], keep[:, :, :], -1.0, BIG, ALU.add, ALU.mult).then_inc(adj1, 1)
                for b in range(B):
                    ins = dve.tensor_copy(val[:, b, :, d:d + 1].rearrange("s h a -> s (h a)"),
                                          keep_c[:, b:b + 1].broadcast_to([S2, heads]))
                ins.then_inc(ones_col, 1)
                dve.wait_ge(adj1, 3)
            else:
                dve.memset(val[:, :, :, d:d + 1], 1.0).then_inc(ones_col, 1)
            if adjust == "replace":
                dve.tensor_scalar(keep[:, :, :], mask_i[:, :, :], 0.0, None, ALU.not_equal).then_inc(adj1, 1)
                dve.wait_ge(adj1, 1)
                dve.tensor_scalar(low[:, :, :], keep[:, :, :], -1.0, 1e9 / scale, ALU.add, ALU.mult).then_inc(adj1, 1)
                dve.wait_ge(adj1, 2)
            dve.wait_ge(kv_evac, KD)
            for b in range(B):
                for k in range(KD):
                    dve.tensor_tensor(k_diag[:, b, k], kT[:, k, b * S2:(b + 1) * S2].unsqueeze(1).broadcast_to([P, hb, S2]),
                                      rows[:, :].unsqueeze(2).broadcast_to([P, hb, S2]), ALU.mult).then_inc(diag, 1)

            with dve.Fori(0, B) as b:
                def soft(n):
                    i, r = n // nr, n % nr
                    at = b * NU + n + 1
                    s3, s4 = sc[:, n % 2], by_bank(sc[:, n % 2])
                    dve.wait_ge(s_full, at)
                    dve.wait_ge(exp_done, at)
                    source = m.ps[:, 2 * (n % 2):2 * (n % 2) + nj, 0:4 * S2].rearrange("p j (h s) -> p j h s", s=S2)
                    if adjust == "replace":
                        k4 = keep[:, i:i + 1, :].unsqueeze(1).broadcast_to([P, nj, 4, S2])
                        l3 = low[:, i:i + 1, :].broadcast_to([P, hv, S2])
                        dve.tensor_tensor(s4, source, k4, ALU.mult).then_inc(adj_out, 1)
                        dve.wait_ge(adj_out, at + 2)
                        dve.tensor_tensor(s3, s3, l3, ALU.add).then_inc(adjusted, 1)
                    if adjust == "keep":
                        l4 = low[:, bass.ds(b, 1), :].unsqueeze(1).broadcast_to([P, nj, 4, S2])
                        dve.tensor_tensor(s4, source, l4, ALU.add).then_inc(adjusted, 1)
                    if adjust == "bias":
                        dve.wait_ge(bias_in[i % 2], b * (8 * NT) + 16 * (i // 2 + 1))
                        dve.tensor_tensor(s4, source, by_bank(bias_t[:, i % 2, hv * r:hv * (r + 1)]), ALU.add).then_inc(adjusted, 1)
                    if adjust:
                        dve.wait_ge(adjusted, at + credit(adjusted))
                        source = s4
                    dve.tensor_reduce(mx[:, n % 2, :].rearrange("p (j h) -> p j h", j=nj), source, AX, ALU.max).then_inc(s_max, 1)
                    dve.wait_ge(s_max, at)
                    dve.tensor_tensor(s4, source, mx[:, n % 2, :].rearrange("p (j h) -> p j h", j=nj).unsqueeze(3).broadcast_to([P, nj, 4, S2]),
                                      ALU.subtract).then_inc(s_sub, 1)

                def norm(i):
                    o = m.ps[:, 6 + i % 2, 0:heads * (d + 1)].rearrange("p (h e) -> p h e", e=d + 1)
                    dve.wait_ge(o_full, b * NU + (i + 1) * nr + 2)
                    if adjust == "keep":
                        dve.tensor_scalar(rec[:, i % 2].unsqueeze(2), o[:, :, d:d + 1], 1e-30, None, ALU.max).then_inc(floor, 1)
                        dve.wait_ge(floor, b * NT + i + 1)
                        dve.reciprocal(rec[:, i % 2], rec[:, i % 2]).then_inc(o_rec, 1)
                    else:
                        dve.reciprocal(rec[:, i % 2].unsqueeze(2), o[:, :, d:d + 1]).then_inc(o_rec, 1)
                    dve.wait_ge(o_rec, b * NT + i + 1)
                    dve.wait_ge(oT_full, b * NT + i + 1)
                    dve.tensor_tensor(on[:, i % 2, :].rearrange("p (h e) -> p h e", e=d), o[:, :, 0:d],
                                      rec[:, i % 2].unsqueeze(2).broadcast_to([P, heads, d]), ALU.mult).then_inc(o_norm, 1)

                for n in range(NU + 3):
                    if n < NU:
                        soft(n)
                    if n >= 3 and (n - 3) % nr == nr - 1:
                        norm((n - 3) // nr)


def experts(nc, m, name, raw, src, dst, n_exp, func, w1_d, w2_d, b1, b2, mode, gates_d=None):
    blocks = mode == "blocks"
    per_chunks = 1 if blocks else NC
    width = 2 * P if blocks else CH
    RING = 4
    LAG = 2
    names = ["w1_in", "w2_in", "w_high", "w1_split", "w2_split", "gate_in0", "gate_in1", "src_high", "src_split", "h_full", "h_raw", "h_high",
             "h_split", "y_step", "y_evac", "y_tmp"]
    with ExitStack() as ctx:
        sems = ctx.enter_context(phase(nc, [f"{name}_{s}" for s in names]))
        (w1_in, w2_in, w_high, w1_split, w2_split, gate_in0, gate_in1, src_high, src_split, h_full, h_raw, h_high,
         h_split, y_step, y_evac, y_tmp) = sems
        gate_in = [gate_in0, gate_in1]

        def sb(nm, shape, dt=F32):
            return ctx.enter_context(nc.sbuf_tensor(f"{name}_{nm}", shape, dt))

        slots = min(n_exp, 2)
        xh, xl = sb("xh", [P, KD, T], F32R), sb("xl", [P, KD, T], F32R)
        raw1, raw2 = raw
        w1h, w1l = sb("w1h", [P, slots, KD, FF], F32R), sb("w1l", [P, slots, KD, FF], F32R)
        w2h, w2l = sb("w2h", [P, slots, NF, D], F32R), sb("w2l", [P, slots, NF, D], F32R)
        hr = sb("hr", [P, RING, width])
        hh, hl = sb("hh", [P, RING, width], F32R), sb("hl", [P, RING, width], F32R)
        yt = sb("yt", [P, 2, width])
        if mode == "gated":
            gate = sb("gate", [P, 2, T])
        block = ctx.enter_context(nc.Block())

        def view(buf, k, c):
            if blocks:
                return buf[:, k, :].rearrange("p (b q) -> p b q", b=B)[:, :, bass.ds(c * P, P)]
            return buf[:, k, tok(c)]

        def cut(ap):
            return ap.rearrange("p (b q) -> p b q", b=B) if blocks else ap

        def units(eng):
            if n_exp == 1:
                for c, cc in chunks(eng):
                    yield 0, 0, c, c
            else:
                with eng.Fori(0, n_exp // 2) as i:
                    for par in range(2):
                        e = i * 2 + par
                        for c in range(per_chunks):
                            yield e, par, (e if blocks else c), i * (2 * per_chunks) + par * per_chunks + c

        TURN = 2 if n_exp == 1 else 2 * per_chunks

        @block.sync
        def _(sp):
            def load(e, par):
                ex = bass.ds(e, 1)
                for raw, w_d, w_in, w_split in ((raw1, w1_d, w1_in, w1_split), (raw2, w2_d, w2_in, w2_split)):
                    if isinstance(e, int) and e == 0:
                        continue
                    sp.wait_ge(w_split, e)
                    sp.dma_start(raw[:, :, :], w_d[ex].rearrange("a (k p) n -> p (a k) n", p=P)).then_inc(w_in, 16)
                if mode == "gated":
                    if not (isinstance(e, int) and e < 2):
                        sp.wait_ge(y_evac, e * (2 * per_chunks) + 4 - 2 * per_chunks)
                    sp.dma_start(gate[:, par, :], gates_d[ex].broadcast_to([P, T])).then_inc(gate_in[par], 16)
            for e in range(slots):
                load(e, e)
            if n_exp > 1:
                with sp.Fori(1, n_exp // 2) as i:
                    for par in range(2):
                        load(i * 2 + par, par)

        @block.tensor
        def _(pe):
            def three(bank_ap, st_h, st_l, mv_h, mv_l, first, last):
                pe.matmul(bank_ap, st_h, mv_h, start=first, stop=False)
                pe.matmul(bank_ap, st_h, mv_l, start=False, stop=False)
                return pe.matmul(bank_ap, st_l, mv_h, start=False, stop=last)

            def hidden_of(J, f, e, par, c, j, unit):
                if f == 0:
                    if n_exp == 1 or blocks or unit == 0:
                        pe.wait_ge(src_split, NC if blocks else c + 1)
                    elif unit < NC:
                        pe.wait_ge(src_split, c + 1)
                    pe.wait_ge(w1_split, e + 1)
                pe.wait_ge(h_raw, J + 1)
                for k in range(KD):
                    mm = three(cut(m.ps[:, f % 4, 0:width]), w1h[:, par, k, f * P:(f + 1) * P], w1l[:, par, k, f * P:(f + 1) * P],
                               view(xh, k, c), view(xl, k, c), k == 0, k == KD - 1)
                mm.then_inc(h_full, 1)

            def out_of(J, f, e, par, c, j, unit):
                pe.wait_ge(h_split, J + RING + 1)
                if f == 0:
                    pe.wait_ge(w2_split, e + 1)
                    pe.wait_ge(y_evac, j * 2 + 2)
                for o in range(KD):
                    mm = three(m.ps[:, 4 + 2 * (unit % 2) + o, 0:width], w2h[:, par, f, o * P:(o + 1) * P], w2l[:, par, f, o * P:(o + 1) * P],
                               hh[:, f % RING, :], hl[:, f % RING, :], f == 0, f == NF - 1)
                mm.then_inc(y_step, 1)

            waiting = []
            for unit, (e, par, c, j) in enumerate(units(pe)):
                for f in range(NF):
                    here = (j * NF + f, f, e, par, c, j, unit)
                    hidden_of(*here)
                    waiting.append(here)
                    if len(waiting) > LAG:
                        out_of(*waiting.pop(0))
                if unit % TURN == TURN - 1:
                    while waiting:
                        out_of(*waiting.pop(0))

        @block.scalar
        def _(act):
            act.sem_inc(h_raw, RING)
            act.activation(w1h[:, 0], raw1[:, :, :], ACT.Copy).then_inc(w_high, 1)
            for c, cc in chunks(act):
                act.activation(xh[:, :, tok(c)], src[:, :, tok(c)], ACT.Copy).then_inc(src_high, 1)
            act.activation(w2h[:, 0], raw2[:, :, :], ACT.Copy).then_inc(w_high, 1)
            for e, par, c, j in units(act):
                for f in range(NF):
                    if b1 is None:
                        bias = 0.0
                    elif n_exp == 1:
                        bias = m.col(b1, f)
                    else:
                        bias = m.vec[:, bass.ds(e * NF + (VEC_AT[b1] + f), 1)]
                    wait_apart(m, act, h_full, j * NF + f + 1)
                    wait_apart(m, act, h_split, j * NF + f + 1)
                    act.activation(hr[:, f % RING, :], m.ps[:, f % 4, 0:width], func, bias=bias).then_inc(h_raw, 1)

        @block.gpsimd
        def _(pool):
            pool.sem_inc(y_step, RING)
            pool.sem_inc(y_evac, 4)

            def weights_of(e, par):
                if isinstance(e, int):
                    pool.wait_ge(w_high, 2)
                if not (isinstance(e, int) and e < 2):
                    wait_apart(m, pool, y_step, e * (NF * per_chunks) - NF * per_chunks + RING)
                for z, (high, low, raw, w_in, w_split) in enumerate(((w1h, w1l, raw1, w1_in, w1_split), (w2h, w2l, raw2, w2_in, w2_split))):
                    wait_apart(m, pool, w_in, e * 16)
                    pool.tensor_scalar(high[:, par], raw[:, :, :], 1.0, 1.0, ALU.mult, ALU.mult).then_inc(w_high, 1)
                    wait_apart(m, pool, w_high, e * 2 + z + 1)
                    pool.tensor_tensor(low[:, par], raw[:, :, :], high[:, par].bitcast(F32), ALU.subtract).then_inc(w_split, 1)
            if n_exp > 1:
                weights_of(1, 1)
                with pool.Fori(1, n_exp // 2) as i:
                    for par in range(2):
                        weights_of(i * 2 + par, par)

        @block.vector
        def _(dve):
            dve.sem_inc(h_split, RING)
            dve.wait_ge(w_high, 1)
            dve.tensor_tensor(w1l[:, 0], raw1[:, :, :], w1h[:, 0].bitcast(F32), ALU.subtract).then_inc(w1_split, 1)
            for c, cc in chunks(dve):
                dve.wait_ge(src_high, c + 1)
                dve.tensor_tensor(xl[:, :, tok(c)], src[:, :, tok(c)], xh[:, :, tok(c)].bitcast(F32), ALU.subtract).then_inc(src_split, 1)
            dve.wait_ge(w_high, 2)
            dve.tensor_tensor(w2l[:, 0], raw2[:, :, :], w2h[:, 0].bitcast(F32), ALU.subtract).then_inc(w2_split, 1)

            def outputs(e, par, c, j, unit):
                dve.wait_ge(y_step, j * NF + NF + RING)
                if mode == "gated":
                    dve.wait_ge(gate_in[par], e * 8 + 16 - 8 * par)
                for o in range(KD):
                    y = m.ps[:, 4 + 2 * (unit % 2) + o, 0:width]
                    to = view(dst, o, c)
                    if mode == "gated":
                        bias = m.vec[:, bass.ds(e * KD + (VEC_AT[b2] + o), 1)] if b2 else 0.0
                        dve.scalar_tensor_tensor(out=yt[:, o, :], in0=y, scalar=bias, in1=gate[:, par, tok(c)],
                                                 op0=ALU.add, op1=ALU.mult).then_inc(y_tmp, 1)
                        dve.wait_ge(y_tmp, j * 2 + o + 1)
                        dve.tensor_tensor(to, to, yt[:, o, :], ALU.add).then_inc(y_evac, 1)
                    else:
                        bias = m.vec[:, bass.ds(e * KD + (VEC_AT[b2] + o), 1)] if n_exp > 1 else m.col(b2, o)
                        dve.scalar_tensor_tensor(out=to, in0=cut(y), scalar=bias, in1=to, op0=ALU.add, op1=ALU.add).then_inc(y_evac, 1)

            last = None
            for unit, (e, par, c, j) in enumerate(units(dve)):
                for f in range(NF):
                    J = j * NF + f
                    dve.wait_ge(h_raw, J + RING + 1)
                    dve.wait_ge(y_step, J + 1)
                    dve.tensor_copy(hh[:, f % RING, :], hr[:, f % RING, :]).then_inc(h_high, 1)
                    dve.wait_ge(h_high, J + 1)
                    dve.tensor_tensor(hl[:, f % RING, :], hr[:, f % RING, :], hh[:, f % RING, :].bitcast(F32), ALU.subtract).then_inc(h_split, 1)
                    if f == LAG + 1 and last is not None:
                        outputs(*last)
                last = (e, par, c, j, unit)
                if unit % TURN == TURN - 1:
                    outputs(*last)
                    last = None


def fixed_point_network(nc, m, weights, src, dst, b1, b2):
    HB = NF // 2
    W = HB * CH
    NU = 2 * NC
    names = [f"f3_{s}" for s in ("b1_scaled", "h_full", "h_evac", "whole", "place", "floor", "frac", "g_low",
                                 "g_high", "diff", "prod", "summed", "scaled", "hidden", "y_full", "y_scaled", "y_whole", "y_evac")]
    with ExitStack() as ctx:
        (b1_scaled, h_full, h_evac, whole, place, floor, frac, g_low, g_high, diff, prod, summed, scaled, hidden,
         y_full, y_scaled, y_whole, y_evac) = ctx.enter_context(phase(nc, names))

        def sb(nm, shape):
            return ctx.enter_context(nc.sbuf_tensor(f"f3_{nm}", shape, F32))

        w1, w2 = weights
        b1s = sb("b1s", [P, NF])
        steps = sb("steps", [P, 2, W])
        quarter = sb("quarter", [P, 2, W])
        low, high = sb("low", [P, 2, W]), sb("high", [P, 2, W])
        h = sb("h", [P, 2, NF, CH])
        yt = sb("yt", [P, KD, CH])
        block = ctx.enter_context(nc.Block())

        def at(c):
            return slice(c * CH, (c + 1) * CH)

        @block.tensor
        def _(pe):
            def hidden_of(u):
                c, part = u // 2, u % 2
                for f in range(HB):
                    if u >= 1:
                        pe.wait_ge(h_evac, (u - 1) * HB + f + 1)
                    for k in range(KD):
                        mm = pe.matmul(m.ps[:, f, :], w1[:, k, (part * HB + f) * P:(part * HB + f + 1) * P], src[:, k, at(c)],
                                       start=k == 0, stop=k == KD - 1)
                    mm.then_inc(h_full, 1)

            def out_of(u):
                c, part = u // 2, u % 2
                pe.wait_ge(hidden, u + 1)
                if part == 0 and c >= 2:
                    pe.wait_ge(y_evac, KD * (c - 1))
                for o in range(KD):
                    for f in range(part * HB, (part + 1) * HB):
                        mm = pe.matmul(m.ps[:, 4 + 2 * (c % 2) + o, :], w2[:, f, o * P:(o + 1) * P], h[:, c % 2, f, :],
                                       start=f == 0, stop=f == NF - 1)
                    if part == 1:
                        mm.then_inc(y_full, 1)

            for u in range(NU + 2):
                if u < NU:
                    hidden_of(u)
                if u >= 2:
                    out_of(u - 2)

        @block.scalar
        def _(act):
            act.wait_ge(b1_scaled, 1)
            for u in range(NU + 1):
                if u < NU:
                    for f in range(HB):
                        act.wait_ge(h_full, u * HB + f + 1)
                        if f == 0 and u >= 2:
                            act.wait_ge(prod, u - 1)
                        act.activation(steps[:, u % 2, f * CH:(f + 1) * CH], m.ps[:, f, :], ACT.Identity,
                                       bias=b1s[:, (u % 2) * HB + f:(u % 2) * HB + f + 1], scale=FIX).then_inc(h_evac, 1)
                if u >= 1:
                    act.wait_ge(floor, u)
                    if u >= 3:
                        act.wait_ge(scaled, u - 2)
                    act.activation(low[:, (u - 1) % 2], quarter[:, (u - 1) % 2], ACT.Gelu, scale=0.25).then_inc(g_low, 1)
                    act.activation(high[:, (u - 1) % 2], quarter[:, (u - 1) % 2], ACT.Gelu, scale=0.25, bias=m.quarter[:, 0:1]).then_inc(g_high, 1)

        @block.gpsimd
        def _(pool):
            for u in range(NU):
                pool.wait_ge(g_low, u + 1)
                pool.wait_ge(g_high, u + 1)
                pool.tensor_tensor(high[:, u % 2], high[:, u % 2], low[:, u % 2], ALU.subtract).then_inc(diff, 1)

        @block.vector
        def _(dve):
            dve.tensor_scalar(b1s[:, :], m.vec[:, VEC_AT[b1]:VEC_AT[b1] + NF], FIX, None, ALU.mult).then_inc(b1_scaled, 1)

            def positions(u):
                st, qu = steps[:, u % 2], quarter[:, u % 2]
                dve.wait_ge(h_evac, (u + 1) * HB)
                dve.tensor_scalar(st, st, MAGIC, -MAGIC, ALU.add, ALU.add).then_inc(whole, 1)
                dve.wait_ge(whole, u + 1)
                if u >= 2:
                    dve.wait_ge(g_high, u - 1)
                dve.tensor_scalar(qu, st, 4 / FIX, -(0.5 - 2 / FIX), ALU.mult, ALU.add).then_inc(place, 1)
                dve.wait_ge(place, u + 1)
                dve.tensor_scalar(qu, qu, MAGIC, -MAGIC, ALU.add, ALU.add).then_inc(floor, 1)
                dve.wait_ge(floor, u + 1)
                dve.scalar_tensor_tensor(out=st, in0=st, scalar=4 / FIX, in1=qu, op0=ALU.mult, op1=ALU.subtract).then_inc(frac, 1)

            def lines(u):
                st = steps[:, u % 2]
                dve.wait_ge(frac, u + 1)
                dve.wait_ge(diff, u + 1)
                dve.tensor_tensor(high[:, u % 2], st, high[:, u % 2], ALU.mult).then_inc(prod, 1)
                dve.wait_ge(prod, u + 1)
                dve.tensor_tensor(low[:, u % 2], high[:, u % 2], low[:, u % 2], ALU.add).then_inc(summed, 1)
                dve.wait_ge(summed, u + 1)
                if u % 2 == 0 and u >= 4:
                    dve.wait_ge(y_full, KD * (u // 2 - 1))
                to = h[:, u // 2 % 2, (u % 2) * HB:(u % 2 + 1) * HB, :].rearrange("p f n -> p (f n)")
                dve.tensor_scalar(to, low[:, u % 2], FIX, MAGIC, ALU.mult, ALU.add).then_inc(scaled, 1)
                dve.wait_ge(scaled, u + 1)
                dve.tensor_scalar(to, to, -MAGIC, 1 / FIX, ALU.add, ALU.mult).then_inc(hidden, 1)

            def outputs(c):
                for o in range(KD):
                    n = c * KD + o + 1
                    dve.wait_ge(y_full, n)
                    dve.tensor_scalar(yt[:, o, :], m.ps[:, 4 + 2 * (c % 2) + o, :], m.col(b2, o), FIX, ALU.add, ALU.mult).then_inc(y_scaled, 1)
                    dve.wait_ge(y_scaled, n)
                    dve.tensor_scalar(yt[:, o, :], yt[:, o, :], MAGIC, -MAGIC, ALU.add, ALU.add).then_inc(y_whole, 1)
                    dve.wait_ge(y_whole, n)
                    dve.scalar_tensor_tensor(out=dst[:, o, at(c)], in0=yt[:, o, :], scalar=1 / FIX, in1=dst[:, o, at(c)],
                                             op0=ALU.mult, op1=ALU.add).then_inc(y_evac, 1)

            positions(0)
            for u in range(NU + 2):
                if u + 1 < NU:
                    positions(u + 1)
                if u < NU:
                    lines(u)
                if u >= 2 and u % 2 == 1:
                    outputs((u - 3) // 2)


def router(nc, m, name, src, w_d, b_d, top, gates_d, tri_d):
    names = ["in", "full", "logit", "max", "shifted", "exp", "above", "equal", "ahead", "beat", "rank", "kept",
             "gate", "sum", "rec", "out", "t_full", "t_evac", "stored"]
    NTT = T // P
    with ExitStack() as ctx:
        sems = ctx.enter_context(phase(nc, [f"{name}_{s}" for s in names]))
        (loaded, full, logit, s_max, shifted, exp_done, above, equal, ahead, beat, rank_done, kept, gate_done, sum_done,
         rec_done, out, t_full, t_evac, stored) = sems

        def sb(nm, shape):
            return ctx.enter_context(nc.sbuf_tensor(f"{name}_{nm}", shape, F32))

        w = sb("w", [P, KD, E])
        bias = sb("bias", [P, E])
        tri = sb("tri", [P, E, E])
        sh = sb("sh", [P, NTT, E])
        lg, ex, col, rank, g = sb("lg", [P, NTT, E]), sb("ex", [P, NTT, E]), sb("col", [P, NTT]), sb("rank", [P, NTT, E]), sb("g", [P, NTT, E])
        gt, eq = sb("gt", [P, NTT, E, E]), sb("eq", [P, NTT, E, E])
        gT = sb("gT", [E, T])
        n_in = 3 if b_d is not None else 2
        block = ctx.enter_context(nc.Block())

        @block.sync
        def _(sp):
            sp.dma_start(w[:, :, :], w_d.rearrange("(k p) e -> p k e", p=P)).then_inc(loaded, 16)
            sp.dma_start(tri[:, :, :], tri_d).then_inc(loaded, 16)
            if b_d is not None:
                sp.dma_start(bias[:, :], b_d.broadcast_to([P, E])).then_inc(loaded, 16)
            sp.wait_ge(t_evac, 4)
            sp.dma_start(gates_d, gT[:, :]).then_inc(stored, 16)
            sp.wait_ge(stored, 16)

        @block.tensor
        def _(pe):
            pe.wait_ge(loaded, 16 * n_in)
            for i in range(NTT):
                for k in range(KD):
                    mm = pe.matmul(m.ps[:, 0, i * E:(i + 1) * E], src[:, k, i * P:(i + 1) * P], w[:, k, :],
                                   start=k == 0, stop=k == KD - 1)
            mm.then_inc(full, 1)
            pe.wait_ge(out, 1)
            for c in range(NC):
                for i in range(4 * c, 4 * c + 4):
                    mm = pe.transpose(m.ps[0:E, 4 + c, (i % 4) * P:(i % 4 + 1) * P], g[:, i, :], m.ident[:, :])
                mm.then_inc(t_full, 1)

        @block.scalar
        def _(act):
            act.wait_ge(shifted, 1)
            act.activation(ex[:, :, :], sh[:, :, :], ACT.Exp).then_inc(exp_done, 1)
            for c in range(NC):
                act.wait_ge(t_full, c + 1)
                act.activation(gT[:, c * CH:(c + 1) * CH], m.ps[0:E, 4 + c, :], ACT.Copy).then_inc(t_evac, 1)

        @block.vector
        def _(dve):
            dve.wait_ge(loaded, 16 * n_in)
            dve.wait_ge(full, 1)
            p3 = m.ps[:, 0, 0:NTT * E].rearrange("p (i e) -> p i e", e=E)
            if b_d is not None:
                dve.tensor_tensor(lg[:, :, :], p3, bias[:, :].unsqueeze(1).broadcast_to([P, NTT, E]), ALU.add).then_inc(logit, 1)
            else:
                dve.tensor_copy(lg[:, :, :], p3).then_inc(logit, 1)
            dve.wait_ge(logit, 1)
            dve.tensor_reduce(col[:, :], lg[:, :, :], AX, ALU.max).then_inc(s_max, 1)
            dve.wait_ge(s_max, 1)
            dve.tensor_tensor(sh[:, :, :], lg[:, :, :], col[:, :].unsqueeze(2).broadcast_to([P, NTT, E]), ALU.subtract).then_inc(shifted, 1)
            dve.wait_ge(shifted, 1)
            for i in range(NTT):
                lj = lg[:, i:i + 1, :].broadcast_to([P, E, E])
                le = lg[:, i, :].unsqueeze(2).broadcast_to([P, E, E])
                ins = dve.tensor_tensor(gt[:, i], lj, le, ALU.is_gt)
                ins2 = dve.tensor_tensor(eq[:, i], lj, le, ALU.is_equal)
            ins.then_inc(above, 1)
            ins2.then_inc(equal, 1)
            dve.wait_ge(above, 1)
            dve.wait_ge(equal, 1)
            dve.tensor_tensor(eq[:, :, :, :], eq[:, :, :, :], tri[:, :, :].unsqueeze(1).broadcast_to([P, NTT, E, E]), ALU.mult).then_inc(ahead, 1)
            dve.wait_ge(ahead, 1)
            dve.tensor_tensor(gt[:, :, :, :], gt[:, :, :, :], eq[:, :, :, :], ALU.add).then_inc(beat, 1)
            dve.wait_ge(beat, 1)
            dve.tensor_reduce(rank[:, :, :], gt[:, :, :, :], AX, ALU.add).then_inc(rank_done, 1)
            dve.wait_ge(rank_done, 1)
            dve.tensor_scalar(rank[:, :, :], rank[:, :, :], float(top), None, ALU.is_lt).then_inc(kept, 1)
            dve.wait_ge(kept, 1)
            dve.wait_ge(exp_done, 1)
            dve.tensor_tensor(g[:, :, :], ex[:, :, :], rank[:, :, :], ALU.mult).then_inc(gate_done, 1)
            dve.wait_ge(gate_done, 1)
            dve.tensor_reduce(col[:, :], g[:, :, :], AX, ALU.add).then_inc(sum_done, 1)
            dve.wait_ge(sum_done, 1)
            dve.reciprocal(col[:, :], col[:, :]).then_inc(rec_done, 1)
            dve.wait_ge(rec_done, 1)
            dve.tensor_tensor(g[:, :, :], g[:, :, :], col[:, :].unsqueeze(2).broadcast_to([P, NTT, E]), ALU.mult).then_inc(out, 1)


def self_attention(nc, m, src, dst, io):
    names = ["const", "vg_set", "v_full", "v_evac", "w_in", "job_full", "job_evac", "high", "keys", "v_group", "max_full", "max_part",
             "max_both", "max_ready", "s_full", "exp", "pv", "o_evac", "o_out0", "o_out1", "o_in", "sum_in", "recip", "recip_out",
             "spread"]
    with ExitStack() as ctx:
        sems = ctx.enter_context(phase(nc, [f"self_{s}" for s in names]))
        (const, vg_set, v_full, v_evac, w_in, job_full, job_evac, high, keys, v_group, max_full, max_part, max_both, max_ready,
         s_full, exp_done, pv, o_evac, o_out0, o_out1, o_in, sum_in, recip, recip_out, spread) = sems
        o_out = [o_out0, o_out1]

        def sb(nm, shape, dt=F32):
            return ctx.enter_context(nc.sbuf_tensor(f"self_{nm}", shape, dt))

        w = sb("w", [P, 2, KD, P])
        wv = sb("wv", [P, KD, D])
        rows = sb("rows", [P, 7])
        hi = sb("hi", [P, 2, CH])
        q = sb("q", [P, 2, S], F32R)
        qm = sb("qm", [P, S], F32R)
        kk = sb("kk", [P, S], F32R)
        km = sb("km", [P, 2, HG, S], F32R)
        v = sb("v", [P, B * NKC, SH, SD])
        vg = sb("vg", [P, 2, NKC, HG, 32])
        mp = sb("mp", [P, NT, HG, 2])
        mf = sb("mf", [P, NT, HG])
        mt = sb("mt", [P, NT, P])
        pr = sb("pr", [P, 2, HG, CH])
        o = sb("o", [P, 2, CH])
        sums = sb("sums", [P, SH * T // P])
        o_d = nc.dram_tensor("self_out", (D, T), F32).ap()
        sum_d = nc.dram_tensor("self_sum", (SH, T), F32).ap()
        rec_d = nc.dram_tensor("self_rec", (SH, T), F32).ap()
        block = ctx.enter_context(nc.Block())
        FIRST_BANKS = [7, 2, 3, 4]
        STEPS = 2 * NKC
        UNITS = HG * NT * 2
        PER = UNITS // STEPS
        JOB_AT = {3: 0, 6: 1, 9: 2, 12: 3}

        def idx(g, b, n):
            return g * (2 * n) + b * n

        def jobs_before(g, b):
            last = isinstance(g, int) and g == NG - 1 and b == 1
            return 8 + 12 * g + 2 if last else idx(g, b, 6) + 8

        def groups(eng, body):
            with eng.Fori(0, NG - 1) as g:
                body(g, 0, (g, 1), True)
                body(g, 1, (g + 1, 0), True)
            body(NG - 1, 0, (NG - 1, 1), False)
            body(NG - 1, 1, None, False)

        @block.sync
        def _(sp):
            def load(g):
                for z, nm in enumerate(("s_wq", "s_wk")):
                    sp.dma_start(w[:, z], io[nm][g].rearrange("a (k p) n -> p (a k) n", p=P)).then_inc(w_in, 16)
            sp.dma_start(wv[:, :, :], io["s_wv"].rearrange("(k p) n -> p k n", p=P)).then_inc(const, 16)
            sp.dma_start(rows[:, :], io["s_rows"]).then_inc(const, 16)
            load(slice(0, 1))

            def body(g, b, nxt, project):
                if b == 0 and project:
                    sp.wait_ge(job_full, g * 12 + 8)
                    load(bass.ds(g + 1, 1))
                for half in range(2):
                    sp.wait_ge(o_evac, idx(g, b, 2) + half + 2)
                    at = slice(b * S + half * CH, b * S + half * CH + CH)
                    for j in range(HG):
                        sp.dma_start(o_d[bass.ds(g * 32 + 8 * j, SD), at], o[32 * j:32 * j + SD, half, :]).then_inc(o_out[half], 16)
                    sp.dma_start(sum_d[bass.ds(g * HG, HG), at], o[SD:P:32, half, :]).then_inc(o_out[half], 16)
            groups(sp, body)
            for half in range(2):
                sp.wait_ge(o_out[half], 80 + 80 * 2 * NG)
            sp.dma_start(sums[:, :], sum_d.rearrange("h (a n) -> (h a) n", n=SH * T // P)).then_inc(sum_in, 16)
            sp.dma_start(dst[:, :, :], o_d.rearrange("(k p) n -> p k n", p=P)).then_inc(o_in, 16)
            sp.wait_ge(recip, 1)
            sp.dma_start(rec_d.rearrange("h (a n) -> (h a) n", n=SH * T // P), sums[:, :]).then_inc(recip_out, 16)
            sp.wait_ge(recip_out, 16)
            for h in range(SH):
                k, p = h * SD // P, h * SD % P
                sp.dma_start(src[p:p + SD, k, :], rec_d[h:h + 1, :].broadcast_to([SD, T])).then_inc(spread, 16)

        @block.tensor
        def _(pe):
            pe.wait_ge(const, 32)
            def project(bank, r, b, ks=range(KD)):
                z, half = r // 2, r % 2
                for k in ks:
                    mm = pe.matmul(m.ps[:, bank, :], w[:, z, k, :], src[:, k, b * S + half * CH:b * S + half * CH + CH],
                                   start=k == 0, stop=k == KD - 1)
                    if k == KD - 1:
                        mm.then_inc(job_full, 1)

            def max_unit(g, b, un):
                j, i, half = un // (2 * NT), un // 2 % NT, un % 2
                if i == 0 and half == 0:
                    pe.wait_ge(keys, idx(g, b, HG) + j + 1)
                pe.wait_ge(max_part, idx(g, b, UNITS) + un + 1)
                pe.matmul(m.ps[:, un % 2, :], q[:, b, i * P:(i + 1) * P], km[:, b, j, half * CH:(half + 1) * CH],
                          start=True, stop=True).then_inc(max_full, 1)

            pe.wait_ge(w_in, 32)
            for job in range(8):
                if job >= 4:
                    pe.wait_ge(job_evac, job - 3)
                project(FIRST_BANKS[job % 4], job % 4, job // 4)
            for un in range(UNITS):
                max_unit(0, 0, un)
                if un % (UNITS // (B * NKC)) == 0:
                    i = un // (UNITS // (B * NKC))
                    if i >= 2:
                        pe.wait_ge(v_evac, i - 1)
                    for k in range(KD):
                        mm = pe.matmul(m.ps[:, 5 + i % 2, 0:D], src[:, k, i * P:(i + 1) * P], wv[:, k, :], start=k == 0, stop=k == KD - 1)
                    mm.then_inc(v_full, 1)
            pe.wait_ge(v_evac, B * NKC)
            pe.wait_ge(job_evac, 8)

            def body(g, b, nxt, projects):
                before = jobs_before(g, b)

                def turn_maxima(half):
                    pe.wait_ge(job_evac, before + half)
                    for i in range(4):
                        mm = pe.transpose(m.ps[:, 7, i * P:(i + 1) * P], mt[:, half * 4 + i, :], m.ident[:, :])
                    mm.then_inc(job_full, 1)

                def values(s):
                    half, kc = s // NKC, s % NKC
                    pe.wait_ge(exp_done, idx(g, b, 2 * STEPS) + 2 * s + 2 + 2)
                    if s == 0:
                        pe.wait_ge(v_group, idx(g, b, 1) + 1)
                    if kc == 0:
                        pe.wait_ge(o_evac, idx(g, b, 2) + half + 1)
                    for j in range(HG):
                        mm = pe.matmul(m.ps[32 * j:32 * j + 32, 6, :], vg[:, b, kc, j, :], pr[:, s % 2, j, :],
                                       start=kc == 0, stop=kc == NKC - 1)
                    mm.then_inc(pv, 1)

                def next_max(s, i):
                    if nxt is not None:
                        max_unit(*nxt, s * PER + i)

                pe.wait_ge(max_ready, idx(g, b, 1) + 1)
                turn_maxima(0)
                for s in range(STEPS):
                    half, kc = s // NKC, s % NKC
                    for pair in range(2):
                        if kc == 0 and pair == 0:
                            pe.wait_ge(job_evac, before + half + 1)
                        pe.wait_ge(exp_done, idx(g, b, 2 * STEPS) + 2 * s + pair + 1)
                        for jj in range(2):
                            mm = pe.matmul(m.ps[:, 2 + 2 * pair + jj, :], km[:, b, 2 * pair + jj, kc * P:(kc + 1) * P],
                                           qm[:, half * CH:(half + 1) * CH], start=True, stop=True)
                        mm.then_inc(s_full, 1)
                        next_max(s, pair)
                    if s >= 1:
                        values(s - 1)
                    next_max(s, 2)
                    if s == 1:
                        turn_maxima(1)
                    if projects and s in JOB_AT:
                        if s == 3:
                            pe.wait_ge(w_in, g * 32 + 64)
                        pe.wait_ge(job_evac, before + 2 + JOB_AT[s])
                        project(7, JOB_AT[s], b, range(0, 1))
                    if projects and s - 1 in JOB_AT:
                        project(7, JOB_AT[s - 1], b, range(1, KD))
                    next_max(s, 3)
                values(STEPS - 1)
            groups(pe, body)

        @block.scalar
        def _(act):
            act.sem_inc(exp_done, 2)
            act.sem_inc(o_evac, 1)
            def high_part(r, bank, job):
                act.wait_ge(job_full, job + 1)
                if not isinstance(job, int) or job >= 2:
                    act.wait_ge(job_evac, job - 1)
                act.activation(hi[:, r % 2, :], m.ps[:, bank, :], ACT.Copy, scale=rows[:, r // 2:r // 2 + 1]).then_inc(high, 1)

            for job in range(8):
                high_part(job % 4, FIRST_BANKS[job % 4], job)
            for i in range(B * NKC):
                act.wait_ge(v_full, i + 1)
                act.activation(v[:, i], m.ps[:, 5 + i % 2, 0:D].rearrange("p (h d) -> p h d", d=SD), ACT.Copy).then_inc(v_evac, 1)

            def body(g, b, nxt, projects):
                before = jobs_before(g, b)
                for s in range(STEPS):
                    act.wait_ge(pv, idx(g, b, STEPS) + s + 1)
                    for pair in range(2):
                        act.wait_ge(s_full, idx(g, b, 2 * STEPS) + 2 * s + pair + 2)
                        act.activation(pr[:, s % 2, 2 * pair:2 * pair + 2, :], m.ps[:, 2 + 2 * pair:4 + 2 * pair, :], ACT.Exp,
                                       scale=1.0 / float(np.float32(np.sqrt(SD)))).then_inc(exp_done, 1)
                        if pair == 0 and projects and s - 2 in JOB_AT:
                            high_part(JOB_AT[s - 2], 7, before + 2 + JOB_AT[s - 2])
                    if s in (NKC, STEPS - 1):
                        half = s // NKC - (s == NKC)
                        act.wait_ge(pv, idx(g, b, STEPS) + NKC * (half + 1) + 2)
                        act.wait_ge(o_out[half], idx(g, b, 80) + 80)
                        act.activation(o[:, half, :], m.ps[:, 6, :], ACT.Copy).then_inc(o_evac, 1)
            groups(act, body)

        @block.gpsimd
        def _(pool):
            pool.sem_inc(pv, 2)
            pool.sem_inc(s_full, 1)
            for half in range(2):
                pool.sem_inc(o_out[half], 80)
            pool.memset(vg[:, :, :, :, :], 0.0).then_inc(vg_set, 1)
            pool.wait_ge(vg_set, 1)
            pool.memset(vg[:, :, :, :, SD:SD + 1], 1.0).then_inc(vg_set, 1)
            pool.wait_ge(vg_set, 2)
            pool.wait_ge(const, 32)

            def spread_keys(b):
                for j in range(HG):
                    pool.tensor_scalar(km[:, b, j, :], kk[:, :].bitcast(F32), rows[:, 3 + j:4 + j], 1.0, ALU.mult, ALU.mult).then_inc(keys, 1)

            def pick_values(g, b):
                pool.tensor_copy(vg[:, b, :, :, 0:SD], v[:, b * NKC:(b + 1) * NKC, bass.ds(g * HG, HG), :]).then_inc(v_group, 1)

            pool.wait_ge(job_evac, 4)
            spread_keys(0)
            pool.wait_ge(v_evac, B * NKC)
            pick_values(0, 0)

            def body(g, b, nxt, projects):
                if nxt is not None:
                    if not isinstance(g, int):
                        wait_apart(m, pool, job_evac, jobs_before(g, b))
                        wait_apart(m, pool, s_full, idx(g, b, 2 * STEPS) + 1)
                    else:
                        pool.wait_ge(job_evac, jobs_before(g, b))
                        pool.wait_ge(s_full, idx(g, b, 2 * STEPS) + 1)
                    spread_keys(nxt[1])
                    pool.wait_ge(pv, idx(g, b, STEPS) + 2)
                    pick_values(*nxt)
            groups(pool, body)

            pool.wait_ge(o_in, 16)
            pool.wait_ge(spread, 16 * SH)
            pool.tensor_tensor(dst[:, :, 0:T // 4], dst[:, :, 0:T // 4], src[:, :, 0:T // 4], ALU.mult)

        @block.vector
        def _(dve):
            dve.sem_inc(max_part, 2)
            dve.memset(mt[:, :, :], 0.0).then_inc(max_both, 1)
            dve.wait_ge(max_both, 1)
            dve.wait_ge(const, 32)

            def split(r, b, bank, job, high_at):
                z, half = r // 2, r % 2
                dve.wait_ge(job_full, job + 1)
                dve.wait_ge(high, high_at)
                at = slice(half * CH, (half + 1) * CH)
                if z == 0:
                    dve.tensor_tensor(q[:, b, at], m.ps[:, bank, :], hi[:, r % 2, :], ALU.subtract).then_inc(job_evac, 1)
                else:
                    dve.scalar_tensor_tensor(out=kk[:, at], in0=m.ps[:, bank, :], scalar=rows[:, 2:3], in1=hi[:, r % 2, :],
                                             op0=ALU.add, op1=ALU.subtract).then_inc(job_evac, 1)

            def max_unit(g, b, un):
                j, i, half = un // (2 * NT), un // 2 % NT, un % 2
                dve.wait_ge(max_full, idx(g, b, UNITS) + un + 1)
                dve.tensor_reduce(mp[:, i, j, half:half + 1], m.ps[:, un % 2, :], AX, ALU.max).then_inc(max_part, 1)
                if un == UNITS - 1:
                    dve.wait_ge(max_part, idx(g, b, UNITS) + UNITS + 2)
                    dve.tensor_tensor(mf[:, :, :], mp[:, :, :, 0:1].rearrange("p i j a -> p i (j a)"),
                                      mp[:, :, :, 1:2].rearrange("p i j a -> p i (j a)"), ALU.max).then_inc(max_both, 1)
                    dve.wait_ge(max_both, idx(g, b, 1) + 2)
                    dve.tensor_scalar(mt[:, :, 24:P:32], mf[:, :, :], -1.0, None, ALU.mult).then_inc(max_ready, 1)

            for job in range(8):
                if job == 6:
                    dve.wait_ge(keys, HG)
                split(job % 4, job // 4, FIRST_BANKS[job % 4], job, job + 1)
            for un in range(UNITS):
                max_unit(0, 0, un)

            def body(g, b, nxt, projects):
                before = jobs_before(g, b)

                def with_maxima(half):
                    at = slice(half * CH, (half + 1) * CH)
                    dve.wait_ge(job_full, before + half + 1)
                    dve.tensor_tensor(qm[:, at], m.ps[:, 7, :], q[:, b, at].bitcast(F32), ALU.add).then_inc(job_evac, 1)

                with_maxima(0)
                for s in range(STEPS):
                    if projects and s - 3 in JOB_AT:
                        r = JOB_AT[s - 3]
                        if r == 2:
                            dve.wait_ge(keys, idx(*nxt, HG) + HG)
                        split(r, b, 7, before + 2 + r, idx(g, b, 4) + 8 + r + 1)
                    if nxt is not None:
                        for i in range(PER):
                            max_unit(*nxt, s * PER + i)
                    if s == 1:
                        with_maxima(1)
            groups(dve, body)

            dve.wait_ge(sum_in, 16)
            dve.reciprocal(sums[:, :], sums[:, :]).then_inc(recip, 1)
            dve.wait_ge(o_in, 16)
            dve.wait_ge(spread, 16 * SH)
            dve.tensor_tensor(dst[:, :, T // 4:T], dst[:, :, T // 4:T], src[:, :, T // 4:T], ALU.mult)


def build(nc, io, out):
    class M:
        pass
    m = M()
    with ExitStack() as ctx:
        def sb(name, shape, dt=F32):
            return ctx.enter_context(nc.sbuf_tensor(name, shape, dt))
        m.ps = ctx.enter_context(nc.psum_tensor("ps", [P, 8, 512], F32))
        x, n = (sb(nm, [P, KD, T]) for nm in "xn")
        m.vec = sb("vec_sb", [P, NVEC])
        m.mean_w, m.ones, m.ident = (sb(nm, [P, P]) for nm in ("mean_w", "ones", "ident_sb"))
        m.eps, m.quarter = sb("eps", [P, 1]), sb("quarter", [P, 1])
        m.wp = sb("wp", [P, 4, KD, D])
        m.context, m.context_reversed = sb("context", [P, KD, B * S2]), sb("context_reversed", [P, KD, B * S2])
        m.head_rows = {hb: sb(f"head_rows{hb}", [P, hb]) for hb in (4, 8)}

        def col(name, i):
            at = VEC_AT[name] + i
            return m.vec[:, at:at + 1]
        m.col = col
        m.passed = ctx.enter_context(nc.semaphore("passed"))
        gates_d = [nc.dram_tensor(f"gates{i}", (E, T), F32).ap() for i in range(2)]

        with phase(nc, ["x_in", "const_set"]) as (x_in, const_set), nc.Block() as block:
            @block.sync
            def _(sp):
                sp.dma_start(x[:, :, :], io["xT"].rearrange("(k p) n -> p k n", p=P)).then_inc(x_in, 16)
                sp.dma_start(m.vec[:, :], io["vec"]).then_inc(x_in, 16)
                sp.dma_start(m.ident[:, :], io["ident"]).then_inc(x_in, 16)
                for buf, name in ((m.context, "ctxT"), (m.context_reversed, "ctxT_reversed")):
                    sp.dma_start(buf[:, :, :], io[name].rearrange("(k p) n -> p k n", p=P)).then_inc(x_in, 16)
                for hb, buf in m.head_rows.items():
                    sp.dma_start(buf[:, :], io[f"rows{hb}"]).then_inc(x_in, 16)
                sp.wait_ge(x_in, 16 * 7)

            @block.vector
            def _(dve):
                dve.memset(m.mean_w[:, :], 1.0 / D)
                dve.memset(m.ones[:, :], 1.0)
                dve.memset(m.eps[:, :], EPS)
                dve.memset(m.quarter[:, :], 0.25).then_inc(const_set, 1)
                dve.wait_ge(const_set, 1)

        def norm(name, src, dst, g=None, b=None, loads=()):
            with ExitStack() as sc:
                m.sq = sc.enter_context(nc.sbuf_tensor(f"{name}_sq", [P, NC, KD, CH], F32))
                m.diag = sc.enter_context(nc.sbuf_tensor(f"{name}_diag", [P, NC, CH], F32))
                m.std = sc.enter_context(nc.sbuf_tensor(f"{name}_std", [P, 2, NT], F32))
                m.rs = sc.enter_context(nc.sbuf_tensor(f"{name}_rs", [P, 2, NT], F32))
                layer_norm(nc, m, name, src, dst, g, b, loads)

        @contextmanager
        def scratch(i):
            with nc.sbuf_tensor(f"u{i}", [P, KD, T], F32) as u, nc.sbuf_tensor(f"t{i}", [P, KD, T], F32) as t:
                yield u, t

        def weights(*slots):
            return [(m.wp[:, slot], io[name].rearrange("(k p) n -> p k n", p=P)) for slot, name in slots]

        def attention_weights(layer):
            return weights(*[(slot, f"{layer}_w{name}") for slot, name in enumerate("qokv")])

        @contextmanager
        def landing(name):
            with nc.sbuf_tensor(f"{name}_raw1", [P, KD, FF], F32) as raw1, nc.sbuf_tensor(f"{name}_raw2", [P, NF, D], F32) as raw2:
                yield (raw1, raw2), [(raw1[:, :, :], io[f"{name}_w1"][0:1].rearrange("a (k p) n -> p (a k) n", p=P)),
                                     (raw2[:, :, :], io[f"{name}_w2"][0:1].rearrange("a (k p) n -> p (a k) n", p=P))]

        def store(src):
            with phase(nc, ["stored"]) as (stored,), nc.Block() as block:
                @block.sync
                def _(sp):
                    sp.dma_start(out.rearrange("(k p) n -> p k n", p=P), src[:, :, :]).then_inc(stored, 16)
                    sp.wait_ge(stored, 16)

        with scratch(0) as (u, t):
            norm("n0", x, n, loads=weights((0, "a_wsv"), (1, "a_wso")))
            linear(nc, m, "sv", n, 0, t, bias="a_bsv")
            linear(nc, m, "so", t, 1, u, bias="a_bso", plus=n)
            norm("n1", u, u, "ln1_g", "ln1_b", loads=attention_weights("a"))
            cross_attention(nc, m, "xa", u, t, 8, None, 1.0 / float(np.sqrt(np.float32(32))), "a_bq", "a_bk", io["a_bv"], io)
            linear(nc, m, "ao", t, 1, n, bias="a_bo", plus=u)
        with landing("fa") as (raw, first_weights):
            norm("n2", n, n, "ln2_g", "ln2_b", loads=first_weights)
            experts(nc, m, "fa", raw, n, n, 1, ACT.Relu, io["fa_w1"], io["fa_w2"], "fa_b1", "fa_b2", "dense")
        norm("n3", n, n, "ln3_g", "ln3_b")
        add(nc, m, "r0", x, n)

        norm("n4", x, n)
        with scratch(1) as (u, t):
            norm("n5", n, u, "lni_g", "lni_b", loads=weights((0, "s_wo")))
            self_attention(nc, m, u, t, io)
            with landing("f0") as (raw, first_weights):
                linear(nc, m, "wo", t, 0, n, plus=n, loads=first_weights)
                experts(nc, m, "f0", raw, n, x, E, ACT.Gelu, io["f0_w1"], io["f0_w2"], "f0_b1", "f0_b2", "blocks")

        norm("n6", x, n, loads=attention_weights("b"))
        with scratch(2) as (u, t):
            cross_attention(nc, m, "xb", n, t, 16, "replace", 0.25, "b_bq", "b_bk", io["b_bv"], io)
            linear(nc, m, "bo", t, 1, x, bias="b_bo", plus=x)
        with landing("f1") as (raw, first_weights):
            norm("n7", x, n, loads=first_weights)
            router(nc, m, "r1", n, io["r1_w"], None, 4, gates_d[0], io["tri"])
            experts(nc, m, "f1", raw, n, x, E, ACT.Gelu_apprx_tanh, io["f1_w1"], io["f1_w2"], None, None, "gated", gates_d[0])

        norm("n8", x, n, loads=attention_weights("c"))
        with scratch(3) as (u, t):
            cross_attention(nc, m, "xc", n, t, 16, "bias", 1.0, None, None, None, io)
            linear(nc, m, "co", t, 1, x, plus=x)
        norm("n9", x, n, loads=weights((0, "r2_w1")))
        with scratch(4) as (u, t):
            linear(nc, m, "rh", n, 0, u, bias="r2_b1", func=ACT.Silu)
            router(nc, m, "r2", u, io["r2_w2"], io["r2_b2"], 2, gates_d[1], io["tri"])
        with landing("f2") as (raw, first_weights):
            add(nc, m, "r2x", x, n, loads=first_weights)
            experts(nc, m, "f2", raw, n, x, E, ACT.Silu, io["f2_w1"], io["f2_w2"], "f2_b1", "f2_b2", "gated", gates_d[1])

        norm("n10", x, n, loads=attention_weights("d"))
        with scratch(5) as (u, t):
            cross_attention(nc, m, "xd", n, t, 16, "keep", 0.25, "d_bq", "d_bk", io["d_bv"], io)
            linear(nc, m, "do", t, 1, x, bias="d_bo", plus=x)
        with landing("f3") as (raw, first_weights):
            norm("n11", x, n, loads=first_weights)
            fixed_point_network(nc, m, raw, n, x, "f3_b1", "f3_b2")
        store(x)


def bucket(offset):
    half, exact = BUCKETS // 2, BUCKETS // 4
    r = np.abs(offset)
    far = np.log(np.maximum(r, 1).astype(np.float32) / np.float32(exact)) / np.float32(np.log(128 / exact)) * np.float32(half - exact)
    return half * (offset > 0) + np.where(r < exact, r, np.minimum(exact + far.astype(np.int32), half - 1))


def lay_out(a):
    f = lambda v: np.asarray(v)
    c = np.ascontiguousarray
    io = {"xT": c(f(a["x"]).reshape(T, D).T), "ctxT": c(f(a["ctx_1024"]).reshape(B * S2, D).T)}
    io["ctxT_reversed"] = c(f(a["ctx_1024"])[:, ::-1].reshape(B * S2, D).T)
    vec = {}
    io["a_wsv"], io["a_wso"] = c(f(a["L0_xattn_qkv_w"])[2 * D:].T), c(f(a["L0_xattn_sa_out_w"]).T)
    for z, k in enumerate("qkv"):
        io[f"a_w{k}"] = c(f(a["L0_xattn_in_proj_w"])[z * D:(z + 1) * D].T)
    io["a_wo"] = c(f(a["L0_xattn_mha_out_w"]).T)
    bi = f(a["L0_xattn_in_proj_b"])
    vec["a_bsv"], vec["a_bso"] = f(a["L0_xattn_qkv_b"])[2 * D:], a["L0_xattn_sa_out_b"]
    vec["a_bq"], vec["a_bk"], vec["a_bo"] = bi[0:D], bi[D:2 * D], a["L0_xattn_mha_out_b"]
    io["a_bv"] = c(bi[2 * D:].reshape(1, D))
    io["fa_w1"], io["fa_w2"] = c(f(a["L0_xattn_lin1_w"]).T[None]), c(f(a["L0_xattn_lin2_w"]).T[None])
    vec["fa_b1"], vec["fa_b2"] = a["L0_xattn_lin1_b"], a["L0_xattn_lin2_b"]
    for i in (1, 2, 3):
        vec[f"ln{i}_g"], vec[f"ln{i}_b"] = a[f"L0_xattn_ln{i}_g"], a[f"L0_xattn_ln{i}_b"]
    vec["lni_g"], vec["lni_b"] = a["L0_ffn_ln_g"], a["L0_ffn_ln_b"]
    for nm, key in (("s_wq", "L0_ffn_wq"), ("s_wk", "L0_ffn_wk")):
        w = f(a[key]).reshape(D, NG, HG, SD).transpose(1, 0, 2, 3)
        s = np.zeros((NG, D, HG, 4, SD), w.dtype)
        s[:, :, :, 0:3] = w[:, :, :, None]
        io[nm] = s.reshape(NG, D, P)
    io["s_wv"], io["s_wo"] = f(a["L0_ffn_wv"]), f(a["L0_ffn_wo"])
    io["f0_w1"], io["f0_w2"], vec["f0_b1"], vec["f0_b2"] = (f(a[f"L0_ffn_{k}"]) for k in ("w1", "w2", "b1", "b2"))
    for k in "qkvo":
        io[f"b_w{k}"] = f(a[f"L1_xattn_w{k}"])
        io[f"c_w{k}"] = f(a[f"L2_xattn_w{k}"])
        io[f"d_w{k}"] = c(f(a[f"L3_xattn_W{'p' if k == 'o' else k}"]).T)
    for k in "qko":
        vec[f"b_b{k}"], vec[f"d_b{k}"] = a[f"L1_xattn_b{k}"], a[f"L3_xattn_b{'p' if k == 'o' else k}"]
    io["b_bv"], io["d_bv"] = c(f(a["L1_xattn_bv"]).reshape(1, D)), c(f(a["L3_xattn_bv"]).reshape(1, D))
    io["r1_w"], io["f1_w1"], io["f1_w2"] = f(a["L1_ffn_router_w"]), f(a["L1_ffn_up_w"]), f(a["L1_ffn_down_w"])
    io["r2_w1"], io["r2_w2"], io["r2_b2"] = f(a["L2_ffn_rw1"]), f(a["L2_ffn_rw2"]), c(f(a["L2_ffn_rb2"]).reshape(1, E))
    vec["r2_b1"] = a["L2_ffn_rb1"]
    io["f2_w1"], io["f2_w2"], vec["f2_b1"], vec["f2_b2"] = (f(a[f"L2_ffn_{k}"]) for k in ("we1", "we2", "be1", "be2"))
    io["rel"] = f(a["L2_xattn_rel_bias"])
    io["f3_w1"], io["f3_w2"] = f(a["L3_ffn_w1"])[None], f(a["L3_ffn_w2"])[None]
    vec["f3_b1"], vec["f3_b2"] = a["L3_ffn_b1"], a["L3_ffn_b2"]
    io["vec"] = c(np.concatenate([f(vec[nm]).reshape(k, P) for nm, k in VECS]).T)
    io["mask_q"] = c(f(a["mask_1x1xSxS2_ik0"]).reshape(S, S2))
    io["mask_b"] = f(a["mask_BxS2_ik0"])
    io["mask_bT"] = c(f(a["mask_BxS2_ik0"]).T)
    p = np.arange(P)
    io["ident"] = np.eye(P, dtype=np.float32)
    for hb in (4, 8):
        io[f"rows{hb}"] = (p[:, None] // (P // hb) == np.arange(hb)).astype(np.float32)
    part, row = p % 32 // SD, p % 32
    io["s_rows"] = c(np.stack([part == 2, part == 1, row == 24] + [p // 32 == j for j in range(HG)], 1).astype(np.float32))
    io["tri"] = c(np.broadcast_to(np.arange(E)[None, :] < np.arange(E)[:, None], (P, E, E)).astype(np.float32))
    io["hot"] = (bucket(S2 - 1 - np.arange(OFFS))[None, :] == np.arange(BUCKETS)[:, None]).astype(np.float32)
    return io


def kernel(**inputs):
    import concourse.bacc as bacc
    from concourse.bass_utils import run_bass_kernel_spmd

    laid = lay_out(inputs)
    arrays = {f"in_{name}": v for name, v in laid.items()}
    nc = bacc.Bacc("TRN2", target_bir_lowering=False, num_devices=1)
    io = {name: nc.dram_tensor(f"in_{name}", v.shape, mybir.dt.from_np(v.dtype), kind="ExternalInput").ap()
          for name, v in laid.items()}
    out = nc.dram_tensor("out", (D, T), F32, kind="ExternalOutput").ap()
    build(nc, io, out)
    r = run_bass_kernel_spmd(nc, [arrays], core_ids=[0])
    return np.ascontiguousarray(r.results[0]["out"].T).reshape(B, S, D)
```
